# Optimizing a Trainium2 kernel written in Bass

```python
import numpy as np
import jax
import jax.numpy as jnp

def _softmax(x, axis=-1):
    return jax.nn.softmax(x, axis=axis)

def _gelu(x):
    return jax.nn.gelu(x, approximate=True)

def _silu(x):
    return jax.nn.silu(x)

def _sigmoid(x):
    return jax.nn.sigmoid(x)

def _layernorm(x, axis=-1, eps=1e-05):
    m = jnp.mean(x, axis=axis, keepdims=True)
    v = jnp.var(x, axis=axis, keepdims=True)
    return (x - m) / jnp.sqrt(v + eps)

def _scatter_add(tgt, idx, src, axis=0):
    return tgt.at[idx].add(src)

def _segment_sum(src, seg, n):
    return jax.ops.segment_sum(src, seg, n)
kernel_name = 'mk_decoder_preln_d1_seqx_r8_f31f26'

def setup_inputs(seed: int=0):
    np.random.seed(seed)
    _w = jnp.asarray

    def _rec_inputs():
        import jax
        import jax.numpy as jnp
        _rk = jax.random.key(seed)
        x = -0.0003929 + 0.9999 * jax.random.normal(jax.random.fold_in(_rk, 1), (16, 128, 128), jnp.float32)
        _lenS = 128 - jax.random.randint(jax.random.fold_in(_rk, 7), (16,), 0, max(1, 128 // 4) + 1, jnp.int32)
        _lenS2 = 128 - jax.random.randint(jax.random.fold_in(_rk, 8), (16,), 0, max(1, 128 // 4) + 1, jnp.int32)
        _ctx_512P = jax.random.normal(jax.random.fold_in(_rk, 11), (16, 16, 64), jnp.float32)
        _ctx_512c = jax.random.dirichlet(jax.random.fold_in(_rk, 511), 0.3 * jnp.ones((16,), jnp.float32), (16, 128))
        _ctx_512t = jnp.einsum('bsk,bkd->bsd', _ctx_512c, _ctx_512P)
        _ctx_512t = _ctx_512t * jax.lax.rsqrt(jnp.mean(jnp.square(_ctx_512t)) + 1e-12) * 0.953939
        ctx_512 = 4.13588e-05 + 0.999923 * (_ctx_512t + 0.3 * jax.random.normal(jax.random.fold_in(_rk, 611), (16, 128, 64), jnp.float32))
        return (x, ctx_512)
    x, ctx_512 = _rec_inputs()

    def _L0_attn_setup():
        import jax, jax.numpy as jnp
        import numpy as np
        D_MODEL, STATE, N_EXP, VOCAB = (128, 16, 4, 4000)
        B, L = (4, 256)
        EPS = 1e-05
        key = jax.random.key(seed)
        ks = jax.random.split(key, 20)
        d, s, e, f = (D_MODEL, STATE, N_EXP, 4 * D_MODEL)
        sc = 0.02
        inp = {'x': jax.random.normal(ks[0], (B, L, d), jnp.float32), 'A_log': jnp.log(jax.random.uniform(ks[1], (d, s)) * 0.9 + 0.1), 'D_param': jnp.ones((d,), jnp.float32), 'Wd': jax.random.normal(ks[2], (d, d)) * sc, 'bd': jnp.zeros((d,)), 'WB': jax.random.normal(ks[3], (d, s)) * sc, 'bB': jnp.zeros((s,)), 'WC': jax.random.normal(ks[4], (d, s)) * sc, 'bC': jnp.zeros((s,)), 'Wr': jax.random.normal(ks[5], (d, e)) * sc, 'br': jnp.zeros((e,)), 'up_w': jax.random.normal(ks[6], (e, d, f)) * sc, 'up_b': jnp.zeros((e, f)), 'down_w': jax.random.normal(ks[7], (e, f, d)) * sc, 'down_b': jnp.zeros((e, d)), 'ln_w': jnp.ones((d,)), 'ln_b': jnp.zeros((d,))}
        return inp
    _L0_attn_all = _L0_attn_setup()
    _L0_attn_in = {k: v for k, v in _L0_attn_all.items() if k in ('A_log', 'D_param', 'Wd', 'bd', 'WB', 'bB', 'WC', 'bC', 'Wr', 'br', 'up_w', 'up_b', 'down_w', 'down_b', 'ln_w', 'ln_b')}
    del _L0_attn_all

    def _L0_xattn_setup():
        import jax, jax.numpy as jnp
        import numpy as np
        B, LQ, LK = (8, 256, 256)
        QD, KD, VD = (128, 64, 64)
        key = jax.random.key(seed)
        ks = jax.random.split(key, 9)
        s = 0.02
        return {'query': jax.random.normal(ks[0], (B, LQ, QD), jnp.float32), 'key': jax.random.normal(ks[1], (B, LK, KD), jnp.float32), 'value': jax.random.normal(ks[2], (B, LK, VD), jnp.float32), 'Wq': jax.random.normal(ks[3], (QD, QD), jnp.float32) * s, 'bq': jnp.zeros((QD,), jnp.float32), 'Wk': jax.random.normal(ks[4], (KD, QD), jnp.float32) * s, 'bk': jnp.zeros((QD,), jnp.float32), 'Wv': jax.random.normal(ks[5], (VD, QD), jnp.float32) * s, 'bv': jnp.zeros((QD,), jnp.float32)}
    _L0_xattn_all = _L0_xattn_setup()
    _L0_xattn_in = {k: v for k, v in _L0_xattn_all.items() if k in ('Wq', 'bq', 'Wk', 'bk', 'Wv', 'bv')}
    del _L0_xattn_all

    def _L0_ffn_setup():
        import jax, jax.numpy as jnp
        import numpy as np
        TOP_K = 2
        CAP_FACTOR = 1.25
        EPS = 1.1920929e-07
        key = jax.random.key(seed)
        ks = jax.random.split(key, 6)
        B, S, D, E, H = (8, 256, 128, 8, 512)
        return {'hidden_states': jax.random.normal(ks[0], (B, S, D), jnp.float32), 'wg': jax.random.normal(ks[1], (D, E), jnp.float32) * 0.02, 'fc1_w': jax.random.normal(ks[2], (E, H, D), jnp.float32) * 0.02, 'fc1_b': jnp.zeros((E, H), jnp.float32), 'fc2_w': jax.random.normal(ks[3], (E, H, D), jnp.float32) * 0.02, 'fc2_b': jnp.zeros((E, D), jnp.float32), 'ln_gamma': jnp.ones((D,), jnp.float32), 'ln_beta': jnp.zeros((D,), jnp.float32)}
    _L0_ffn_all = _L0_ffn_setup()
    _L0_ffn_in = {k: v for k, v in _L0_ffn_all.items() if k in ('wg', 'fc1_w', 'fc1_b', 'fc2_w', 'fc2_b', 'ln_gamma', 'ln_beta')}
    del _L0_ffn_all
    return {'x': x, 'ctx_512': ctx_512, 'L0_attn_A_log': _L0_attn_in['A_log'], 'L0_attn_D_param': _L0_attn_in['D_param'], 'L0_attn_Wd': _L0_attn_in['Wd'], 'L0_attn_bd': _L0_attn_in['bd'], 'L0_attn_WB': _L0_attn_in['WB'], 'L0_attn_bB': _L0_attn_in['bB'], 'L0_attn_WC': _L0_attn_in['WC'], 'L0_attn_bC': _L0_attn_in['bC'], 'L0_attn_Wr': _L0_attn_in['Wr'], 'L0_attn_br': _L0_attn_in['br'], 'L0_attn_up_w': _L0_attn_in['up_w'], 'L0_attn_up_b': _L0_attn_in['up_b'], 'L0_attn_down_w': _L0_attn_in['down_w'], 'L0_attn_down_b': _L0_attn_in['down_b'], 'L0_attn_ln_w': _L0_attn_in['ln_w'], 'L0_attn_ln_b': _L0_attn_in['ln_b'], 'L0_xattn_Wq': _L0_xattn_in['Wq'], 'L0_xattn_bq': _L0_xattn_in['bq'], 'L0_xattn_Wk': _L0_xattn_in['Wk'], 'L0_xattn_bk': _L0_xattn_in['bk'], 'L0_xattn_Wv': _L0_xattn_in['Wv'], 'L0_xattn_bv': _L0_xattn_in['bv'], 'L0_ffn_wg': _L0_ffn_in['wg'], 'L0_ffn_fc1_w': _L0_ffn_in['fc1_w'], 'L0_ffn_fc1_b': _L0_ffn_in['fc1_b'], 'L0_ffn_fc2_w': _L0_ffn_in['fc2_w'], 'L0_ffn_fc2_b': _L0_ffn_in['fc2_b'], 'L0_ffn_ln_gamma': _L0_ffn_in['ln_gamma'], 'L0_ffn_ln_beta': _L0_ffn_in['ln_beta']}

def reference(x, ctx_512, L0_attn_A_log, L0_attn_D_param, L0_attn_Wd, L0_attn_bd, L0_attn_WB, L0_attn_bB, L0_attn_WC, L0_attn_bC, L0_attn_Wr, L0_attn_br, L0_attn_up_w, L0_attn_up_b, L0_attn_down_w, L0_attn_down_b, L0_attn_ln_w, L0_attn_ln_b, L0_xattn_Wq, L0_xattn_bq, L0_xattn_Wk, L0_xattn_bk, L0_xattn_Wv, L0_xattn_bv, L0_ffn_wg, L0_ffn_fc1_w, L0_ffn_fc1_b, L0_ffn_fc2_w, L0_ffn_fc2_b, L0_ffn_ln_gamma, L0_ffn_ln_beta):
    import jax
    import jax.numpy as jnp

    def _L0_attn_ref(x, A_log, D_param, Wd, bd, WB, bB, WC, bC, Wr, br, up_w, up_b, down_w, down_b, ln_w, ln_b):
        import jax, jax.numpy as jnp
        import numpy as np
        D_MODEL, STATE, N_EXP, VOCAB = (128, 16, 4, 4000)
        B, L = (4, 256)
        EPS = 1e-05
        Bb, Ll, d = x.shape
        delta = jax.nn.softplus(jnp.einsum('bld,de->ble', x, Wd) + bd)
        Bm = jnp.einsum('bld,ds->bls', x, WB) + bB
        Cm = jnp.einsum('bld,ds->bls', x, WC) + bC
        A = -jnp.exp(A_log)

        def step(h, inps):
            x_t, d_t, B_t, C_t = inps
            bar_A = jnp.exp(jnp.minimum(d_t[:, :, None] * A, 2.0))
            bar_B = jnp.clip(d_t[:, :, None] * B_t[:, None, :], -2.0, 2.0)
            h = jnp.clip(bar_A * h + bar_B * x_t[:, :, None], -100.0, 100.0)
            y = jnp.sum(h * C_t[:, None, :], axis=-1) + x_t * D_param
            return (h, y)
        h0 = jnp.zeros((Bb, d, STATE), x.dtype)
        xs = (jnp.swapaxes(x, 0, 1), jnp.swapaxes(delta, 0, 1), jnp.swapaxes(Bm, 0, 1), jnp.swapaxes(Cm, 0, 1))
        _, ys = jax.lax.scan(step, h0, xs)
        ssm_out = jnp.swapaxes(ys, 0, 1)
        flat = ssm_out.reshape(-1, d)
        routing = jax.nn.softmax(flat @ Wr + br, axis=1)
        top1_w = jnp.max(routing, axis=1)
        top1_i = jnp.argmax(routing, axis=1)
        hid = jax.nn.silu(jnp.einsum('nd,edf->enf', flat, up_w) + up_b[:, None, :])
        all_out = jnp.einsum('enf,efd->end', hid, down_w) + down_b[:, None, :]
        sel = jnp.take_along_axis(jnp.swapaxes(all_out, 0, 1), top1_i[:, None, None], axis=1)[:, 0, :]
        moe_out = (sel * top1_w[:, None]).reshape(Bb, Ll, d)
        out = ssm_out + moe_out
        mu = jnp.mean(out, axis=-1, keepdims=True)
        var = jnp.mean((out - mu) ** 2, axis=-1, keepdims=True)
        return (out - mu) * jax.lax.rsqrt(var + EPS) * ln_w + ln_b

    def _L0_xattn_ref(query, key, value, Wq, bq, Wk, bk, Wv, bv):
        import jax, jax.numpy as jnp
        import numpy as np
        B, LQ, LK = (8, 256, 256)
        QD, KD, VD = (128, 64, 64)
        q = jnp.einsum('bld,de->ble', query, Wq) + bq
        k = jnp.einsum('bld,de->ble', key, Wk) + bk
        v = jnp.einsum('bld,de->ble', value, Wv) + bv
        scores = jnp.einsum('bqe,bke->bqk', q, k)
        attn = jax.nn.softmax(scores, axis=-1)
        out = jnp.einsum('bqk,bke->bqe', attn, v)
        return out

    def _L0_ffn_ref(hidden_states, wg, fc1_w, fc1_b, fc2_w, fc2_b, ln_gamma, ln_beta):
        import jax, jax.numpy as jnp
        import numpy as np
        TOP_K = 2
        CAP_FACTOR = 1.25
        EPS = 1.1920929e-07
        B, S, D = hidden_states.shape
        E = wg.shape[1]
        N = B * S
        k = TOP_K
        C = k * int(CAP_FACTOR * ((N + E - 1) // E))
        x = hidden_states.reshape(N, D)
        scores = jax.nn.softmax(x @ wg, axis=-1)
        gates, idx = jax.lax.top_k(scores, k)
        gates = gates / jnp.clip(jnp.sum(gates, -1, keepdims=True), EPS)
        masks = jax.nn.one_hot(idx, E, dtype=jnp.int32)
        counts = masks.sum(0)
        offsets = jnp.concatenate([jnp.zeros((1, E), jnp.int32), jnp.cumsum(counts, 0)[:-1]], 0)
        loc = jnp.cumsum(masks, 0) - 1 + offsets[None]
        loc_sel = (loc * masks).sum(-1)
        keep = loc_sel < C
        gates = gates * keep.astype(gates.dtype)
        pos = jnp.where(keep, idx * C + loc_sel, E * C)
        xk = jnp.broadcast_to(x[:, None, :], (N, k, D)).reshape(N * k, D)
        buf = jnp.zeros((E * C + 1, D), x.dtype).at[pos.reshape(-1)].set(xk)
        disp = buf[:E * C].reshape(E, C, D)
        h = jax.nn.silu(jnp.einsum('ecd,ehd->ech', disp, fc1_w) + fc1_b[:, None, :])
        y = jnp.einsum('ech,ehd->ecd', h, fc2_w) + fc2_b[:, None, :]
        ybuf = jnp.concatenate([y.reshape(E * C, D), jnp.zeros((1, D), y.dtype)], 0)
        combined = jnp.sum(gates[..., None] * ybuf[pos], axis=1)
        res = hidden_states + combined.reshape(B, S, D)
        mu = jnp.mean(res, -1, keepdims=True)
        var = jnp.var(res, -1, keepdims=True)
        return (res - mu) * jax.lax.rsqrt(var + 1e-05) * ln_gamma + ln_beta
    x = x + _L0_attn_ref(_layernorm(x, axis=-1), L0_attn_A_log, L0_attn_D_param, L0_attn_Wd, L0_attn_bd, L0_attn_WB, L0_attn_bB, L0_attn_WC, L0_attn_bC, L0_attn_Wr, L0_attn_br, L0_attn_up_w, L0_attn_up_b, L0_attn_down_w, L0_attn_down_b, L0_attn_ln_w, L0_attn_ln_b)
    x = x + _L0_xattn_ref(_layernorm(x, axis=-1), ctx_512, ctx_512, L0_xattn_Wq, L0_xattn_bq, L0_xattn_Wk, L0_xattn_bk, L0_xattn_Wv, L0_xattn_bv)
    x = x + _L0_ffn_ref(_layernorm(x, axis=-1), L0_ffn_wg, L0_ffn_fc1_w, L0_ffn_fc1_b, L0_ffn_fc2_w, L0_ffn_fc2_b, L0_ffn_ln_gamma, L0_ffn_ln_beta)
    return x

_drawn_inputs = setup_inputs


def setup_inputs(seed=0):
    import zlib

    import numpy as np

    out = dict(_drawn_inputs(seed))
    spreads = {'L0_attn_D_param': (1.0, 0.2),
     'L0_attn_bd': (0.0, 0.8),
     'L0_attn_bB': (0.0, 0.1),
     'L0_attn_bC': (0.0, 0.1),
     'L0_attn_br': (0.0, 0.573),
     'L0_attn_up_b': (0.0, 0.8),
     'L0_attn_down_b': (0.0, 0.472),
     'L0_attn_ln_w': (1.0, 0.2),
     'L0_attn_ln_b': (0.0, 0.1),
     'L0_xattn_bq': (0.0, 0.8),
     'L0_xattn_bk': (0.0, 0.8),
     'L0_xattn_bv': (0.0, 0.1),
     'L0_ffn_fc1_b': (0.0, 0.8),
     'L0_ffn_fc2_b': (0.0, 0.351),
     'L0_ffn_ln_gamma': (1.0, 0.2),
     'L0_ffn_ln_beta': (0.0, 0.1)}
    factors = {'L0_attn_Wr': 3.909,
     'L0_attn_up_w': 6.103,
     'L0_attn_down_w': 5.659,
     'L0_xattn_Wq': 7.942,
     'L0_xattn_Wk': 7.441,
     'L0_ffn_fc1_w': 4.603,
     'L0_ffn_fc2_w': 4.184}
    for name, (base, spread) in spreads.items():
        noise = np.random.default_rng([zlib.crc32(name.encode()), seed]).standard_normal(out[name].shape)
        drawn = base * np.exp(spread * noise) if base else spread * noise
        out[name] = jnp.asarray(drawn.astype(out[name].dtype))
    for name, factor in factors.items():
        out[name] = (out[name] * factor).astype(out[name].dtype)
    return out
```

```python
from contextlib import ExitStack

import concourse.bass as bass
from concourse import mybir

ALU = mybir.AluOpType
ACT = mybir.ActivationFunctionType
AX = mybir.AxisListType
F32 = mybir.dt.float32
BF16 = mybir.dt.bfloat16
U32 = mybir.dt.uint32
I32 = mybir.dt.int32

P = 128
TILES = 16
GT = 4
G = TILES // GT
GW = GT * P
NS = 16
CTXD = 64
E1 = 4
E2 = 8
FT = 4
HID = FT * P
NROW = 2 * NS + 1
CAP = 2 * int(1.25 * ((TILES * P + E2 - 1) // E2))
EPS = 1e-5
GATE_EPS = 1.1920929e-07
CLIP_DB = 2.0
CLIP_H = 100.0
LOW = -3.0e38
C_UPB, C_FCB, C_BD, C_D, C_BQ, C_BK = 0, 16, 48, 49, 50, 51
NVEC = 52
A_RING, HC_RING = 3, 3


def decoder_layer(nc, x, ctx, A_log, D_param, Wd, bd, WB, bB, WC, bC, Wr, br, up_w, up_b, down_w,
                  down_b, ln_w, ln_b, Wq, bq, Wk, bk, Wv, bv, wg, fc1_w, fc1_b, fc2_w, fc2_b,
                  ln_gamma, ln_beta, out):
    with ExitStack() as st:
        def sb(name, shape, dt=F32):
            return st.enter_context(nc.sbuf_tensor(name, shape, dt))

        def sem(name):
            return st.enter_context(nc.semaphore(name))

        x_tok = sb("x_tok", [P, TILES, P])
        xn = sb("xn", [P, TILES, P])
        xT = sb("xT", [P, TILES * P])
        delta = sb("delta", [P, TILES * P])
        u = sb("u", [P, TILES * P])
        yD = sb("yD", [P, TILES * P])
        acc = sb("acc", [P, TILES, P])
        rows = sb("rows", [3 * NROW, TILES * P], BF16)
        parts = sb("parts", [P, GT, 3 * NROW], BF16)
        bcm = sb("bcm", [P, GT, NROW])
        rem = sb("rem", [P, GT, NROW])
        z0 = sb("z0", [P, GW])
        z1 = sb("z1", [P, GW])
        z2 = sb("z2", [P, GW])
        a = sb("a", [P, A_RING, GT, P])
        bu = sb("bu", [P, 2, GW])
        h = sb("h", [P, 2, GW])
        hc = sb("hc", [P, HC_RING, GW])
        hid = sb("hid", [P, 2, FT, GW])
        w1 = sb("w1", [P, E1, HID])
        w2 = sb("w2", [P, E1, FT, P])
        fc1T = sb("fc1T", [P, E2, HID])
        fc2 = sb("fc2", [P, E2, FT, P])
        fc1raw = hid[:, :, :, :].rearrange("p a b c -> p (a b c)").rearrange(
            "p (e t d) -> p e t d", e=E2, t=FT)
        ctx_tok = sb("ctx_tok", [P, TILES, CTXD])
        ctxT = sb("ctxT", [CTXD, TILES * P])
        kT = delta
        v_tok = u[:, :].rearrange("p (i d) -> p i d", d=P)
        ident = sb("ident", [P, P])
        ident_bf = sb("ident_bf", [P, P], BF16)
        diagD = sb("diagD", [P, P])
        tri = sb("tri", [P, P], BF16)
        ones_bf = sb("ones_bf", [P, P], BF16)
        ones_row = sb("ones_row", [1, P])
        selid = sb("selid", [3 * NROW, NROW], BF16)
        iota8 = sb("iota8", [P, 8])
        nhalf = sb("nhalf", [P, GT])
        vecs = sb("vecs", [NVEC, P])
        cols = sb("cols", [P, NVEC])
        Alog_sb = sb("Alog_sb", [P, NS])
        A_sb = sb("A_sb", [P, NS + 1])
        wd_sb = sb("wd_sb", [P, P])
        wbc_sb = sb("wbc_sb", [P, 2 * NS])
        wr_sb = sb("wr_sb", [P, E1])
        wq_sb = sb("wq_sb", [P, P])
        wk_sb = sb("wk_sb", [CTXD, P])
        wv_sb = sb("wv_sb", [CTXD, P])
        wg_sb = sb("wg_sb", [P, E2])
        bbc_b = sb("bbc_b", [P, 2 * NS])
        br_b = sb("br_b", [P, E1])
        bv_row = sb("bv_row", [1, P])
        db_row = sb("db_row", [1, E1 * P])
        fb_row = sb("fb_row", [1, E2 * P])
        affine = sb("affine", [P, 4, P])
        stats = sb("stats", [P, TILES, 6])
        mv = sb("mv", [P, TILES, 2])
        vpe = sb("vpe", [P, TILES])
        rstd = sb("rstd", [P, TILES])
        bound = sb("bound", [P, G])
        hmax = sb("hmax", [P, G])
        worst = sb("worst", [1, G])
        flags = sb("flags", [1, G], I32)
        lg = sb("lg", [P, TILES, 8])
        mx = sb("mx", [P, TILES, 8])
        ix = sb("ix", [P, TILES, 8], U32)
        ixf = sb("ixf", [P, TILES, 8])
        dif = sb("dif", [P, TILES, 8])
        ex = sb("ex", [P, TILES, 8])
        zs = sb("zs", [P, TILES])
        rz = sb("rz", [P, TILES])
        gate = sb("gate", [P, TILES, 8])
        g2 = sb("g2", [P, TILES, 2])
        den = sb("den", [P, TILES])
        oh = sb("oh", [P, 2, TILES, 8])
        oh_bf = sb("oh_bf", [P, 2, TILES, 8], BF16)
        pre_a = sb("pre_a", [P, 2, TILES, 8])
        pre_b = sb("pre_b", [P, 2, TILES, 8])
        loc = sb("loc", [P, 2, TILES, 8])
        locs = sb("locs", [P, 2, TILES])
        nmx = sb("nmx", [P, TILES])
        psums = sb("psums", [P, TILES])
        rps = sb("rps", [P, TILES])

        bank = [st.enter_context(nc.psum_tensor(f"bank{i}", [P, GW], F32)) for i in range(8)]

        ld_x = [sem(f"ld_x{g}") for g in range(G)]
        ld_vec = sem("ld_vec")
        ld_w = sem("ld_w")
        ld_ctx = sem("ld_ctx")
        ld_moe1 = sem("ld_moe1")
        ld_fc = sem("ld_fc")
        dve_done = sem("dve_done")
        slow_done = sem("slow_done")
        const_done = sem("const_done")
        pool_step = sem("pool_step")
        rstd_done = sem("rstd_done")
        cols_ps = sem("cols_ps")
        cols_done = sem("cols_done")
        xT_ps, xT_done = sem("xT_ps"), sem("xT_done")
        z_ps, bc_ps = sem("z_ps"), sem("bc_ps")
        sp_exp, sp_ln = sem("sp_exp"), sem("sp_ln")
        rows_ps, rows_done = sem("rows_ps"), sem("rows_done")
        A_exp = sem("A_exp")
        bmax_ps, amax_done = sem("bmax_ps"), sem("amax_done")
        worst_ps = sem("worst_ps")
        a_done = sem("a_done")
        B_ps, C_ps, y_ps = sem("B_ps"), sem("C_ps"), sem("y_ps")
        y_done = sem("y_done")
        fcT_ps, fcT_done = sem("fcT_ps"), sem("fcT_done")
        ctxT_ps, ctxT_done = sem("ctxT_ps"), sem("ctxT_done")
        kv_ps, kv_done = sem("kv_ps"), sem("kv_done")
        yT_ps, lg_ps, ex_done = sem("yT_ps"), sem("lg_ps"), sem("ex_done")
        up_ps, hid_done, dn_ps = sem("up_ps"), sem("hid_done"), sem("dn_ps")
        q_ps, q_done, sc_ps, p_done = sem("q_ps"), sem("q_done"), sem("sc_ps"), sem("p_done")
        pT_ps, pT_done, o_ps = sem("pT_ps"), sem("pT_done"), sem("o_ps")
        cum_ps = sem("cum_ps")
        stored = sem("stored")

        block = st.enter_context(nc.Block())
        N_W, N_VEC, N_MOE1, N_FC = 17, 6, 3, 3
        N_CONST = 10
        at = {}

        def grp(t, g):
            return t[:, g * GW:(g + 1) * GW]

        def tiles3(t):
            return t.rearrange("p (j n) -> p j n", n=P)

        @block.vector
        def _(v):
            n = [0]

            def do(ins):
                ins.then_inc(dve_done, 1)
                n[0] += 1
                return n[0]

            def link(ins):
                v.wait_ge(dve_done, do(ins))

            def ln_stats(src, g, eps=EPS):
                for j in range(GT):
                    do(v.bn_stats(stats[:, g * GT + j, :], src[:, g * GT + j, :]))
                v.wait_ge(dve_done, n[0])
                for j in range(GT):
                    do(v.bn_aggr(mv[:, g * GT + j, :], stats[:, g * GT + j, :]))
                v.wait_ge(dve_done, n[0])
                link(v.tensor_scalar_add(vpe[:, g * GT:(g + 1) * GT], mv[:, g * GT:(g + 1) * GT, 1], eps))

            def ln_apply(dst, src, g):
                for j in range(GT):
                    i = g * GT + j
                    do(v.tensor_scalar(dst[:, i, :], src[:, i, :], mv[:, i, 0:1], rstd[:, i:i + 1],
                                       ALU.subtract, ALU.mult))
                v.wait_ge(dve_done, n[0])

            for g in range(G):
                v.wait_ge(ld_x[g], 16)
                ln_stats(x_tok, g)
                at["vpe", 0, g] = n[0]
            for g in range(G):
                v.wait_ge(rstd_done, g + 1)
                ln_apply(xn, x_tok, g)
                at["xn", 0, g] = n[0]
            v.wait_ge(A_exp, 1)
            link(v.tensor_scalar_mul(A_sb[:, 0:NS], Alog_sb[:], -1.0))
            link(v.tensor_reduce(A_sb[:, NS:NS + 1], A_sb[:, 0:NS], AX.X, ALU.max))
            at["A"] = n[0]
            v.wait_ge(const_done, N_CONST)
            v.wait_ge(cols_done, 1)
            link(v.tensor_scalar_mul(diagD[:], ident[:], cols[:, C_D:C_D + 1]))
            at["diagD"] = n[0]
            for g in range(G):
                v.wait_ge(z_ps, g + 1)
                zp = bank[2 + g % 2]
                v.wait_ge(sp_exp, 2 * g + 1)
                do(v.tensor_scalar(grp(delta, g), zp[:], cols[:, C_BD:C_BD + 1], 0.0, ALU.add, ALU.max))
                at["z", g] = n[0]
                v.wait_ge(bc_ps, g + 1)
                v.wait_ge(ld_w, 16 * N_W)
                if g:
                    v.wait_ge(rows_ps, g)
                link(v.tensor_tensor(bcm[:, :, 0:2 * NS],
                                     bank[4 + g % 2][:, 0:GT * 2 * NS].rearrange("p (j s) -> p j s", j=GT),
                                     bbc_b[:].unsqueeze(1).to_broadcast([P, GT, 2 * NS]), ALU.add))
                at["bc", g] = n[0]
                link(v.tensor_reduce(bcm[:, :, 2 * NS], bcm[:, :, 0:NS], AX.X, ALU.max,
                                     apply_absolute_value=True))
                link(v.tensor_copy(parts[:, :, 0:NROW], bcm[:]))
                link(v.tensor_tensor(rem[:], bcm[:], parts[:, :, 0:NROW], ALU.subtract))
                link(v.tensor_copy(parts[:, :, NROW:2 * NROW], rem[:]))
                link(v.tensor_tensor(bcm[:], rem[:], parts[:, :, NROW:2 * NROW], ALU.subtract))
                link(v.tensor_copy(parts[:, :, 2 * NROW:3 * NROW], bcm[:]))
                at["parts", g] = n[0]
                v.wait_ge(sp_ln, g + 1)
                link(v.tensor_tensor(grp(delta, g), grp(delta, g), z1[:], ALU.add))
                at["delta", g] = n[0]
                v.wait_ge(xT_done, g + 1)
                link(v.tensor_tensor(grp(u, g), grp(delta, g), grp(xT, g), ALU.mult))
                v.wait_ge(bmax_ps, g + 1)
                link(v.tensor_tensor(z2[:], grp(delta, g), bank[6][:], ALU.mult))
                at["bmax", g] = n[0]
                link(v.tensor_reduce(bound[:, g:g + 1], z2[:], AX.X, ALU.max))
                link(v.scalar_tensor_tensor(bu[:, 1, :], grp(xT, g), -1.0, grp(xT, g), ALU.mult, ALU.max))
                link(v.tensor_tensor(z2[:], z2[:], bu[:, 1, :], ALU.mult))
                v.wait_ge(amax_done, g + 1)
                link(v.tensor_tensor_scan(bu[:, 0, :], a[:, 0, :, :].rearrange("p j n -> p (j n)"),
                                          z2[:], 0.0, ALU.mult, ALU.add))
                at["hbound", g] = n[0]
                link(v.tensor_reduce(hmax[:, g:g + 1], bu[:, 0, :], AX.X, ALU.max))
                link(v.tensor_scalar_mul(bound[:, g:g + 1], bound[:, g:g + 1], CLIP_H / CLIP_DB))
                link(v.tensor_tensor(bound[:, g:g + 1], bound[:, g:g + 1], hmax[:, g:g + 1], ALU.max))
                at["bound", g] = n[0]
            v.wait_ge(worst_ps, G)
            link(v.tensor_reduce(worst[:], bank[7][0:1, :].rearrange("p (g n) -> p g n", g=G), AX.X, ALU.max))
            at["worst"] = n[0]
            link(v.tensor_scalar(flags[:], worst[:], CLIP_H * 0.999, None, ALU.is_gt))

            def drive(k, clipped):
                g = k // NS
                v.wait_ge(B_ps, k + 1)
                if k >= 2:
                    v.wait_ge(dve_done, at["h", k - 2])
                do(v.tensor_tensor(bu[:, k % 2, :], grp(u, g), bank[k % 2][:], ALU.mult))
                at["b", k] = n[0]

            def scan(k, clipped):
                v.wait_ge(dve_done, at["b", k])
                v.wait_ge(a_done, k + 1)
                if k >= 2:
                    v.wait_ge(dve_done, at["hc", k - 2])
                if clipped:
                    scan_clipped(k)
                    ins = v.tensor_scalar(h[:, k % 2, :], h[:, k % 2, :], CLIP_H, -CLIP_H, ALU.min, ALU.max)
                else:
                    ins = v.tensor_tensor_scan(h[:, k % 2, :], a[:, k % A_RING, :, :].rearrange("p j n -> p (j n)"),
                                               bu[:, k % 2, :], 0.0, ALU.mult, ALU.add)
                do(ins)
                at["h", k] = n[0]

            def scan_clipped(k):
                g = k // NS
                hk = tiles3(h[:, k % 2, :])
                bk_ = tiles3(bu[:, k % 2, :])
                ak = a[:, k % A_RING, :, :]

                def step(ins):
                    ins.then_inc(slow_done, 1)
                    v.wait_ge(slow_done, 1)
                    v.sem_clear(slow_done)

                bk2 = bu[:, k % 2, :]
                step(v.scalar_tensor_tensor(z0[:], grp(xT, g), -1.0, grp(xT, g), ALU.mult, ALU.max))
                step(v.scalar_tensor_tensor(bk2, z0[:], CLIP_DB, bk2, ALU.mult, ALU.min))
                step(v.scalar_tensor_tensor(bk2, z0[:], -CLIP_DB, bk2, ALU.mult, ALU.max))
                step(v.tensor_scalar(hk[:, :, 0:1], bk_[:, :, 0:1], CLIP_H, -CLIP_H, ALU.min, ALU.max))
                with v.Fori(1, P) as t:
                    now, before = bass.ds(t, 1), bass.ds(t - 1, 1)
                    step(v.tensor_tensor(hk[:, :, now], ak[:, :, now], hk[:, :, before], ALU.mult))
                    step(v.tensor_tensor(hk[:, :, now], hk[:, :, now], bk_[:, :, now], ALU.add))
                    step(v.tensor_scalar(hk[:, :, now], hk[:, :, now], CLIP_H, -CLIP_H, ALU.min, ALU.max))

            def read_out(k, clipped):
                v.wait_ge(dve_done, at["h", k])
                v.wait_ge(C_ps, k + 1)
                if k >= HC_RING:
                    v.wait_ge(y_ps, k - HC_RING + 1)
                do(v.tensor_tensor(hc[:, k % HC_RING, :], h[:, k % 2, :], bank[2 + k % 2][:], ALU.mult))
                at["hc", k] = n[0]

            def group_scan(g, clipped):
                first, last = g * NS, g * NS + NS - 1
                drive(first, clipped)
                for k in range(first, last + 1):
                    if k < last:
                        drive(k + 1, clipped)
                    scan(k, clipped)
                    if k > first:
                        read_out(k - 1, clipped)
                read_out(last, clipped)

            for g in range(G):
                flag = v.value_load(flags[0:1, g:g + 1], min_val=0, max_val=1)
                before = n[0]
                with v.If(flag == 1):
                    group_scan(g, True)
                n[0] = before
                with v.Else():
                    group_scan(g, False)

            for g in range(G):
                v.wait_ge(yT_ps, g + 1)
                do(v.tensor_copy(acc[:, g * GT:(g + 1) * GT, :], tiles3(bank[6 + g % 2][:])))
                at["yT", g] = n[0]

            def route(logits, first):
                for i in range(TILES):
                    do(v.max(mx[:, i, :], lg[:, i, :]))
                v.wait_ge(dve_done, n[0])
                for i in range(TILES):
                    do(v.max_index(ix[:, i, :], mx[:, i, :], lg[:, i, :]))
                v.wait_ge(dve_done, n[0])
                do(v.tensor_copy(ixf[:], ix[:]))
                link(v.tensor_tensor(dif[:], lg[:], mx[:, :, 0:1].to_broadcast([P, TILES, 8]), ALU.subtract))
                at["dif", first] = n[0]
                v.wait_ge(ex_done, 1 + first)
                link(v.tensor_reduce(zs[:], ex[:], AX.X, ALU.add))
                link(v.reciprocal(rz[:], zs[:]))

            link(v.memset(lg[:], LOW))
            v.wait_ge(lg_ps, 1)
            link(v.tensor_tensor(lg[:, :, 0:E1], bank[0][:, 0:TILES * E1].rearrange("p (i e) -> p i e", e=E1),
                                 br_b[:].unsqueeze(1).to_broadcast([P, TILES, E1]), ALU.add))
            at["lg", 0] = n[0]
            route(lg, 0)
            link(v.tensor_tensor(gate[:], ixf[:, :, 0:1].to_broadcast([P, TILES, 8]),
                                 iota8[:].unsqueeze(1).to_broadcast([P, TILES, 8]), ALU.is_equal))
            link(v.tensor_tensor(gate[:], gate[:], rz[:].unsqueeze(2).to_broadcast([P, TILES, 8]), ALU.mult))

            def mixture(experts, base):
                for m in range(experts * G):
                    e, g = m // G, m % G
                    v.wait_ge(dn_ps, base + m + 1)
                    v.wait_ge(dve_done, at.get(("acc", base + m - G), n[0]))
                    for j in range(GT):
                        i = g * GT + j
                        do(v.scalar_tensor_tensor(acc[:, i, :], bank[4 + (base + m) % 2][:, j * P:(j + 1) * P],
                                                  gate[:, i, e:e + 1], acc[:, i, :], ALU.mult, ALU.add))
                    at["acc", base + m] = n[0]
                v.wait_ge(dve_done, n[0])

            mixture(E1, 0)

            def affine_add(g, src, w, b, res, dst):
                sl = slice(g * GT, (g + 1) * GT)
                link(v.tensor_tensor(src[:, sl, :], src[:, sl, :],
                                     affine[:, w, :].unsqueeze(1).to_broadcast([P, GT, P]), ALU.mult))
                link(v.tensor_tensor(src[:, sl, :], src[:, sl, :],
                                     affine[:, b, :].unsqueeze(1).to_broadcast([P, GT, P]), ALU.add))
                link(v.tensor_tensor(dst[:, sl, :], src[:, sl, :], res[:, sl, :], ALU.add))

            for g in range(G):
                ln_stats(acc, g)
                at["vpe", 1, g] = n[0]
            for g in range(G):
                v.wait_ge(rstd_done, G + g + 1)
                ln_apply(acc, acc, g)
                affine_add(g, acc, 0, 1, x_tok, x_tok)
                ln_stats(x_tok, g)
                at["vpe", 2, g] = n[0]
            for g in range(G):
                v.wait_ge(rstd_done, 2 * G + g + 1)
                ln_apply(xn, x_tok, g)
                at["xn", 1, g] = n[0]
            for g in range(G):
                sl = slice(g * GT, (g + 1) * GT)
                v.wait_ge(sc_ps, g + 1)
                link(v.tensor_reduce(nmx[:, sl], tiles3(bank[2 + g % 2][:]), AX.X, ALU.max, negate=True))
                at["nmx", g] = n[0]
            for g in range(G):
                sl = slice(g * GT, (g + 1) * GT)
                v.wait_ge(p_done, g + 1)
                link(v.reciprocal(rps[:, sl], psums[:, sl]))
                v.wait_ge(o_ps, g + 1)
                for j in range(GT):
                    i = g * GT + j
                    do(v.scalar_tensor_tensor(x_tok[:, i, :], bank[6 + g % 2][:, j * P:(j + 1) * P],
                                              rps[:, i:i + 1], x_tok[:, i, :], ALU.mult, ALU.add))
                v.wait_ge(dve_done, n[0])
                at["x2", g] = n[0]
                ln_stats(x_tok, g)
                at["vpe", 3, g] = n[0]
            for g in range(G):
                v.wait_ge(rstd_done, 3 * G + g + 1)
                ln_apply(xn, x_tok, g)
                at["xn", 2, g] = n[0]
                link(v.tensor_copy(acc[:, g * GT:(g + 1) * GT, :], xn[:, g * GT:(g + 1) * GT, :]))
            v.wait_ge(lg_ps, 2)
            link(v.tensor_copy(lg[:], bank[6][:, 0:TILES * E2].rearrange("p (i e) -> p i e", e=E2)))
            at["lg", 1] = n[0]
            route(lg, 1)
            link(v.tensor_tensor(dif[:, :, 0:2], mx[:, :, 0:2], mx[:, :, 0:1].to_broadcast([P, TILES, 2]),
                                 ALU.subtract))
            at["dif2"] = n[0]
            v.wait_ge(ex_done, 3)
            link(v.tensor_tensor(g2[:], ex[:, :, 0:2], rz[:].unsqueeze(2).to_broadcast([P, TILES, 2]), ALU.mult))
            link(v.tensor_tensor(den[:], g2[:, :, 0], g2[:, :, 1], ALU.add))
            link(v.tensor_scalar_max(den[:], den[:], GATE_EPS))
            link(v.reciprocal(den[:], den[:]))
            link(v.tensor_tensor(g2[:], g2[:], den[:].unsqueeze(2).to_broadcast([P, TILES, 2]), ALU.mult))
            for r in range(2):
                link(v.tensor_tensor(oh[:, r, :, :], ixf[:, :, r:r + 1].to_broadcast([P, TILES, 8]),
                                     iota8[:].unsqueeze(1).to_broadcast([P, TILES, 8]), ALU.is_equal))
            link(v.tensor_copy(oh_bf[:], oh[:]))
            at["oh"] = n[0]
            v.wait_ge(cum_ps, 1)
            link(v.tensor_copy(pre_a[:], bank[7][:, 256:512].rearrange("p (r i e) -> p r i e", r=2, i=TILES)))
            src, dst = pre_a, pre_b
            for step in (1, 2, 4, 8):
                do(v.tensor_copy(dst[:, :, 0:step, :], src[:, :, 0:step, :]))
                link(v.tensor_tensor(dst[:, :, step:, :], src[:, :, step:, :], src[:, :, 0:TILES - step, :], ALU.add))
                src, dst = dst, src
            link(v.tensor_scalar_add(loc[:], bank[7][:, 0:256].rearrange("p (r i e) -> p r i e", r=2, i=TILES), -1.0))
            at["cum"] = n[0]
            link(v.tensor_tensor(loc[:, :, 1:, :], loc[:, :, 1:, :], src[:, :, 0:TILES - 1, :], ALU.add))
            link(v.tensor_tensor(loc[:, 1, :, :], loc[:, 1, :, :],
                                 src[:, 0, TILES - 1:TILES, :].to_broadcast([P, TILES, 8]), ALU.add))
            link(v.tensor_tensor(loc[:], loc[:], oh[:], ALU.mult))
            link(v.tensor_reduce(locs[:], loc[:], AX.X, ALU.add))
            for r in range(2):
                link(v.tensor_scalar(locs[:, r, :], locs[:, r, :], CAP - 0.5, None, ALU.is_lt))
                link(v.tensor_tensor(locs[:, r, :], locs[:, r, :], g2[:, :, r], ALU.mult))
                link(v.tensor_tensor(oh[:, r, :, :], oh[:, r, :, :],
                                     locs[:, r, :].unsqueeze(2).to_broadcast([P, TILES, 8]), ALU.mult))
            link(v.tensor_tensor(gate[:], oh[:, 0, :, :], oh[:, 1, :, :], ALU.add))

            mixture(E2, E1 * G)
            for g in range(G):
                ln_stats(acc, g)
                at["vpe", 4, g] = n[0]
            for g in range(G):
                v.wait_ge(rstd_done, 4 * G + g + 1)
                ln_apply(acc, acc, g)
                affine_add(g, acc, 2, 3, x_tok, acc)
                at["out", g] = n[0]

        @block.sync
        def _(sp):
            for g in range(G):
                sp.dma_start(x_tok[:, g * GT:(g + 1) * GT, :],
                             x[g * GT:(g + 1) * GT].rearrange("b t d -> t b d")).then_inc(ld_x[g], 16)
            sp.dma_start(ctx_tok[:], ctx.rearrange("b t d -> t b d")).then_inc(ld_ctx, 16)
            sp.dma_start(w1[:], up_w.rearrange("e d f -> d e f")).then_inc(ld_moe1, 16)
            sp.dma_start(w2[:], down_w.rearrange("e (t p) d -> p e t d", p=P)).then_inc(ld_moe1, 16)
            sp.dma_start(db_row[:], down_b.rearrange("(o e) d -> o (e d)", o=1)).then_inc(ld_moe1, 16)
            sp.dma_start(fc1raw, fc1_w.rearrange("e (t p) d -> p e t d", p=P)).then_inc(ld_fc, 16)
            sp.dma_start(fc2[:], fc2_w.rearrange("e (t p) d -> p e t d", p=P)).then_inc(ld_fc, 16)
            sp.dma_start(fb_row[:], fc2_b.rearrange("(o e) d -> o (e d)", o=1)).then_inc(ld_fc, 16)
            for g in range(G):
                sp.wait_ge(dve_done, at["out", g])
                sp.dma_start(out[g * GT:(g + 1) * GT].rearrange("b t d -> t b d"),
                             acc[:, g * GT:(g + 1) * GT, :]).then_inc(stored, 16)
            sp.wait_ge(stored, 16 * G)

        @block.gpsimd
        def _(pool):
            made = [0]

            def step(ins):
                ins.then_inc(pool_step, 1)
                made[0] += 1

            step(pool.memset(ident[:], 0.0))
            step(pool.memset(ident_bf[:], 0.0))
            step(pool.memset(tri[:], 1.0))
            step(pool.memset(selid[:], 0.0))
            pool.memset(ones_bf[:], 1.0).then_inc(const_done, 1)
            pool.memset(ones_row[:], 1.0).then_inc(const_done, 1)
            pool.memset(nhalf[:], -0.5).then_inc(const_done, 1)
            pool.memset(a[:], 0.0).then_inc(const_done, 1)
            pool.iota(iota8[:], pattern=[[1, 8]], base=0, channel_multiplier=0,
                      allow_small_or_imprecise_dtypes=True).then_inc(const_done, 1)
            pool.wait_ge(pool_step, made[0])
            for m in (ident, ident_bf):
                pool.affine_select(out=m[:], in_=m[:], compare_op=ALU.not_equal, fill=1.0, base=0,
                                   pattern=[[-1, P]], channel_multiplier=1).then_inc(const_done, 1)
            pool.affine_select(out=tri[:], in_=tri[:], compare_op=ALU.is_ge, fill=0.0, base=0,
                               pattern=[[1, P]], channel_multiplier=-1).then_inc(const_done, 1)
            for r in range(3):
                ins = pool.affine_select(out=selid[:], in_=selid[:], compare_op=ALU.not_equal, fill=1.0,
                                         base=-NROW * r, pattern=[[-1, NROW]], channel_multiplier=1)
                if r < 2:
                    step(ins)
                    pool.wait_ge(pool_step, made[0])
                else:
                    ins.then_inc(const_done, 1)
            pool.wait_ge(const_done, 9)
            pool.memset(bound[:], 0.0).then_inc(const_done, 1)
            for k in range(5):
                for g in range(G):
                    pool.wait_ge(dve_done, at["vpe", k, g])
                    pool.tensor_tensor(rstd[:, g * GT:(g + 1) * GT], vpe[:, g * GT:(g + 1) * GT],
                                       nhalf[:], ALU.pow).then_inc(rstd_done, 1)

        @block.scalar
        def _(act):
            for src, r, k in ((up_b.rearrange("e (t p) -> (e t) p", p=P), C_UPB, E1 * FT),
                              (fc1_b.rearrange("e (t p) -> (e t) p", p=P), C_FCB, E2 * FT),
                              (bd.rearrange("(o d) -> o d", o=1), C_BD, 1),
                              (D_param.rearrange("(o d) -> o d", o=1), C_D, 1),
                              (bq.rearrange("(o d) -> o d", o=1), C_BQ, 1),
                              (bk.rearrange("(o d) -> o d", o=1), C_BK, 1)):
                act.dma_start(vecs[r:r + k, :], src).then_inc(ld_vec, 16)

            def load(dst, src):
                act.dma_start(dst, src).then_inc(ld_w, 16)

            def everywhere(t, k):
                return t.rearrange("(o d) -> o d", o=1).broadcast_to([P, k])

            load(Alog_sb[:], A_log)
            load(wd_sb[:], Wd)
            load(wbc_sb[:, 0:NS], WB)
            load(wbc_sb[:, NS:2 * NS], WC)
            load(bbc_b[:, 0:NS], everywhere(bB, NS))
            load(bbc_b[:, NS:2 * NS], everywhere(bC, NS))
            load(wr_sb[:], Wr)
            load(br_b[:], everywhere(br, E1))
            load(wq_sb[:], Wq)
            load(wk_sb[:], Wk)
            load(wv_sb[:], Wv)
            load(bv_row[:], bv.rearrange("(o d) -> o d", o=1))
            load(wg_sb[:], wg)
            for k, t in enumerate((ln_w, ln_b, ln_gamma, ln_beta)):
                load(affine[:, k, :], everywhere(t, P))

            act.wait_ge(ld_w, 16 * N_W)
            act.activation(Alog_sb[:], Alog_sb[:], ACT.Exp).then_inc(A_exp, 1)
            act.wait_ge(cols_ps, 1)
            act.activation(cols[:], bank[7][:, 0:NVEC], ACT.Copy).then_inc(cols_done, 1)
            for g in range(G):
                act.wait_ge(xT_ps, g + 1)
                act.activation(grp(xT, g), bank[g % 2][:], ACT.Copy).then_inc(xT_done, 1)
            for g in range(G):
                act.wait_ge(z_ps, g + 1)
                act.activation(z0[:], bank[2 + g % 2][:], ACT.Abs,
                               bias=cols[:, C_BD:C_BD + 1]).then_inc(sp_exp, 1)
                act.wait_ge(sp_exp, 2 * g + 1)
                act.activation(z0[:], z0[:], ACT.Exp, scale=-1.0).then_inc(sp_exp, 1)
                act.wait_ge(sp_exp, 2 * g + 2)
                if g:
                    act.wait_ge(dve_done, at["delta", g - 1])
                act.activation(z1[:], z0[:], ACT.Ln, bias=1.0).then_inc(sp_ln, 1)
                act.wait_ge(rows_ps, g + 1)
                act.activation(grp(rows, g), bank[7][0:3 * NROW, 0:GW // 2].bitcast(BF16),
                               ACT.Copy).then_inc(rows_done, 1)
                act.wait_ge(dve_done, at["delta", g])
                if g:
                    act.wait_ge(dve_done, at["hbound", g - 1])
                act.activation(a[:, 0, :, 1:P], tiles3(grp(delta, g))[:, :, 1:P], ACT.Exp,
                               scale=A_sb[:, NS:NS + 1]).then_inc(amax_done, 1)

            def copy_fc(e):
                act.wait_ge(fcT_ps, e + 1)
                act.activation(fc1T[:, e, :], bank[6 + e % 2][:], ACT.Copy).then_inc(fcT_done, 1)

            def copy_y(g):
                act.wait_ge(y_ps, NS * (g + 1))
                act.activation(grp(yD, g), bank[4 + g % 2][:], ACT.Copy).then_inc(y_done, 1)

            act.wait_ge(dve_done, at["hbound", G - 1])
            for k in range(G * NS):
                g, s = k // NS, k % NS
                if k >= A_RING:
                    act.wait_ge(dve_done, at["h", k - A_RING])
                act.activation(a[:, k % A_RING, :, 1:P], tiles3(grp(delta, g))[:, :, 1:P], ACT.Exp,
                               scale=A_sb[:, s:s + 1]).then_inc(a_done, 1)
                if s == 6 and g:
                    copy_y(g - 1)
                if k % 5 == 4 and k // 5 < E2:
                    copy_fc(k // 5)
                if k % 4 == 3 and k >= 44 and (k - 44) // 4 < G:
                    act.wait_ge(ctxT_ps, (k - 44) // 4 + 1)
                    act.activation(grp(ctxT, (k - 44) // 4), bank[6 + (k // 4) % 2][0:CTXD, :],
                                   ACT.Copy).then_inc(ctxT_done, 1)
            copy_y(G - 1)
            for g in range(G):
                act.wait_ge(kv_ps, 2 * g + 1)
                act.activation(grp(kT, g), bank[0][:], ACT.Identity,
                               bias=cols[:, C_BK:C_BK + 1]).then_inc(kv_done, 1)
                act.wait_ge(kv_ps, 2 * g + 2)
                act.activation(v_tok[:, g * GT:(g + 1) * GT, :], tiles3(bank[1][:]),
                               ACT.Copy).then_inc(kv_done, 1)

            def exp_scores(k):
                act.wait_ge(dve_done, at["dif", k])
                act.activation(ex[:], dif[:], ACT.Exp).then_inc(ex_done, 1)

            exp_scores(0)

            def silus(experts, base, col):
                for m in range(experts * G):
                    e = m // G
                    for f in range(FT):
                        k = (base + m) * FT + f
                        act.wait_ge(up_ps, k + 1)
                        if f == 0 and base + m >= 2:
                            act.wait_ge(dn_ps, base + m - 1)
                        act.activation(hid[:, (base + m) % 2, f, :], bank[k % 4][:], ACT.Silu,
                                       bias=cols[:, col + e * FT + f:col + e * FT + f + 1]).then_inc(hid_done, 1)

            silus(E1, 0, C_UPB)
            for g in range(G):
                act.wait_ge(xT_ps, G + g + 1)
                act.activation(grp(xT, g), bank[6 + g % 2][:], ACT.Copy).then_inc(xT_done, 1)
                act.wait_ge(q_ps, g + 1)
                act.activation(grp(yD, g), bank[g % 2][:], ACT.Identity,
                               bias=cols[:, C_BQ:C_BQ + 1]).then_inc(q_done, 1)
            for g in range(G):
                act.wait_ge(dve_done, at["nmx", g])
                for j in range(GT):
                    i = g * GT + j
                    ins = act.activation(xn[:, i, :], bank[2 + g % 2][:, j * P:(j + 1) * P], ACT.Exp,
                                         bias=nmx[:, i:i + 1], accum_out=psums[:, i:i + 1])
                    ins.then_inc(p_done if j == GT - 1 else A_exp, 1)
                act.wait_ge(pT_ps, g + 1)
                act.activation(grp(xT, g), bank[4 + g % 2][:], ACT.Copy).then_inc(pT_done, 1)
            for g in range(G):
                act.wait_ge(xT_ps, 2 * G + g + 1)
                act.activation(grp(xT, g), bank[g % 2][:], ACT.Copy).then_inc(xT_done, 1)
            exp_scores(1)
            act.wait_ge(dve_done, at["dif2"])
            act.activation(ex[:, :, 0:2], dif[:, :, 0:2], ACT.Exp).then_inc(ex_done, 1)
            silus(E2, E1 * G, C_FCB)

        @block.tensor
        def _(pe):
            pe.wait_ge(const_done, N_CONST)
            pe.wait_ge(ld_vec, 16 * N_VEC)
            pe.transpose(bank[7][:, 0:NVEC], vecs[:], ident[0:NVEC, 0:NVEC]).then_inc(cols_ps, 1)

            def transpose_xn(k, g, b):
                pe.wait_ge(dve_done, at["xn", k, g])
                for j in range(GT):
                    ins = pe.transpose(b[:, j * P:(j + 1) * P], xn[:, g * GT + j, :], ident[:])
                ins.then_inc(xT_ps, 1)

            for g in range(G):
                if g >= 2:
                    pe.wait_ge(xT_done, g - 1)
                transpose_xn(0, g, bank[g % 2])
            pe.wait_ge(ld_w, 16 * N_W)
            pe.wait_ge(cols_done, 1)
            for g in range(G):
                pe.wait_ge(xT_done, g + 1)
                if g >= 2:
                    pe.wait_ge(dve_done, at["z", g - 2])
                pe.matmul(bank[2 + g % 2][:], wd_sb[:], grp(xT, g), start=True, stop=True).then_inc(z_ps, 1)
                if g >= 2:
                    pe.wait_ge(dve_done, at["bc", g - 2])
                for j in range(GT):
                    ins = pe.matmul(bank[4 + g % 2][:, j * 2 * NS:(j + 1) * 2 * NS],
                                    xT[:, (g * GT + j) * P:(g * GT + j + 1) * P], wbc_sb[:],
                                    start=True, stop=True)
                ins.then_inc(bc_ps, 1)
                pe.wait_ge(dve_done, at["parts", g])
                if g:
                    pe.wait_ge(rows_done, g)
                for j in range(GT):
                    ins = pe.transpose(bank[7][0:3 * NROW, j * P // 2:(j + 1) * P // 2].bitcast(BF16),
                                       parts[:, j, :], ident_bf[:])
                ins.then_inc(rows_ps, 1)
                pe.wait_ge(rows_done, g + 1)
                if g:
                    pe.wait_ge(dve_done, at["bmax", g - 1])
                pe.matmul(bank[6][:], selid[:, NROW - 1:NROW].to_broadcast([3 * NROW, P]), grp(rows, g),
                          start=True, stop=True).then_inc(bmax_ps, 1)
            for g in range(G):
                pe.wait_ge(dve_done, at["bound", g])
                pe.transpose(bank[7][0:1, g * P:(g + 1) * P], bound[:, g:g + 1], ident[:]).then_inc(worst_ps, 1)
            pe.wait_ge(dve_done, at["worst"])

            def broadcast_row(out_bank, row, g, done):
                pe.matmul(out_bank[:], selid[:, row:row + 1].to_broadcast([3 * NROW, P]), grp(rows, g),
                          start=True, stop=True).then_inc(done, 1)

            def add_state(k):
                g, s = k // NS, k % NS
                if s == 0:
                    if g >= 2:
                        pe.wait_ge(y_done, g - 1)
                    if g == 0:
                        pe.wait_ge(dve_done, at["diagD"])
                    pe.matmul(bank[4 + g % 2][:], diagD[:], grp(xT, g), start=True, stop=False)
                pe.wait_ge(dve_done, at["hc", k])
                pe.matmul(bank[4 + g % 2][:], ident[:], hc[:, k % HC_RING, :], start=False,
                          stop=(s == NS - 1)).then_inc(y_ps, 1)

            for k in range(G * NS):
                g, s = k // NS, k % NS
                if k >= 2:
                    pe.wait_ge(dve_done, at["b", k - 2])
                broadcast_row(bank[k % 2], s, g, B_ps)
                if k >= 2:
                    pe.wait_ge(dve_done, at["hc", k - 2])
                broadcast_row(bank[2 + k % 2], NS + s, g, C_ps)
                if k >= 2:
                    add_state(k - 2)
                if k % 5 == 3 and k // 5 < E2:
                    e = k // 5
                    pe.wait_ge(ld_fc, 16 * N_FC)
                    if e >= 2:
                        pe.wait_ge(fcT_done, e - 1)
                    for f in range(FT):
                        ins = pe.transpose(bank[6 + e % 2][:, f * P:(f + 1) * P], fc1raw[:, e, f, :], ident[:])
                    ins.then_inc(fcT_ps, 1)
                if k % 4 == 2 and k >= 44 and (k - 44) // 4 < G:
                    c = (k - 44) // 4
                    pe.wait_ge(ld_ctx, 16)
                    pe.wait_ge(fcT_done, E2)
                    if c >= 2:
                        pe.wait_ge(ctxT_done, c - 1)
                    for j in range(GT):
                        ins = pe.transpose(bank[6 + (k // 4) % 2][0:CTXD, j * P:(j + 1) * P],
                                           ctx_tok[:, c * GT + j, :], ident[:])
                    ins.then_inc(ctxT_ps, 1)
            add_state(G * NS - 2)
            add_state(G * NS - 1)
            pe.wait_ge(ctxT_done, G)
            pe.wait_ge(a_done, G * NS)
            for g in range(G):
                if g:
                    pe.wait_ge(kv_done, 2 * g - 1)
                pe.matmul(bank[0][:], wk_sb[:], grp(ctxT, g), start=True, stop=True).then_inc(kv_ps, 1)
                if g:
                    pe.wait_ge(kv_done, 2 * g)
                for j in range(GT):
                    i = g * GT + j
                    pe.matmul(bank[1][:, j * P:(j + 1) * P], ones_row[:], bv_row[:], start=True, stop=False)
                    ins = pe.matmul(bank[1][:, j * P:(j + 1) * P], ctxT[:, i * P:(i + 1) * P], wv_sb[:],
                                    start=False, stop=True)
                ins.then_inc(kv_ps, 1)
            pe.wait_ge(y_done, G)
            pe.wait_ge(kv_done, 2 * G - 1)
            for i in range(TILES):
                ins = pe.matmul(bank[0][:, i * E1:(i + 1) * E1], yD[:, i * P:(i + 1) * P], wr_sb[:],
                                start=True, stop=True)
            ins.then_inc(lg_ps, 1)
            for g in range(G):
                if g >= 2:
                    pe.wait_ge(dve_done, at["yT", g - 2])
                for j in range(GT):
                    i = g * GT + j
                    ins = pe.transpose(bank[6 + g % 2][:, j * P:(j + 1) * P], yD[:, i * P:(i + 1) * P], ident[:])
                ins.then_inc(yT_ps, 1)

            def mixture(experts, base, src, wa, wb, brow):
                def up(m):
                    e, g = m // G, m % G
                    for f in range(FT):
                        k = (base + m) * FT + f
                        if k >= 4:
                            pe.wait_ge(hid_done, k - 3)
                        pe.matmul(bank[k % 4][:], wa[:, e, f * P:(f + 1) * P], grp(src, g),
                                  start=True, stop=True).then_inc(up_ps, 1)

                def down(m):
                    e, g = m // G, m % G
                    pe.wait_ge(hid_done, (base + m + 1) * FT)
                    if m >= 2:
                        pe.wait_ge(dve_done, at["acc", base + m - 2])
                    b = bank[4 + (base + m) % 2]
                    for j in range(GT):
                        o = b[:, j * P:(j + 1) * P]
                        pe.matmul(o, ones_row[:], brow[:, e * P:(e + 1) * P], start=True, stop=False)
                        for f in range(FT):
                            ins = pe.matmul(o, hid[:, (base + m) % 2, f, j * P:(j + 1) * P], wb[:, e, f, :],
                                            start=False, stop=(f == FT - 1))
                    ins.then_inc(dn_ps, 1)

                up(0)
                for m in range(1, experts * G):
                    up(m)
                    down(m - 1)
                down(experts * G - 1)

            pe.wait_ge(ld_moe1, 16 * N_MOE1)
            pe.wait_ge(dve_done, at["lg", 0])
            pe.wait_ge(kv_done, 2 * G)
            mixture(E1, 0, yD, w1, w2, db_row)
            def attend(g):
                pe.wait_ge(p_done, g + 1)
                if g >= 2:
                    pe.wait_ge(pT_done, g - 1)
                for j in range(GT):
                    ins = pe.transpose(bank[4 + g % 2][:, j * P:(j + 1) * P], xn[:, g * GT + j, :], ident[:])
                ins.then_inc(pT_ps, 1)
                pe.wait_ge(pT_done, g + 1)
                if g >= 2:
                    pe.wait_ge(dve_done, at["x2", g - 2])
                for j in range(GT):
                    i = g * GT + j
                    ins = pe.matmul(bank[6 + g % 2][:, j * P:(j + 1) * P], xT[:, i * P:(i + 1) * P],
                                    v_tok[:, i, :], start=True, stop=True)
                ins.then_inc(o_ps, 1)

            pe.wait_ge(hid_done, E1 * G * FT)
            for g in range(G):
                if g >= 2:
                    pe.wait_ge(xT_done, G + g - 1)
                transpose_xn(1, g, bank[6 + g % 2])
                pe.wait_ge(xT_done, G + g + 1)
                if g >= 2:
                    pe.wait_ge(q_done, g - 1)
                pe.matmul(bank[g % 2][:], wq_sb[:], grp(xT, g), start=True, stop=True).then_inc(q_ps, 1)
            for g in range(G):
                pe.wait_ge(q_done, g + 1)
                if g >= 2:
                    pe.wait_ge(p_done, g - 1)
                for j in range(GT):
                    i = g * GT + j
                    ins = pe.matmul(bank[2 + g % 2][:, j * P:(j + 1) * P], yD[:, i * P:(i + 1) * P],
                                    kT[:, i * P:(i + 1) * P], start=True, stop=True)
                ins.then_inc(sc_ps, 1)
                if g >= 1:
                    attend(g - 1)
            attend(G - 1)
            for g in range(G):
                if g >= 2:
                    pe.wait_ge(xT_done, 2 * G + g - 1)
                transpose_xn(2, g, bank[g % 2])
            pe.wait_ge(dve_done, at["x2", G - 1])
            for g in range(G):
                pe.wait_ge(xT_done, 2 * G + g + 1)
                for j in range(GT):
                    i = g * GT + j
                    ins = pe.matmul(bank[6][:, i * E2:(i + 1) * E2], xT[:, i * P:(i + 1) * P], wg_sb[:],
                                    start=True, stop=True)
            ins.then_inc(lg_ps, 1)
            pe.wait_ge(dve_done, at["oh"])
            flat = oh_bf[:].rearrange("p r i e -> p (r i e)")
            pe.matmul(bank[7][:, 0:256], tri[:], flat, start=True, stop=True)
            pe.matmul(bank[7][:, 256:512], ones_bf[:], flat, start=True, stop=True).then_inc(cum_ps, 1)
            pe.wait_ge(pT_done, G)
            mixture(E2, E1 * G, xT, fc1T, fc2, fb_row)


_INS = ['x', 'ctx_512', 'L0_attn_A_log', 'L0_attn_D_param', 'L0_attn_Wd', 'L0_attn_bd', 'L0_attn_WB',
        'L0_attn_bB', 'L0_attn_WC', 'L0_attn_bC', 'L0_attn_Wr', 'L0_attn_br', 'L0_attn_up_w',
        'L0_attn_up_b', 'L0_attn_down_w', 'L0_attn_down_b', 'L0_attn_ln_w', 'L0_attn_ln_b',
        'L0_xattn_Wq', 'L0_xattn_bq', 'L0_xattn_Wk', 'L0_xattn_bk', 'L0_xattn_Wv', 'L0_xattn_bv',
        'L0_ffn_wg', 'L0_ffn_fc1_w', 'L0_ffn_fc1_b', 'L0_ffn_fc2_w', 'L0_ffn_fc2_b',
        'L0_ffn_ln_gamma', 'L0_ffn_ln_beta']


def kernel(**inputs):
    import numpy as _np
    import concourse.bacc as _bacc
    from concourse import mybir as _mybir
    from concourse.bass_utils import run_bass_kernel_spmd as _run

    nc = _bacc.Bacc("TRN2", target_bir_lowering=False, num_devices=1)
    arrays, args = {}, []
    for name in _INS:
        arr = _np.ascontiguousarray(inputs[name])
        arrays[f"in_{name}_dram"] = arr
        args.append(nc.dram_tensor(f"in_{name}_dram", arr.shape, _mybir.dt.from_np(arr.dtype),
                                   kind="ExternalInput").ap())
    args.append(nc.dram_tensor("out_0_dram", (TILES, P, P), F32, kind="ExternalOutput").ap())
    decoder_layer(nc, *args)
    r = _run(nc, [arrays], core_ids=[0])
    return r.results[0]["out_0_dram"]
```

```python
from contextlib import ExitStack

import concourse.bass as bass
from concourse import mybir

ALU = mybir.AluOpType
ACT = mybir.ActivationFunctionType
AX = mybir.AxisListType
F32 = mybir.dt.float32
BF16 = mybir.dt.bfloat16
U32 = mybir.dt.uint32
I32 = mybir.dt.int32

P = 128
TILES = 16
GT = 4
G = TILES // GT
GW = GT * P
TOKENS = TILES * P
NS = 16
UNITS = G * NS
CTXD = 64
E1 = 4
E2 = 8
FT = 4
HID = FT * P
NROW = 2 * NS + 1
CAP = 2 * int(1.25 * ((TOKENS + E2 - 1) // E2))
CT = CAP // P
SLOTS = E2 * CAP
HALF = CAP // 2
QN = SLOTS // GW
ROW = P + 1
NOWHERE = 0x7F000000
EPS = 1e-5
GATE_EPS = 1.1920929e-07
CLIP_DB = 2.0
CLIP_H = 100.0
LOW = -3.0e38
C_UPB, C_FCB, C_BD, C_D, C_BQ, C_BK = 0, 16, 48, 49, 50, 51
NVEC = 52
A_RING, A_BATCH, HC_RING = 8, 4, 3

PRE0 = -NS


def pre_at(k, step):
    g, r = divmod(k - PRE0 - step, NS)
    return g if r == 0 and 0 <= g < G else None


def mix_at(k, step):
    g, r = divmod(k - NS - 1 - step, NS)
    return g if r == 0 and 0 <= g < G else None


def kv_at(k, step):
    g, r = divmod(k - NS - 9 - step, NS)
    return g if r == 0 and 0 <= g < G else None


def att_at(k, step):
    g, r = divmod(k - NS - 22 - step, NS)
    return g if r == 0 and 0 <= g < G else None


FC_SLOT = 7
FIRST_SLOT = PRE0
LAST_SLOT = NS * G + 22 + 21


def decoder_layer(nc, x, ctx, A_log, D_param, Wd, bd, WB, bB, WC, bC, Wr, br, up_w, up_b, down_w,
                  down_b, ln_w, ln_b, Wq, bq, Wk, bk, Wv, bv, wg, fc1_w, fc1_b, fc2_w, fc2_b,
                  ln_gamma, ln_beta, out):
    with ExitStack() as st:
        def sb(name, shape, dt=F32):
            return st.enter_context(nc.sbuf_tensor(name, shape, dt))

        def sem(name):
            return st.enter_context(nc.semaphore(name))

        x_tok = sb("x_tok", [P, TILES, P])
        xrow = sb("xrow", [P, TILES, ROW])
        xn = xrow[:, :, 0:P]
        xT = sb("xT", [P, TOKENS])
        delta = sb("delta", [P, TOKENS])
        u = sb("u", [P, TOKENS])
        yD = sb("yD", [P, TOKENS])
        acc = sb("acc", [P, TILES, P])
        rows = sb("rows", [3 * NROW, 2, GW], BF16)
        parts = sb("parts", [P, GT, 3 * NROW], BF16)
        bcm = sb("bcm", [P, GT, NROW])
        rem = sb("rem", [P, GT, NROW])
        z0 = sb("z0", [P, GW])
        z1 = sb("z1", [P, GW])
        z2 = sb("z2", [P, GW])
        absx = z0
        hb = z1
        am = sb("am", [P, GT, P])
        a = sb("a", [P, A_RING, GT, P])
        bu = sb("bu", [P, 2, GW])
        h = sb("h", [P, 2, GW])
        hc = sb("hc", [P, HC_RING, GW])
        hid2 = sb("hid2", [P, 2, FT, CAP])
        hid = hid2[:, :, :, 0:GW]
        w1 = sb("w1", [P, E1, HID])
        w2 = sb("w2", [P, E1, FT, P])
        fb_b = w1[:, 0:2, :].rearrange("p a (e d) -> p (a e) d", d=P)
        fc1T = sb("fc1T", [P, E2, HID])
        fc2 = sb("fc2", [P, E2, FT, P])
        fc1raw = hid2[:].rearrange("p a b c -> p (a b c)")[:, 0:E2 * HID].rearrange(
            "p (e t d) -> p e t d", e=E2, t=FT)
        xe_tok = sb("xe_tok", [P, 2, CT, ROW])
        xeT = w2[:].rearrange("p e t d -> p (e t d)")[:, 0:2 * CAP].rearrange("p (b n) -> p b n", b=2)
        yslot = sb("yslot", [P, 2, GW])
        first_y = yD[:, :].rearrange("p (i d) -> p i d", d=P)
        second_y = xT[:, :].rearrange("p (i d) -> p i d", d=P)
        blank = yslot[:].rearrange("p b n -> p (b n)")[:, 0:GT * ROW].rearrange("p (j n) -> p j n", n=ROW)
        token = sb("token", [P, TILES], I32)
        pos = sb("pos", [P, 2, TILES])
        posu = sb("posu", [P, 2, TILES], U32)
        slot_no = sb("slot_no", [P, CT])
        second = sb("second", [P, CT])
        dest = sb("dest", [P, E2, CT], U32)
        slots_in = nc.dram_tensor("slots_in", [SLOTS, ROW], F32)
        y_rows = nc.dram_tensor("y_rows", [2 * TOKENS, P], F32)
        ctx_tok = sb("ctx_tok", [P, TILES, CTXD])
        ctxT = sb("ctxT", [CTXD, GW])
        kT = delta
        v_tok = u[:, :].rearrange("p (i d) -> p i d", d=P)
        ident = sb("ident", [P, P])
        ident_bf = sb("ident_bf", [P, P], BF16)
        tri = sb("tri", [P, P], BF16)
        ones_bf = sb("ones_bf", [P, P], BF16)
        ones_row = sb("ones_row", [1, P])
        selid = sb("selid", [3 * NROW, NROW], BF16)
        iota8 = sb("iota8", [P, 8])
        nhalf = sb("nhalf", [P, GT])
        vecs = sb("vecs", [NVEC, P])
        cols = sb("cols", [P, NVEC])
        Alog_sb = sb("Alog_sb", [P, NS])
        A_sb = sb("A_sb", [P, NS + 1])
        wd_sb = sb("wd_sb", [P, P])
        wbc_sb = sb("wbc_sb", [P, 2 * NS])
        wr_sb = sb("wr_sb", [P, E1])
        wq_sb = sb("wq_sb", [P, P])
        wk_sb = sb("wk_sb", [CTXD, P])
        wv_sb = sb("wv_sb", [CTXD, P])
        wg_sb = sb("wg_sb", [P, E2])
        bbc_b = sb("bbc_b", [P, 2 * NS])
        br_b = sb("br_b", [P, E1])
        bv_row = sb("bv_row", [1, P])
        bias1 = sb("bias1", [8, P])
        gT = sb("gT", [8, GW])
        affine = sb("affine", [P, 4, P])
        stats = sb("stats", [P, TILES, 6])
        mv = sb("mv", [P, TILES, 2])
        vpe = sb("vpe", [P, TILES])
        rstd = sb("rstd", [P, TILES])
        bound = sb("bound", [P, G])
        hmax = sb("hmax", [P, G])
        worst = sb("worst", [1, G])
        flags = sb("flags", [1, G], I32)
        lg = sb("lg", [P, 2, TILES, 8])
        mx = sb("mx", [P, 2, TILES, 8])
        ix = sb("ix", [P, 2, TILES, 8], U32)
        ixf = sb("ixf", [P, 2, TILES, 8])
        dif = sb("dif", [P, 2, TILES, 10])
        ex = sb("ex", [P, 2, TILES, 10])
        zs = sb("zs", [P, 2, TILES])
        rz = sb("rz", [P, 2, TILES])
        gate = sb("gate", [P, TILES, 8])
        g2 = sb("g2", [P, TILES, 2])
        den = sb("den", [P, TILES])
        oh = sb("oh", [P, 2, TILES, 8])
        oh_bf = sb("oh_bf", [P, 2, TILES, 8], BF16)
        off = sb("off", [P, TILES + 1, 2, 8])
        loc = sb("loc", [P, 2, TILES, 8])
        locs = sb("locs", [P, 2, TILES])
        keep = sb("keep", [P, 2, TILES])
        ahead = sb("ahead", [P, TILES, 8])
        aheads = sb("aheads", [P, TILES])
        nmx = sb("nmx", [P, TILES])
        psums = sb("psums", [P, TILES])
        rps = sb("rps", [P, TILES])

        bank = [st.enter_context(nc.psum_tensor(f"bank{i}", [P, GW], F32)) for i in range(8)]
        B_BANK, C_BANK, MIX_BANK, DOWN_BANK, PRE_BANK, ATT_BANK = 0, 1, 2, 5, 6, 7
        UP_BANKS = (3, 4)

        ld_x = [sem(f"ld_x{g}") for g in range(G)]
        ld_vec, ld_w, ld_w2, ld_ctx = sem("ld_vec"), sem("ld_w"), sem("ld_w2"), sem("ld_ctx")
        ld_moe1, ld_fc, ld_fb, ld_affine = sem("ld_moe1"), sem("ld_fc"), sem("ld_fb"), sem("ld_affine")
        dve_done = sem("dve_done")
        slow_done = sem("slow_done")
        const_done, pool_step = sem("const_done"), sem("pool_step")
        rstd_done = [sem(f"rstd_done{k}") for k in range(5)]
        u_done, w_done = sem("u_done"), sem("w_done")
        xb_done, acc_done, fin_done = sem("xb_done"), sem("acc_done"), sem("fin_done")
        cols_ps, cols_done, A_exp = sem("cols_ps"), sem("cols_done"), sem("A_exp")
        xT_ps = [sem(f"xT_ps{k}") for k in range(3)]
        xT_done = [sem(f"xT_done{k}") for k in range(3)]
        z_ps, bc_ps, sp_exp, sp_ln = sem("z_ps"), sem("bc_ps"), sem("sp_exp"), sem("sp_ln")
        rows_ps, rows_done = sem("rows_ps"), sem("rows_done")
        bmax_ps, absx_done, amax_done = sem("bmax_ps"), sem("absx_done"), sem("amax_done")
        worst_ps = sem("worst_ps")
        a_done, B_ps, C_ps, y_started, summed = sem("a_done"), sem("B_ps"), sem("C_ps"), sem("y_started"), sem("summed")
        fcT_ps, fcT_done = sem("fcT_ps"), sem("fcT_done")
        ctxT_ps, ctxT_done = sem("ctxT_ps"), sem("ctxT_done")
        k_ps, k_done, v_ps, v_done = sem("k_ps"), sem("k_done"), sem("v_ps"), sem("v_done")
        lg_ps = [sem(f"lg_ps{k}") for k in range(2)]
        ex_done = [sem(f"ex_done{k}") for k in range(2)]
        gT_ps, gT_done, init_ps, init_done = sem("gT_ps"), sem("gT_done"), sem("init_ps"), sem("init_done")
        up_ps, hid_done, dn_ps = sem("up_ps"), sem("hid_done"), sem("dn_ps")
        q_ps, q_done, sc_ps, p_step, p_done = sem("q_ps"), sem("q_done"), sem("sc_ps"), sem("p_step"), sem("p_done")
        pT_ps, pT_done, o_ps, cum_ps = sem("pT_ps"), sem("pT_done"), sem("o_ps"), sem("cum_ps")
        zeroed, scattered = sem("zeroed"), sem("scattered")
        ld_xe = [sem(f"ld_xe{k}") for k in range(2)]
        xeT_ps, xeT_done = sem("xeT_ps"), sem("xeT_done")
        up2_ps, hid2_done, dn2_ps = sem("up2_ps"), sem("hid2_done"), sem("dn2_ps")
        y_sent = [sem(f"y_sent{k}") for k in range(2)]
        ld_y = [sem(f"ld_y{g}") for g in range(G)]
        stored = sem("stored")

        block = st.enter_context(nc.Block())
        N_W, N_W2, N_VEC, N_MOE1, N_FC = 6, 7, 6, 3, 2
        N_CONST = 14
        at = {}

        def grp(t, g):
            return t[:, g * GW:(g + 1) * GW]

        def gsl(g):
            return slice(g * GT, (g + 1) * GT)

        def tiles3(t):
            return t.rearrange("p (j n) -> p j n", n=P)

        @block.vector
        def _(v):
            n = [0]

            def do(ins):
                ins.then_inc(dve_done, 1)
                n[0] += 1
                return n[0]

            def link(ins):
                v.wait_ge(dve_done, do(ins))

            def ln_stats(src, g, k):
                for j in range(GT):
                    do(v.bn_stats(stats[:, g * GT + j, :], src[:, g * GT + j, :]))
                v.wait_ge(dve_done, n[0])
                for j in range(GT):
                    do(v.bn_aggr(mv[:, g * GT + j, :], stats[:, g * GT + j, :]))
                v.wait_ge(dve_done, n[0])
                do(v.tensor_scalar_add(vpe[:, gsl(g)], mv[:, gsl(g), 1], EPS))
                at["vpe", k, g] = n[0]

            def ln_apply(dst, src, g, k):
                v.wait_ge(rstd_done[k], g + 1)
                v.wait_ge(dve_done, at["vpe", k, g])
                for j in range(GT):
                    i = g * GT + j
                    do(v.tensor_scalar(dst[:, i, :], src[:, i, :], mv[:, i, 0:1], rstd[:, i:i + 1],
                                       ALU.subtract, ALU.mult))
                at["norm", k, g] = n[0]

            def ln_center(g, w):
                v.wait_ge(ld_affine, 16 * 4)
                v.wait_ge(dve_done, n[0])
                for j in range(GT):
                    i = g * GT + j
                    do(v.scalar_tensor_tensor(acc[:, i, :], acc[:, i, :], mv[:, i, 0:1], affine[:, w, :],
                                              ALU.subtract, ALU.mult))

            def ln_scale_add(dst, g):
                v.wait_ge(dve_done, n[0])
                for j in range(GT):
                    i = g * GT + j
                    do(v.scalar_tensor_tensor(dst[:, i, :], acc[:, i, :], rstd[:, i:i + 1], x_tok[:, i, :],
                                              ALU.mult, ALU.add))
                v.wait_ge(dve_done, n[0])

            def decays():
                v.wait_ge(A_exp, 1)
                link(v.tensor_scalar_mul(A_sb[:, 0:NS], Alog_sb[:], -1.0))
                link(v.tensor_reduce(A_sb[:, NS:NS + 1], A_sb[:, 0:NS], AX.X, ALU.max))
                at["A"] = n[0]
                v.wait_ge(const_done, N_CONST)
                v.wait_ge(cols_done, 1)

            def positive_part(g):
                v.wait_ge(z_ps, g + 1)
                v.wait_ge(sp_exp, 2 * g + 1)
                do(v.tensor_scalar(grp(delta, g), bank[MIX_BANK][:], cols[:, C_BD:C_BD + 1], 0.0,
                                   ALU.add, ALU.max))
                at["z", g] = n[0]

            def split_rows(g):
                v.wait_ge(bc_ps, g + 1)
                v.wait_ge(ld_w, 16 * N_W)
                if g:
                    v.wait_ge(rows_ps, g)
                link(v.tensor_tensor(bcm[:, :, 0:2 * NS],
                                     bank[PRE_BANK][:, 0:GT * 2 * NS].rearrange("p (j s) -> p j s", j=GT),
                                     bbc_b[:].unsqueeze(1).to_broadcast([P, GT, 2 * NS]), ALU.add))
                at["bc", g] = n[0]
                link(v.tensor_reduce(bcm[:, :, 2 * NS], bcm[:, :, 0:NS], AX.X, ALU.max,
                                     apply_absolute_value=True))
                link(v.tensor_copy(parts[:, :, 0:NROW], bcm[:]))
                link(v.tensor_tensor(rem[:], bcm[:], parts[:, :, 0:NROW], ALU.subtract))
                link(v.tensor_copy(parts[:, :, NROW:2 * NROW], rem[:]))
                link(v.tensor_tensor(bcm[:], rem[:], parts[:, :, NROW:2 * NROW], ALU.subtract))
                link(v.tensor_copy(parts[:, :, 2 * NROW:3 * NROW], bcm[:]))
                at["parts", g] = n[0]

            def add_log(g):
                v.wait_ge(sp_ln, g + 1)
                v.wait_ge(dve_done, at["z", g])
                do(v.tensor_tensor(grp(delta, g), grp(delta, g), z1[:], ALU.add))
                at["delta", g] = n[0]

            def bound_drive(g):
                v.wait_ge(bmax_ps, g + 1)
                v.wait_ge(dve_done, at["delta", g])
                if g:
                    v.wait_ge(dve_done, at["hbound", g - 1])
                link(v.tensor_tensor(z2[:], grp(delta, g), bank[PRE_BANK][:], ALU.mult))
                at["bmax", g] = n[0]
                do(v.tensor_reduce(bound[:, g:g + 1], z2[:], AX.X, ALU.max))
                at["boundmax", g] = n[0]

            def bound_state(g):
                v.wait_ge(amax_done, g + 1)
                v.wait_ge(w_done, g + 1)
                v.wait_ge(dve_done, at["boundmax", g])
                link(v.tensor_tensor_scan(hb[:], am[:].rearrange("p j n -> p (j n)"), z2[:], 0.0,
                                          ALU.mult, ALU.add))
                at["hbound", g] = n[0]
                link(v.tensor_reduce(hmax[:, g:g + 1], hb[:], AX.X, ALU.max))
                link(v.tensor_scalar_mul(bound[:, g:g + 1], bound[:, g:g + 1], CLIP_H / CLIP_DB))
                link(v.tensor_tensor(bound[:, g:g + 1], bound[:, g:g + 1], hmax[:, g:g + 1], ALU.max))
                at["bound", g] = n[0]

            def decide(g):
                v.wait_ge(worst_ps, g + 1)
                link(v.tensor_reduce(worst[:, g:g + 1], bank[PRE_BANK][0:1, 0:P], AX.X, ALU.max))
                at["worst", g] = n[0]
                link(v.tensor_scalar(flags[:, g:g + 1], worst[:, g:g + 1], CLIP_H * 0.999, None, ALU.is_gt))

            def drive(k):
                g = k // NS
                v.wait_ge(B_ps, k + 1)
                v.wait_ge(u_done, g + 1)
                if k >= 2:
                    v.wait_ge(dve_done, at["h", k - 2])
                do(v.tensor_tensor(bu[:, k % 2, :], grp(u, g), bank[B_BANK][:], ALU.mult))
                at["b", k] = n[0]

            def scan(k, clipped):
                v.wait_ge(dve_done, at["b", k])
                v.wait_ge(a_done, k + 1)
                if k >= 2:
                    v.wait_ge(dve_done, at["hc", k - 2])
                if clipped:
                    scan_clipped(k)
                    ins = v.tensor_scalar(h[:, k % 2, :], h[:, k % 2, :], CLIP_H, -CLIP_H, ALU.min, ALU.max)
                else:
                    ins = v.tensor_tensor_scan(h[:, k % 2, :], a[:, k % A_RING, :, :].rearrange("p j n -> p (j n)"),
                                               bu[:, k % 2, :], 0.0, ALU.mult, ALU.add)
                do(ins)
                at["h", k] = n[0]

            def scan_clipped(k):
                g = k // NS
                hk = tiles3(h[:, k % 2, :])
                bk_ = tiles3(bu[:, k % 2, :])
                ak = a[:, k % A_RING, :, :]

                def step(ins):
                    ins.then_inc(slow_done, 1)
                    v.wait_ge(slow_done, 1)
                    v.sem_clear(slow_done)

                bk2 = bu[:, k % 2, :]
                hk2 = h[:, k % 2, :]
                step(v.scalar_tensor_tensor(hk2, grp(xT, g), -1.0, grp(xT, g), ALU.mult, ALU.max))
                step(v.scalar_tensor_tensor(bk2, hk2, CLIP_DB, bk2, ALU.mult, ALU.min))
                step(v.scalar_tensor_tensor(bk2, hk2, -CLIP_DB, bk2, ALU.mult, ALU.max))
                step(v.tensor_scalar(hk[:, :, 0:1], bk_[:, :, 0:1], CLIP_H, -CLIP_H, ALU.min, ALU.max))
                with v.Fori(1, P) as t:
                    now, before = bass.ds(t, 1), bass.ds(t - 1, 1)
                    step(v.tensor_tensor(hk[:, :, now], ak[:, :, now], hk[:, :, before], ALU.mult))
                    step(v.tensor_tensor(hk[:, :, now], hk[:, :, now], bk_[:, :, now], ALU.add))
                    step(v.tensor_scalar(hk[:, :, now], hk[:, :, now], CLIP_H, -CLIP_H, ALU.min, ALU.max))

            def read_out(k):
                v.wait_ge(dve_done, at["h", k])
                v.wait_ge(C_ps, k + 1)
                if k >= HC_RING:
                    v.wait_ge(summed, k - HC_RING + 1)
                do(v.tensor_tensor(hc[:, k % HC_RING, :], h[:, k % 2, :], bank[C_BANK][:], ALU.mult))
                at["hc", k] = n[0]

            def rank(g, k):
                sl = gsl(g)
                v.wait_ge(dve_done, n[0])
                for i in range(g * GT, (g + 1) * GT):
                    do(v.max(mx[:, k, i, :], lg[:, k, i, :]))
                v.wait_ge(dve_done, n[0])
                for i in range(g * GT, (g + 1) * GT):
                    do(v.max_index(ix[:, k, i, :], mx[:, k, i, :], lg[:, k, i, :]))
                top = mx[:, k, sl, 0:1]
                do(v.tensor_tensor(dif[:, k, sl, 0:8], lg[:, k, sl, :], top.to_broadcast([P, GT, 8]), ALU.subtract))
                do(v.tensor_tensor(dif[:, k, sl, 8:10], mx[:, k, sl, 0:2], top.to_broadcast([P, GT, 2]),
                                   ALU.subtract))
                at["dif", k, g] = n[0]
                v.wait_ge(dve_done, n[0])
                do(v.tensor_copy(ixf[:, k, sl, 0:2], ix[:, k, sl, 0:2]))
                at["ixf", k, g] = n[0]

            def one_hot(dst, g, k, r):
                return v.tensor_tensor(dst, ixf[:, k, gsl(g), r:r + 1].to_broadcast([P, GT, 8]),
                                       iota8[:].unsqueeze(1).to_broadcast([P, GT, 8]), ALU.is_equal)

            def route_first(g):
                v.wait_ge(lg_ps[0], g + 1)
                v.wait_ge(ld_w2, 16 * N_W2)
                do(v.tensor_tensor(lg[:, 0, gsl(g), 0:E1],
                                   bank[MIX_BANK][:, 0:GT * E1].rearrange("p (i e) -> p i e", e=E1),
                                   br_b[:].unsqueeze(1).to_broadcast([P, GT, E1]), ALU.add))
                at["lg", 0, g] = n[0]
                rank(g, 0)

            def inverse_sum(g, k):
                sl = gsl(g)
                v.wait_ge(ex_done[k], g + 1)
                v.wait_ge(dve_done, at["ixf", k, g])
                link(v.tensor_reduce(zs[:, k, sl], ex[:, k, sl, 0:8], AX.X, ALU.add))
                link(v.reciprocal(rz[:, k, sl], zs[:, k, sl]))

            def gate_first(g):
                sl = gsl(g)
                inverse_sum(g, 0)
                link(one_hot(gate[:, sl, :], g, 0, 0))
                do(v.tensor_tensor(gate[:, sl, :], gate[:, sl, :],
                                   rz[:, 0, sl].unsqueeze(2).to_broadcast([P, GT, 8]), ALU.mult))
                at["gate", g] = n[0]

            def add_expert(g, e):
                v.wait_ge(dn_ps, (g * E1 + e + 1) * GT)
                v.wait_ge(init_done, g + 1)
                v.wait_ge(dve_done, at["acc", g, e - 1] if e else at["gate", g])
                for j in range(GT):
                    i = g * GT + j
                    do(v.scalar_tensor_tensor(acc[:, i, :], bank[DOWN_BANK][:, j * P:(j + 1) * P],
                                              gate[:, i, e:e + 1], acc[:, i, :], ALU.mult, ALU.add))
                at["acc", g, e] = n[0]

            def row_max(g):
                v.wait_ge(sc_ps, g + 1)
                do(v.tensor_reduce(nmx[:, gsl(g)], tiles3(bank[ATT_BANK][:]), AX.X, ALU.max, negate=True))
                at["nmx", g] = n[0]

            def add_attention(g):
                v.wait_ge(p_done, g + 1)
                link(v.reciprocal(rps[:, gsl(g)], psums[:, gsl(g)]))
                v.wait_ge(o_ps, g + 1)
                for j in range(GT):
                    i = g * GT + j
                    do(v.scalar_tensor_tensor(x_tok[:, i, :], bank[ATT_BANK][:, j * P:(j + 1) * P],
                                              rps[:, i:i + 1], x_tok[:, i, :], ALU.mult, ALU.add))
                at["x2", g] = n[0]
                v.wait_ge(dve_done, n[0])

            def number_tokens(g):
                do(v.tensor_copy(xrow[:, gsl(g), P:P + 1].bitcast(I32), token[:, gsl(g)].unsqueeze(2)))
                at["row", g] = n[0]

            def route_second(g):
                v.wait_ge(lg_ps[1], g + 1)
                do(v.tensor_copy(lg[:, 1, gsl(g), :],
                                 bank[ATT_BANK][:, 0:GT * E2].rearrange("p (i e) -> p i e", e=E2)))
                at["lg", 1, g] = n[0]
                rank(g, 1)

            def gate_second(g):
                sl = gsl(g)
                inverse_sum(g, 1)
                link(v.tensor_tensor(g2[:, sl, :], ex[:, 1, sl, 8:10],
                                     rz[:, 1, sl].unsqueeze(2).to_broadcast([P, GT, 2]), ALU.mult))
                link(v.tensor_tensor(den[:, sl], g2[:, sl, 0], g2[:, sl, 1], ALU.add))
                link(v.tensor_scalar_max(den[:, sl], den[:, sl], GATE_EPS))
                link(v.reciprocal(den[:, sl], den[:, sl]))
                do(v.tensor_tensor(g2[:, sl, :], g2[:, sl, :], den[:, sl].unsqueeze(2).to_broadcast([P, GT, 2]),
                                   ALU.mult))
                for r in range(2):
                    link(one_hot(oh[:, r, sl, :], g, 1, r))
                do(v.tensor_copy(oh_bf[:, :, sl, :], oh[:, :, sl, :]))
                at["oh", g] = n[0]

            def places(g):
                sl = gsl(g)
                v.wait_ge(cum_ps, g + 1)
                cum = bank[ATT_BANK][:, 0:2 * GT * 8].rearrange("p (r i e) -> p r i e", r=2, i=GT)
                tot = bank[ATT_BANK][:, 2 * GT * 8:4 * GT * 8].rearrange("p (r i e) -> p r i e", r=2, i=GT)
                for j in range(GT):
                    i = g * GT + j
                    link(v.tensor_tensor(off[:, i + 1, :, :], off[:, i, :, :], tot[:, :, j, :], ALU.add))
                link(v.tensor_scalar_add(loc[:, :, sl, :], cum, -1.0))
                at["cum", g] = n[0]
                for r in range(2):
                    do(v.tensor_tensor(loc[:, r, sl, :], loc[:, r, sl, :], off[:, sl, r, :], ALU.add))
                v.wait_ge(dve_done, n[0])
                choose(sl)
                at["pos", g] = n[0]

            def keep_second(sl, seen):
                first = off[:, seen:seen + 1, 0, :].to_broadcast([P, sl.stop - sl.start, 8])
                link(v.tensor_tensor(ahead[:, sl, :], oh[:, 1, sl, :], first, ALU.mult))
                link(v.tensor_reduce(aheads[:, sl], ahead[:, sl, :], AX.X, ALU.add))
                link(v.tensor_tensor(aheads[:, sl], aheads[:, sl], locs[:, 1, sl], ALU.add))
                link(v.tensor_scalar(keep[:, 1, sl], aheads[:, sl], CAP - 0.5, None, ALU.is_lt))

            def choose(sl):
                for r in range(2):
                    do(v.tensor_tensor(loc[:, r, sl, :], loc[:, r, sl, :], oh[:, r, sl, :], ALU.mult))
                v.wait_ge(dve_done, n[0])
                for r in range(2):
                    do(v.tensor_reduce(locs[:, r, sl], loc[:, r, sl, :], AX.X, ALU.add))
                v.wait_ge(dve_done, n[0])
                do(v.tensor_scalar(keep[:, 0, sl], locs[:, 0, sl], CAP - 0.5, None, ALU.is_lt))
                keep_second(sl, sl.stop)
                do(v.scalar_tensor_tensor(pos[:, 0, sl], ixf[:, 1, sl, 0], float(CAP), locs[:, 0, sl],
                                          ALU.mult, ALU.add))
                link(v.scalar_tensor_tensor(pos[:, 1, sl], ixf[:, 1, sl, 1], float(CAP), locs[:, 1, sl],
                                            ALU.mult, ALU.subtract))
                link(v.tensor_scalar_add(pos[:, 1, sl], pos[:, 1, sl], float(CAP - 1)))
                link(v.scalar_tensor_tensor(pos[:, :, sl], pos[:, :, sl], -float(SLOTS), keep[:, :, sl],
                                            ALU.add, ALU.mult))
                link(v.tensor_scalar_add(posu[:, :, sl], pos[:, :, sl], float(SLOTS)))

            def around(k):
                for e in range(E1):
                    if (g := mix_at(k, 4 * e + 8)) is not None:
                        add_expert(g, e)
                if (g := pre_at(k, 0)) is not None:
                    v.wait_ge(ld_x[g], 16)
                    ln_stats(x_tok, g, 0)
                if (g := pre_at(k, 1)) is not None:
                    ln_apply(xn, x_tok, g, 0)
                    if g == 0:
                        decays()
                if (g := pre_at(k, 4)) is not None:
                    positive_part(g)
                if (g := pre_at(k, 4)) is not None:
                    split_rows(g)
                if (g := pre_at(k, 6)) is not None:
                    add_log(g)
                if (g := pre_at(k, 7)) is not None:
                    bound_drive(g)
                if (g := pre_at(k, 11)) is not None:
                    bound_state(g)
                if (g := pre_at(k, 13)) is not None:
                    decide(g)
                if (g := mix_at(k, 1)) is not None:
                    route_first(g)
                if (g := mix_at(k, 5)) is not None:
                    gate_first(g)
                if (g := att_at(k, 0)) is not None:
                    v.wait_ge(dve_done, at["acc", g, E1 - 1])
                    ln_stats(acc, g, 1)
                    ln_center(g, 0)
                if (g := att_at(k, 1)) is not None:
                    v.wait_ge(rstd_done[1], g + 1)
                    v.wait_ge(xb_done, g + 1)
                    ln_scale_add(x_tok, g)
                    ln_stats(x_tok, g, 2)
                if (g := att_at(k, 2)) is not None:
                    ln_apply(xn, x_tok, g, 2)
                if (g := att_at(k, 9)) is not None:
                    row_max(g)
                if (g := att_at(k, 13)) is not None:
                    add_attention(g)
                    ln_stats(x_tok, g, 3)
                if (g := att_at(k, 14)) is not None:
                    ln_apply(xn, x_tok, g, 3)
                    number_tokens(g)
                if (g := att_at(k, 17)) is not None:
                    route_second(g)
                if (g := att_at(k, 19)) is not None:
                    gate_second(g)
                if (g := att_at(k, 21)) is not None:
                    places(g)

            def slot(k, clipped=False):
                if 0 <= k + 1 < UNITS and k >= 0:
                    drive(k + 1)
                if 0 <= k < UNITS:
                    scan(k, clipped)
                if 1 <= k <= UNITS:
                    read_out(k - 1)
                around(k)

            link(v.memset(lg[:], LOW))
            link(v.memset(off[:, 0, :, :], 0.0))
            for k in range(FIRST_SLOT, 0):
                slot(k)
            drive(0)
            for g in range(G):
                flag = v.value_load(flags[0:1, g:g + 1], min_val=0, max_val=1)
                before = n[0]
                with v.If(flag == 1):
                    for k in range(NS * g, NS * (g + 1)):
                        slot(k, True)
                n[0] = before
                with v.Else():
                    for k in range(NS * g, NS * (g + 1)):
                        slot(k)
            for k in range(UNITS, LAST_SLOT + 1):
                slot(k)

            keep_second(slice(0, TILES), TILES)
            for r in range(2):
                link(v.tensor_tensor(g2[:, :, r], g2[:, :, r], keep[:, r, :], ALU.mult))

            def destinations(e):
                v.wait_ge(ld_xe[e % 2], 16 * (e // 2 + 1))
                link(v.tensor_scalar(second[:], slot_no[:], off[:, TILES, 0, e:e + 1], float(TOKENS),
                                     ALU.is_ge, ALU.mult))
                link(v.tensor_tensor(dest[:, e, :], xe_tok[:, e % 2, :, P].bitcast(I32), second[:], ALU.add))
                at["dest", e] = n[0]

            def take_out(q):
                v.wait_ge(dn2_ps, 4 * (q + 1))
                if q >= 2:
                    v.wait_ge(y_sent[q % 2], 16 * GT * (q // 2))
                for j in range(GT):
                    do(v.tensor_tensor(yslot[:, q % 2, j * P:(j + 1) * P], bank[4 + q % 2][:, j * P:(j + 1) * P],
                                       fb_b[:, (q * GT + j) // CT, :], ALU.add))
                at["yslot", q] = n[0]

            v.wait_ge(ld_fb, 16)
            done = 0
            for e in range(E2 + 2):
                if e < E2:
                    destinations(e)
                while done < QN and GT * (done + 1) <= CT * (e - 1):
                    take_out(done)
                    done += 1
            for g in range(G):
                v.wait_ge(ld_y[g], 32)
                v.wait_ge(acc_done, g + 1)
                for r, src in enumerate((first_y, second_y)):
                    for j in range(GT):
                        i = g * GT + j
                        do(v.scalar_tensor_tensor(acc[:, i, :], src[:, i, :], g2[:, i, r:r + 1],
                                                  acc[:, i, :], ALU.mult, ALU.add))
                    v.wait_ge(dve_done, n[0])
                ln_stats(acc, g, 4)
                ln_center(g, 2)
                at["centered", g] = n[0]
            v.wait_ge(xb_done, 2 * G)
            v.wait_ge(rstd_done[4], G)
            ln_scale_add(acc, G - 1)
            at["out"] = n[0]

        @block.sync
        def _(sp):
            def load(dst, src, done):
                sp.dma_start(dst, src).then_inc(done, 16)

            def everywhere(t, k):
                return t.rearrange("(o d) -> o d", o=1).broadcast_to([P, k])

            load(x_tok[:, gsl(0), :], x[gsl(0)].rearrange("b t d -> t b d"), ld_x[0])
            for dst, src in ((wd_sb[:], Wd), (Alog_sb[:], A_log), (wbc_sb[:, 0:NS], WB), (wbc_sb[:, NS:2 * NS], WC),
                             (bbc_b[:, 0:NS], everywhere(bB, NS)), (bbc_b[:, NS:2 * NS], everywhere(bC, NS))):
                load(dst, src, ld_w)
            for k, t in enumerate((ln_w, ln_b, ln_gamma, ln_beta)):
                load(affine[:, k, :], everywhere(t, P), ld_affine)
            load(x_tok[:, gsl(1), :], x[gsl(1)].rearrange("b t d -> t b d"), ld_x[1])
            load(fc1raw, fc1_w.rearrange("e (t p) d -> p e t d", p=P), ld_fc)
            load(w1[:], up_w.rearrange("e d f -> d e f"), ld_moe1)
            load(w2[:], down_w.rearrange("e (t p) d -> p e t d", p=P), ld_moe1)
            sp.wait_ge(const_done, N_CONST)
            load(bias1[0:E1, :], down_b, ld_moe1)
            load(wr_sb[:], Wr, ld_w2)
            load(br_b[:], everywhere(br, E1), ld_w2)
            load(wq_sb[:], Wq, ld_w2)
            load(wk_sb[:], Wk, ld_w2)
            load(wv_sb[:], Wv, ld_w2)
            load(bv_row[:], bv.rearrange("(o d) -> o d", o=1), ld_w2)
            load(wg_sb[:], wg, ld_w2)
            load(ctx_tok[:], ctx.rearrange("b t d -> t b d"), ld_ctx)
            for g in range(2, G):
                load(x_tok[:, gsl(g), :], x[gsl(g)].rearrange("b t d -> t b d"), ld_x[g])
            load(fc2[:], fc2_w.rearrange("e (t p) d -> p e t d", p=P), ld_fc)
            for q in range(QN):
                load(slots_in[q * GW:(q + 1) * GW, :].rearrange("(p r) d -> p r d", p=P), blank, zeroed)
            for q in range(2 * G):
                load(y_rows[q * GW:(q + 1) * GW, :].rearrange("(p r) d -> p r d", p=P), blank[:, :, 0:P], zeroed)
            sp.wait_ge(up_ps, G * E1 * FT)
            sp.dma_start(fb_b, fc2_b.rearrange("(o e) d -> o e d", o=1).broadcast_to([P, E2, P])).then_inc(ld_fb, 16)
            sp.wait_ge(scattered, 16 * 2 * TILES)
            for e in range(E2):
                if e >= 2:
                    sp.wait_ge(xeT_ps, e - 1)
                    sp.wait_ge(dve_done, at["dest", e - 2])
                sp.dma_start(xe_tok[:, e % 2, :, :], slots_in[e * CAP:(e + 1) * CAP, :].rearrange(
                    "(j p) d -> p j d", p=P)).then_inc(ld_xe[e % 2], 16)
            for k in range(2):
                sp.wait_ge(y_sent[k], 16 * GT * (QN // 2))
            for g in range(G):
                for r, dst in enumerate((first_y, second_y)):
                    sp.dma_start(dst[:, gsl(g), :], y_rows[r * TOKENS + g * GW:r * TOKENS + (g + 1) * GW, :]
                                 .rearrange("(j p) d -> p j d", p=P)).then_inc(ld_y[g], 16)
            for g in range(G):
                if g < G - 1:
                    sp.wait_ge(fin_done, 2 * (g + 1))
                else:
                    sp.wait_ge(dve_done, at["out"])
                sp.dma_start(out[gsl(g)].rearrange("b t d -> t b d"), acc[:, gsl(g), :]).then_inc(stored, 16)
            sp.wait_ge(stored, 16 * G)

        @block.gpsimd
        def _(pool):
            made = [0]

            def step(ins):
                ins.then_inc(pool_step, 1)
                made[0] += 1

            def const(ins):
                ins.then_inc(const_done, 1)

            step(pool.memset(ident[:], 0.0))
            step(pool.memset(blank, 0.0))
            step(pool.memset(ident_bf[:], 0.0))
            step(pool.memset(tri[:], 1.0))
            step(pool.memset(selid[:], 0.0))
            const(pool.memset(nhalf[:], -0.5))
            pool.wait_ge(pool_step, made[0])
            for m in (ident, ident_bf):
                const(pool.affine_select(out=m[:], in_=m[:], compare_op=ALU.not_equal, fill=1.0, base=0,
                                         pattern=[[-1, P]], channel_multiplier=1))
            for r in range(3):
                ins = pool.affine_select(out=selid[:], in_=selid[:], compare_op=ALU.not_equal, fill=1.0,
                                         base=-NROW * r, pattern=[[-1, NROW]], channel_multiplier=1)
                if r < 2:
                    step(ins)
                    pool.wait_ge(pool_step, made[0])
                else:
                    const(ins)
            const(pool.memset(am[:, :, 0:1], 0.0))
            const(pool.memset(a[:, :, :, 0:1], 0.0))
            const(pool.affine_select(out=tri[:], in_=tri[:], compare_op=ALU.is_ge, fill=0.0, base=0,
                                     pattern=[[1, P]], channel_multiplier=-1))
            const(pool.memset(ones_bf[:], 1.0))
            const(pool.memset(ones_row[:], 1.0))
            const(pool.iota(iota8[:], pattern=[[1, 8]], base=0, channel_multiplier=0,
                            allow_small_or_imprecise_dtypes=True))
            const(pool.iota(slot_no[:], pattern=[[P, CT]], base=0, channel_multiplier=1,
                            allow_small_or_imprecise_dtypes=True))
            const(pool.iota(token[:], pattern=[[P, TILES]], base=0, channel_multiplier=1))
            const(pool.memset(bias1[:], 0.0))
            const(pool.memset(blank[:, :, P:P + 1].bitcast(I32), NOWHERE))

            def add_bias(g, w):
                pool.tensor_tensor(x_tok[:, gsl(g), :], x_tok[:, gsl(g), :],
                                   affine[:, w, :].unsqueeze(1).to_broadcast([P, GT, P]), ALU.add
                                   ).then_inc(xb_done, 1)

            def inverse_root(g, k):
                pool.wait_ge(dve_done, at["vpe", k, g])
                pool.tensor_tensor(rstd[:, gsl(g)], vpe[:, gsl(g)], nhalf[:], ALU.pow).then_inc(rstd_done[k], 1)

            def dispatch(r, i):
                pool.indirect_dma_start(slots_in[:], bass.IndirectOffsetOnAxis(ap=posu[:, r, i:i + 1], axis=0),
                                        xrow[:, i, :], None, bounds_check=SLOTS - 1,
                                        oob_is_err=False).then_inc(scattered, 16)

            def add_state(k):
                g = k // NS
                if k % NS == 0:
                    pool.wait_ge(y_started, g + 1)
                else:
                    pool.wait_ge(summed, k)
                pool.wait_ge(dve_done, at["hc", k])
                pool.tensor_tensor(grp(yD, g), grp(yD, g), hc[:, k % HC_RING, :], ALU.add).then_inc(summed, 1)

            for k in range(FIRST_SLOT, LAST_SLOT + 1):
                if 0 <= k - 1 < UNITS:
                    add_state(k - 1)
                if (g := pre_at(k, 0)) is not None:
                    inverse_root(g, 0)
                if (g := pre_at(k, 9)) is not None:
                    pool.wait_ge(dve_done, at["norm", 0, g])
                    pool.wait_ge(ld_affine, 16 * 4)
                    add_bias(g, 1)
                if (g := pre_at(k, 7)) is not None:
                    pool.wait_ge(dve_done, at["delta", g])
                    pool.wait_ge(xT_done[0], g + 1)
                    pool.tensor_tensor(grp(u, g), grp(delta, g), grp(xT, g), ALU.mult).then_inc(u_done, 1)
                if (g := pre_at(k, 8)) is not None:
                    pool.wait_ge(dve_done, at["boundmax", g])
                    pool.wait_ge(absx_done, g + 1)
                    pool.tensor_tensor(z2[:], z2[:], absx[:], ALU.mult).then_inc(w_done, 1)
                if (g := att_at(k, 0)) is not None:
                    inverse_root(g, 1)
                if (g := att_at(k, 1)) is not None:
                    inverse_root(g, 2)
                if (g := att_at(k, 13)) is not None:
                    inverse_root(g, 3)
                if (g := att_at(k, 14)) is not None:
                    pool.wait_ge(dve_done, at["norm", 3, g])
                    pool.tensor_copy(acc[:, gsl(g), :], xn[:, gsl(g), :]).then_inc(acc_done, 1)
                    add_bias(g, 3)
                if (g := att_at(k, 21)) is not None:
                    if g == 0:
                        pool.wait_ge(zeroed, 16 * (QN + 2 * G))
                    pool.wait_ge(dve_done, at["pos", g])
                    if g:
                        pool.wait_ge(scattered, 16 * 2 * GT * g)
                    for r in range(2):
                        for j in range(GT):
                            dispatch(r, g * GT + j)
            for q in range(QN):
                pool.wait_ge(dve_done, at["yslot", q])
                for j in range(GT):
                    t = q * GT + j
                    pool.wait_ge(dve_done, at["dest", t // CT])
                    pool.indirect_dma_start(
                        y_rows[:], bass.IndirectOffsetOnAxis(ap=dest[:, t // CT, t % CT:t % CT + 1], axis=0),
                        yslot[:, q % 2, j * P:(j + 1) * P], None, bounds_check=2 * TOKENS - 1,
                        oob_is_err=False).then_inc(y_sent[q % 2], 16)
            for g in range(G):
                inverse_root(g, 4)
                if g < G - 1:
                    pool.wait_ge(dve_done, at["centered", g])
                    pool.wait_ge(rstd_done[4], g + 1)
                    pool.tensor_tensor(acc[:, gsl(g), :], acc[:, gsl(g), :],
                                       rstd[:, gsl(g)].unsqueeze(2).to_broadcast([P, GT, P]), ALU.mult
                                       ).then_inc(fin_done, 1)
                    pool.wait_ge(fin_done, 2 * g + 1)
                    pool.tensor_tensor(acc[:, gsl(g), :], acc[:, gsl(g), :], x_tok[:, gsl(g), :], ALU.add
                                       ).then_inc(fin_done, 1)

        @block.scalar
        def _(act):
            def load(dst, src, done):
                act.dma_start(dst, src).then_inc(done, 16)

            for src, r in ((bd, C_BD), (D_param, C_D), (bq, C_BQ), (bk, C_BK)):
                load(vecs[r:r + 1, :], src.rearrange("(o d) -> o d", o=1), ld_vec)
            load(vecs[C_UPB:C_UPB + E1 * FT, :], up_b.rearrange("e (t p) -> (e t) p", p=P), ld_vec)
            load(vecs[C_FCB:C_FCB + E2 * FT, :], fc1_b.rearrange("e (t p) -> (e t) p", p=P), ld_vec)
            act.wait_ge(ld_w, 16 * N_W)
            act.activation(Alog_sb[:], Alog_sb[:], ACT.Exp).then_inc(A_exp, 1)
            act.wait_ge(cols_ps, 1)
            act.activation(cols[:], bank[ATT_BANK][:, 0:NVEC], ACT.Copy).then_inc(cols_done, 1)
            act.wait_ge(cols_done, 1)
            act.wait_ge(const_done, N_CONST)

            def turn(k, g, b):
                act.wait_ge(xT_ps[k], g + 1)
                act.activation(grp(xT, g), bank[b][:], ACT.Copy).then_inc(xT_done[k], 1)

            def decay(k):
                g, s = k // NS, k % NS
                if s == 0:
                    act.wait_ge(dve_done, at["delta", g])
                if k >= A_RING:
                    act.wait_ge(dve_done, at["h", k - A_RING])
                act.activation(a[:, k % A_RING, :, 1:P], tiles3(grp(delta, g))[:, :, 1:P], ACT.Exp,
                               scale=A_sb[:, s:s + 1]).then_inc(a_done, 1)

            def exp_scores(g, k):
                act.wait_ge(dve_done, at["dif", k, g])
                act.activation(ex[:, k, gsl(g), :], dif[:, k, gsl(g), :], ACT.Exp).then_inc(ex_done[k], 1)

            def silu(g, i):
                e, f = i // FT, i % FT
                m = g * E1 + e
                act.wait_ge(up_ps, m * FT + f + 1)
                if f == 0 and m >= 2:
                    act.wait_ge(dn_ps, GT * (m - 1))
                act.activation(hid[:, m % 2, f, :], bank[UP_BANKS[f % 2]][:], ACT.Silu,
                               bias=cols[:, C_UPB + i:C_UPB + i + 1]).then_inc(hid_done, 1)

            for k in range(FIRST_SLOT, LAST_SLOT + 1):
                if (g := pre_at(k, 4)) is not None:
                    act.wait_ge(sp_exp, 2 * g + 1)
                    act.activation(z0[:], z0[:], ACT.Exp, scale=-1.0).then_inc(sp_exp, 1)
                if (g := mix_at(k, 3)) is not None:
                    exp_scores(g, 0)
                if k % A_BATCH == 0:
                    for i in range(k + A_BATCH, k + 2 * A_BATCH):
                        if 0 <= i < UNITS:
                            decay(i)
                if (g := pre_at(k, 8)) is not None:
                    if g:
                        act.wait_ge(dve_done, at["hbound", g - 1])
                    act.wait_ge(dve_done, at["delta", g])
                    act.activation(am[:, :, 1:P], tiles3(grp(delta, g))[:, :, 1:P], ACT.Exp,
                                   scale=A_sb[:, NS:NS + 1]).then_inc(amax_done, 1)
                if (g := att_at(k, 10)) is not None:
                    act.wait_ge(dve_done, at["nmx", g])
                    for j in range(GT):
                        i = g * GT + j
                        act.activation(xn[:, i, :], bank[ATT_BANK][:, j * P:(j + 1) * P], ACT.Exp,
                                       bias=nmx[:, i:i + 1], accum_out=psums[:, i:i + 1]
                                       ).then_inc(p_done if j == GT - 1 else p_step, 1)
                if (g := att_at(k, 18)) is not None:
                    exp_scores(g, 1)
                if (g := pre_at(k, 4)) is not None:
                    act.wait_ge(sp_exp, 2 * g + 2)
                    if g:
                        act.wait_ge(dve_done, at["bound", g - 1])
                    act.activation(z1[:], z0[:], ACT.Ln, bias=1.0).then_inc(sp_ln, 1)
                if (g := pre_at(k, 7)) is not None:
                    act.wait_ge(xT_done[0], g + 1)
                    act.activation(grp(yD, g), grp(xT, g), ACT.Copy, scale=cols[:, C_D:C_D + 1]
                                   ).then_inc(y_started, 1)
                if (g := pre_at(k, 2)) is not None:
                    turn(0, g, PRE_BANK)
                if (g := pre_at(k, 3)) is not None:
                    act.wait_ge(z_ps, g + 1)
                    if g:
                        act.wait_ge(w_done, g)
                    act.activation(z0[:], bank[MIX_BANK][:], ACT.Abs,
                                   bias=cols[:, C_BD:C_BD + 1]).then_inc(sp_exp, 1)
                if (g := pre_at(k, 5)) is not None:
                    act.wait_ge(rows_ps, g + 1)
                    if g >= 2:
                        act.wait_ge(summed, NS * (g - 1))
                    act.activation(rows[:, g % 2, :], bank[PRE_BANK][0:3 * NROW, 0:GW // 2].bitcast(BF16),
                                   ACT.Copy).then_inc(rows_done, 1)
                if (g := pre_at(k, 6)) is not None:
                    act.wait_ge(sp_ln, g + 1)
                    act.activation(absx[:], grp(xT, g), ACT.Abs).then_inc(absx_done, 1)
                if 0 <= (e := k - FC_SLOT) < E2:
                    act.wait_ge(fcT_ps, e + 1)
                    act.activation(fc1T[:, e, :], bank[ATT_BANK][:], ACT.Copy).then_inc(fcT_done, 1)
                if (g := mix_at(k, 6)) is not None:
                    act.wait_ge(gT_ps, g + 1)
                    act.activation(gT[:], bank[MIX_BANK][0:8, :], ACT.Copy).then_inc(gT_done, 1)
                if (g := mix_at(k, 7)) is not None:
                    act.wait_ge(init_ps, g + 1)
                    act.activation(acc[:, gsl(g), :], tiles3(bank[MIX_BANK][:]), ACT.Copy).then_inc(init_done, 1)
                if (g := kv_at(k, 0)) is not None:
                    act.wait_ge(ctxT_ps, g + 1)
                    act.activation(ctxT[:], bank[MIX_BANK][0:CTXD, :], ACT.Copy).then_inc(ctxT_done, 1)
                if (g := kv_at(k, 2)) is not None:
                    act.wait_ge(k_ps, g + 1)
                    act.activation(grp(kT, g), bank[MIX_BANK][:], ACT.Identity,
                                   bias=cols[:, C_BK:C_BK + 1]).then_inc(k_done, 1)
                if (g := kv_at(k, 4)) is not None:
                    act.wait_ge(v_ps, g + 1)
                    act.activation(v_tok[:, gsl(g), :], tiles3(bank[MIX_BANK][:]), ACT.Copy).then_inc(v_done, 1)
                if (g := att_at(k, 5)) is not None:
                    turn(1, g, ATT_BANK)
                if (g := att_at(k, 6)) is not None:
                    act.wait_ge(q_ps, g + 1)
                    act.activation(grp(yD, g), bank[ATT_BANK][:], ACT.Identity,
                                   bias=cols[:, C_BQ:C_BQ + 1]).then_inc(q_done, 1)
                if (g := att_at(k, 11)) is not None:
                    act.wait_ge(pT_ps, g + 1)
                    act.activation(grp(xT, g), bank[ATT_BANK][:], ACT.Copy).then_inc(pT_done, 1)
                if (g := att_at(k, 15)) is not None:
                    turn(2, g, ATT_BANK)
                for i in range(E1 * FT):
                    if (g := mix_at(k, i)) is not None:
                        silu(g, i)

            def copy_expert(e):
                act.wait_ge(xeT_ps, e + 1)
                if e >= 2:
                    act.wait_ge(up2_ps, 2 * FT * (e - 1))
                act.activation(xeT[:, e % 2, 0:GW], bank[6][:], ACT.Copy).then_inc(xeT_done, 1)
                act.activation(xeT[:, e % 2, GW:CAP], bank[7][:, 0:CAP - GW], ACT.Copy).then_inc(xeT_done, 1)

            copy_expert(0)
            for e in range(E2):
                for k in range(2 * FT):
                    hf, f = k // FT, k % FT
                    m = e * 2 * FT + k
                    act.wait_ge(up2_ps, m + 1)
                    if k == 0 and e >= 2:
                        act.wait_ge(dn2_ps, CT * (e - 1))
                    act.activation(hid2[:, e % 2, f, hf * HALF:(hf + 1) * HALF], bank[m % 4][:, 0:HALF],
                                   ACT.Silu, bias=cols[:, C_FCB + e * FT + f:C_FCB + e * FT + f + 1]
                                   ).then_inc(hid2_done, 1)
                if e + 1 < E2:
                    copy_expert(e + 1)

        @block.tensor
        def _(pe):
            pe.wait_ge(const_done, N_CONST)
            pe.wait_ge(ld_vec, 16 * N_VEC)
            pe.transpose(bank[ATT_BANK][:, 0:NVEC], vecs[:], ident[0:NVEC, 0:NVEC]).then_inc(cols_ps, 1)
            read = {MIX_BANK: None, PRE_BANK: None, ATT_BANK: (cols_done, 1)}

            def claim(b, reader):
                if read[b]:
                    pe.wait_ge(*read[b])
                read[b] = reader
                return bank[b]

            def turn_xn(k, g, b):
                o = claim(b, (xT_done[k], g + 1))
                pe.wait_ge(dve_done, at["norm", (0, 2, 3)[k], g])
                for j in range(GT):
                    ins = pe.transpose(o[:, j * P:(j + 1) * P], xn[:, g * GT + j, :], ident[:])
                ins.then_inc(xT_ps[k], 1)

            def send_B(k):
                if k:
                    pe.wait_ge(dve_done, at["b", k - 1])
                broadcast_row(B_BANK, k % NS, k // NS, B_ps)

            def send_C(k):
                if k:
                    pe.wait_ge(dve_done, at["hc", k - 1])
                broadcast_row(C_BANK, NS + k % NS, k // NS, C_ps)

            def broadcast_row(b, row, g, done):
                pe.wait_ge(rows_done, g + 1)
                pe.matmul(bank[b][:], selid[:, row:row + 1].to_broadcast([3 * NROW, P]), rows[:, g % 2, :],
                          start=True, stop=True).then_inc(done, 1)

            def up(g, i):
                e, f = i // FT, i % FT
                m = (g * E1 + e) * FT + f
                if m >= 2:
                    pe.wait_ge(hid_done, m - 1)
                pe.matmul(bank[UP_BANKS[f % 2]][:], w1[:, e, f * P:(f + 1) * P], grp(yD, g),
                          start=True, stop=True).then_inc(up_ps, 1)

            def down(g, e, j):
                m = g * E1 + e
                pe.wait_ge(hid_done, (m + 1) * FT)
                if j == 0 and m:
                    pe.wait_ge(dve_done, at["acc", (m - 1) // E1, (m - 1) % E1])
                for f in range(FT):
                    ins = pe.matmul(bank[DOWN_BANK][:, j * P:(j + 1) * P], hid[:, m % 2, f, j * P:(j + 1) * P],
                                    w2[:, e, f, :], start=(f == 0), stop=(f == FT - 1))
                ins.then_inc(dn_ps, 1)

            def around(k):
                if (g := pre_at(k, 2)) is not None:
                    turn_xn(0, g, PRE_BANK)
                if (g := pre_at(k, 3)) is not None:
                    o = claim(MIX_BANK, (dve_done, at["z", g]))
                    pe.wait_ge(ld_w, 16 * N_W)
                    pe.wait_ge(xT_done[0], g + 1)
                    pe.matmul(o[:], wd_sb[:], grp(xT, g), start=True, stop=True).then_inc(z_ps, 1)
                if (g := pre_at(k, 3)) is not None:
                    o = claim(PRE_BANK, (dve_done, at["bc", g]))
                    for j in range(GT):
                        i = g * GT + j
                        ins = pe.matmul(o[:, j * 2 * NS:(j + 1) * 2 * NS], xT[:, i * P:(i + 1) * P], wbc_sb[:],
                                        start=True, stop=True)
                    ins.then_inc(bc_ps, 1)
                if (g := pre_at(k, 5)) is not None:
                    o = claim(PRE_BANK, (rows_done, g + 1))
                    pe.wait_ge(dve_done, at["parts", g])
                    for j in range(GT):
                        ins = pe.transpose(o[0:3 * NROW, j * P // 2:(j + 1) * P // 2].bitcast(BF16),
                                           parts[:, j, :], ident_bf[:])
                    ins.then_inc(rows_ps, 1)
                if (g := pre_at(k, 6)) is not None:
                    o = claim(PRE_BANK, (dve_done, at["bmax", g]))
                    pe.matmul(o[:], selid[:, NROW - 1:NROW].to_broadcast([3 * NROW, P]), rows[:, g % 2, :],
                              start=True, stop=True).then_inc(bmax_ps, 1)
                if (g := pre_at(k, 12)) is not None:
                    o = claim(PRE_BANK, (dve_done, at["worst", g]))
                    pe.wait_ge(dve_done, at["bound", g])
                    pe.transpose(o[0:1, 0:P], bound[:, g:g + 1], ident[:]).then_inc(worst_ps, 1)
                if 0 <= (e := k - FC_SLOT) < E2:
                    o = claim(ATT_BANK, (fcT_done, e + 1))
                    pe.wait_ge(ld_fc, 16 * N_FC)
                    for f in range(FT):
                        ins = pe.transpose(o[:, f * P:(f + 1) * P], fc1raw[:, e, f, :], ident[:])
                    ins.then_inc(fcT_ps, 1)
                if k >= 0:
                    around_attention(k)
                    around_mixture(k)

            def around_mixture(k):
                if (g := mix_at(k, 0)) is not None:
                    o = claim(MIX_BANK, (dve_done, at["lg", 0, g]))
                    pe.wait_ge(ld_w2, 16 * N_W2)
                    for j in range(GT):
                        i = g * GT + j
                        if j == 0:
                            pe.wait_ge(summed, NS * (g + 1))
                        ins = pe.matmul(o[:, j * E1:(j + 1) * E1], yD[:, i * P:(i + 1) * P], wr_sb[:],
                                        start=True, stop=True)
                    ins.then_inc(lg_ps[0], 1)
                if (g := mix_at(k, 6)) is not None:
                    o = claim(MIX_BANK, (gT_done, g + 1))
                    pe.wait_ge(dve_done, at["gate", g])
                    for j in range(GT):
                        ins = pe.transpose(o[0:8, j * P:(j + 1) * P], gate[:, g * GT + j, :], ident[:])
                    ins.then_inc(gT_ps, 1)
                if (g := mix_at(k, 7)) is not None:
                    o = claim(MIX_BANK, (init_done, g + 1))
                    for j in range(GT):
                        i = g * GT + j
                        pe.matmul(o[:, j * P:(j + 1) * P], yD[:, i * P:(i + 1) * P], ident[:],
                                  start=True, stop=False)
                        ins = pe.matmul(o[:, j * P:(j + 1) * P], gT[:, j * P:(j + 1) * P], bias1[:],
                                        start=False, stop=True)
                    ins.then_inc(init_ps, 1)
                for i in range(E1 * FT):
                    if (g := mix_at(k, i)) is not None:
                        if i == 0:
                            pe.wait_ge(ld_moe1, 16 * N_MOE1)
                            pe.wait_ge(summed, NS * (g + 1))
                        up(g, i)
                for e in range(E1):
                    for j in range(GT):
                        if (g := mix_at(k, 4 * e + 5 + (j + 1) // 2)) is not None:
                            down(g, e, j)

            def around_attention(k):
                if (g := kv_at(k, 0)) is not None:
                    o = claim(MIX_BANK, (ctxT_done, g + 1))
                    pe.wait_ge(ld_ctx, 16)
                    for j in range(GT):
                        ins = pe.transpose(o[0:CTXD, j * P:(j + 1) * P], ctx_tok[:, g * GT + j, :], ident[:])
                    ins.then_inc(ctxT_ps, 1)
                if (g := kv_at(k, 2)) is not None:
                    o = claim(MIX_BANK, (k_done, g + 1))
                    pe.matmul(o[:], wk_sb[:], ctxT[:], start=True, stop=True).then_inc(k_ps, 1)
                if (g := kv_at(k, 4)) is not None:
                    o = claim(MIX_BANK, (v_done, g + 1))
                    for j in range(GT):
                        pe.matmul(o[:, j * P:(j + 1) * P], ones_row[:], bv_row[:], start=True, stop=False)
                        ins = pe.matmul(o[:, j * P:(j + 1) * P], ctxT[:, j * P:(j + 1) * P], wv_sb[:],
                                        start=False, stop=True)
                    ins.then_inc(v_ps, 1)
                if (g := att_at(k, 5)) is not None:
                    turn_xn(1, g, ATT_BANK)
                if (g := att_at(k, 6)) is not None:
                    o = claim(ATT_BANK, (q_done, g + 1))
                    pe.matmul(o[:], wq_sb[:], grp(xT, g), start=True, stop=True).then_inc(q_ps, 1)
                if (g := att_at(k, 7)) is not None:
                    o = claim(ATT_BANK, (p_done, g + 1))
                    pe.wait_ge(k_done, g + 1)
                    for j in range(GT):
                        i = g * GT + j
                        ins = pe.matmul(o[:, j * P:(j + 1) * P], yD[:, i * P:(i + 1) * P],
                                        kT[:, i * P:(i + 1) * P], start=True, stop=True)
                    ins.then_inc(sc_ps, 1)
                if (g := att_at(k, 11)) is not None:
                    o = claim(ATT_BANK, (pT_done, g + 1))
                    for j in range(GT):
                        ins = pe.transpose(o[:, j * P:(j + 1) * P], xn[:, g * GT + j, :], ident[:])
                    ins.then_inc(pT_ps, 1)
                if (g := att_at(k, 12)) is not None:
                    o = claim(ATT_BANK, (dve_done, at["x2", g]))
                    pe.wait_ge(v_done, g + 1)
                    for j in range(GT):
                        i = g * GT + j
                        ins = pe.matmul(o[:, j * P:(j + 1) * P], xT[:, i * P:(i + 1) * P], v_tok[:, i, :],
                                        start=True, stop=True)
                    ins.then_inc(o_ps, 1)
                if (g := att_at(k, 15)) is not None:
                    turn_xn(2, g, ATT_BANK)
                if (g := att_at(k, 16)) is not None:
                    o = claim(ATT_BANK, (dve_done, at["lg", 1, g]))
                    for j in range(GT):
                        i = g * GT + j
                        ins = pe.matmul(o[:, j * E2:(j + 1) * E2], xT[:, i * P:(i + 1) * P], wg_sb[:],
                                        start=True, stop=True)
                    ins.then_inc(lg_ps[1], 1)
                if (g := att_at(k, 20)) is not None:
                    o = claim(ATT_BANK, (dve_done, at["cum", g]))
                    pe.wait_ge(dve_done, at["oh", g])
                    nc_ = 2 * GT * 8
                    pe.matmul(o[:, 0:nc_], tri[:], oh_bf[:, :, gsl(g), :], start=True, stop=True)
                    pe.matmul(o[:, nc_:2 * nc_], ones_bf[:], oh_bf[:, :, gsl(g), :], start=True,
                              stop=True).then_inc(cum_ps, 1)

            for k in range(FIRST_SLOT, LAST_SLOT + 1):
                if k == 0:
                    send_B(0)
                    send_B(1)
                    send_C(0)
                    send_B(2)
                around(k)
                if 0 <= k and k + 3 < UNITS:
                    send_B(k + 3)
                if 0 <= k and k + 1 < UNITS:
                    send_C(k + 1)

            def turn_expert(e):
                pe.wait_ge(ld_xe[e % 2], 16 * (e // 2 + 1))
                if e:
                    pe.wait_ge(xeT_done, 2 * e)
                else:
                    claim(MIX_BANK, None)
                    claim(PRE_BANK, None)
                    claim(ATT_BANK, None)
                for j in range(CT):
                    b, c = (bank[6], j) if j < GT else (bank[7], 0)
                    ins = pe.transpose(b[:, c * P:(c + 1) * P], xe_tok[:, e % 2, j, 0:P], ident[:])
                ins.then_inc(xeT_ps, 1)

            def expert_up(e):
                pe.wait_ge(xeT_done, 2 * (e + 1))
                for k in range(2 * FT):
                    hf, f = k // FT, k % FT
                    m = e * 2 * FT + k
                    if m >= 4:
                        pe.wait_ge(hid2_done, m - 3)
                    pe.matmul(bank[m % 4][:, 0:HALF], fc1T[:, e, f * P:(f + 1) * P],
                              xeT[:, e % 2, hf * HALF:(hf + 1) * HALF], start=True, stop=True
                              ).then_inc(up2_ps, 1)

            def expert_down(e):
                pe.wait_ge(hid2_done, 2 * FT * (e + 1))
                for j in range(CT):
                    t = e * CT + j
                    q, c = t // GT, t % GT
                    if c == 0 and q >= 2:
                        pe.wait_ge(dve_done, at["yslot", q - 2])
                    for f in range(FT):
                        ins = pe.matmul(bank[4 + q % 2][:, c * P:(c + 1) * P],
                                        hid2[:, e % 2, f, j * P:(j + 1) * P], fc2[:, e, f, :],
                                        start=(f == 0), stop=(f == FT - 1))
                    ins.then_inc(dn2_ps, 1)

            turn_expert(0)
            for e in range(E2):
                expert_up(e)
                if e + 1 < E2:
                    turn_expert(e + 1)
                if e:
                    expert_down(e - 1)
            expert_down(E2 - 1)


_INS = ['x', 'ctx_512', 'L0_attn_A_log', 'L0_attn_D_param', 'L0_attn_Wd', 'L0_attn_bd', 'L0_attn_WB',
        'L0_attn_bB', 'L0_attn_WC', 'L0_attn_bC', 'L0_attn_Wr', 'L0_attn_br', 'L0_attn_up_w',
        'L0_attn_up_b', 'L0_attn_down_w', 'L0_attn_down_b', 'L0_attn_ln_w', 'L0_attn_ln_b',
        'L0_xattn_Wq', 'L0_xattn_bq', 'L0_xattn_Wk', 'L0_xattn_bk', 'L0_xattn_Wv', 'L0_xattn_bv',
        'L0_ffn_wg', 'L0_ffn_fc1_w', 'L0_ffn_fc1_b', 'L0_ffn_fc2_w', 'L0_ffn_fc2_b',
        'L0_ffn_ln_gamma', 'L0_ffn_ln_beta']


def kernel(**inputs):
    import numpy as _np
    import concourse.bacc as _bacc
    from concourse import mybir as _mybir
    from concourse.bass_utils import run_bass_kernel_spmd as _run

    nc = _bacc.Bacc("TRN2", target_bir_lowering=False, num_devices=1)
    arrays, args = {}, []
    for name in _INS:
        arr = _np.ascontiguousarray(inputs[name])
        arrays[f"in_{name}_dram"] = arr
        args.append(nc.dram_tensor(f"in_{name}_dram", arr.shape, _mybir.dt.from_np(arr.dtype),
                                   kind="ExternalInput").ap())
    args.append(nc.dram_tensor("out_0_dram", (TILES, P, P), F32, kind="ExternalOutput").ap())
    decoder_layer(nc, *args)
    r = _run(nc, [arrays], core_ids=[0])
    return r.results[0]["out_0_dram"]
```

```python
from contextlib import ExitStack

import concourse.bass as bass
from concourse import mybir

ALU = mybir.AluOpType
ACT = mybir.ActivationFunctionType
AX = mybir.AxisListType
F32 = mybir.dt.float32
BF16 = mybir.dt.bfloat16
U32 = mybir.dt.uint32
I32 = mybir.dt.int32

P = 128
TILES = 16
GT = 4
G = TILES // GT
GW = GT * P
TOKENS = TILES * P
NS = 16
UNITS = G * NS
CTXD = 64
E1 = 4
E2 = 8
FT = 4
HID = FT * P
NROW = 2 * NS + 1
CAP = 2 * int(1.25 * ((TOKENS + E2 - 1) // E2))
CT = CAP // P
SLOTS = E2 * CAP
HALF = CAP // 2
QN = SLOTS // GW
ROW = P + 1
NOWHERE = 0x7F000000
EPS = 1e-5
GATE_EPS = 1.1920929e-07
CLIP_DB = 2.0
CLIP_H = 100.0
LOW = -3.0e38
C_UPB, C_FCB, C_BD, C_D, C_BQ, C_BK = 0, 16, 48, 49, 50, 51
NVEC = 52
A_RING, A_BATCH, HC_RING = 8, 4, 3

PRE0 = -NS


def pre_at(k, step):
    g, r = divmod(k - PRE0 - step, NS)
    return g if r == 0 and 0 <= g < G else None


def mix_at(k, step):
    g, r = divmod(k - NS - 1 - step, NS)
    return g if r == 0 and 0 <= g < G else None


KV_SLOTS = [[NS * (g + 1) + r for r in (10, 14, 15)] for g in range(G - 2)]
KV_SLOTS += [[NS * (G - 1) + r for r in (3, 5, 6)], [NS * (G - 1) + r for r in (10, 14, 15)]]


def kv_at(k, step):
    at_step = [slots[step] for slots in KV_SLOTS]
    return at_step.index(k) if k in at_step else None


LATE_STEPS = {0: 0, 1: 0, 2: 1, 3: 1, 4: 2, 5: 3, 6: 4, 7: 5, 9: 6, 10: 6, 11: 7, 12: 8, 13: 9, 14: 10, 15: 11,
              16: 12, 17: 13, 18: 13, 19: 14, 20: 15, 21: 16, 22: 17}
LATE_PLACES = 20


def att_at(k, step):
    for g in range(G):
        at_step = step if g < G - 2 else LATE_STEPS[step]
        if step >= 21 and g == G - 2:
            at_step = LATE_PLACES + step - 21
        if k == NS * (g + 1) + 22 + at_step:
            return g
    return None


def dispatches_at(k):
    found = []
    for g in range(G):
        first = next(s for s in range(NS * (G + 3)) if att_at(s, 21) == g)
        for n in range(2 * GT):
            if k == first + (n // 2 if first + GT <= UNITS else 0):
                found.append((g, n // GT, n % GT))
    return found


FC_SLOT = 7
FIRST_SLOT = PRE0
LAST_SLOT = NS * G + 22 + LATE_STEPS[22]


def decoder_layer(nc, x, ctx, A_log, D_param, Wd, bd, WB, bB, WC, bC, Wr, br, up_w, up_b, down_w,
                  down_b, ln_w, ln_b, Wq, bq, Wk, bk, Wv, bv, wg, fc1_w, fc1_b, fc2_w, fc2_b,
                  ln_gamma, ln_beta, out):
    with ExitStack() as st:
        def sb(name, shape, dt=F32):
            return st.enter_context(nc.sbuf_tensor(name, shape, dt))

        def sem(name):
            return st.enter_context(nc.semaphore(name))

        x_tok = sb("x_tok", [P, TILES, P])
        xrow = sb("xrow", [P, TILES, ROW])
        xn = xrow[:, :, 0:P]
        xT = sb("xT", [P, TOKENS])
        delta = sb("delta", [P, TOKENS])
        u = sb("u", [P, TOKENS])
        yD = sb("yD", [P, TOKENS])
        acc = sb("acc", [P, TILES, P])
        rows = sb("rows", [3 * NROW, 2, GW], BF16)
        parts = sb("parts", [P, GT, 3 * NROW], BF16)
        bcm = sb("bcm", [P, GT, NROW])
        rem = sb("rem", [P, GT, NROW])
        z0 = sb("z0", [P, GW])
        z1 = sb("z1", [P, GW])
        z2 = sb("z2", [P, GW])
        absx = z0
        hb = z1
        am = sb("am", [P, GT, P])
        a = sb("a", [P, A_RING, GT, P])
        bu = sb("bu", [P, 2, GW])
        h = sb("h", [P, 2, GW])
        hc = sb("hc", [P, HC_RING, GW])
        hid2 = sb("hid2", [P, 2, FT, CAP])
        hid = hid2[:, :, :, 0:GW]
        w1 = sb("w1", [P, E1, HID])
        w2 = sb("w2", [P, E1, FT, P])
        fb_b = w1[:, 0:2, :].rearrange("p a (e d) -> p (a e) d", d=P)
        fc1T = sb("fc1T", [P, E2, HID])
        fc2 = sb("fc2", [P, E2, FT, P])
        fc1raw = hid2[:].rearrange("p a b c -> p (a b c)")[:, 0:E2 * HID].rearrange(
            "p (e t d) -> p e t d", e=E2, t=FT)
        xe_tok = sb("xe_tok", [P, 2, CT, ROW])
        xeT = w2[:].rearrange("p e t d -> p (e t d)")[:, 0:2 * CAP].rearrange("p (b n) -> p b n", b=2)
        yslot = sb("yslot", [P, 2, GW])
        first_y = yD[:, :].rearrange("p (i d) -> p i d", d=P)
        second_y = xT[:, :].rearrange("p (i d) -> p i d", d=P)
        blank = yslot[:].rearrange("p b n -> p (b n)")[:, 0:GT * ROW].rearrange("p (j n) -> p j n", n=ROW)
        token = sb("token", [P, TILES], I32)
        pos = sb("pos", [P, 2, TILES])
        posu = sb("posu", [P, 2, TILES], U32)
        slot_no = sb("slot_no", [P, CT])
        second = sb("second", [P, CT])
        dest = sb("dest", [P, E2, CT], U32)
        slots_in = nc.dram_tensor("slots_in", [SLOTS, ROW], F32)
        y_rows = nc.dram_tensor("y_rows", [2 * TOKENS, P], F32)
        ctx_tok = sb("ctx_tok", [P, TILES, CTXD])
        ctxT = sb("ctxT", [CTXD, GW])

        def keys(g):
            return delta[:, g * GW:(g + 1) * GW] if g < G - 1 else z1[:]

        def values(g):
            return (u[:, g * GW:(g + 1) * GW] if g < G - 1 else z2[:]).rearrange("p (j d) -> p j d", d=P)

        ident = sb("ident", [P, P])
        ident_bf = sb("ident_bf", [P, P], BF16)
        tri = sb("tri", [P, P], BF16)
        ones_bf = sb("ones_bf", [P, P], BF16)
        selid = sb("selid", [3 * NROW, NROW], BF16)
        iota8 = sb("iota8", [P, 8])
        nhalf = sb("nhalf", [P, GT])
        vecs = sb("vecs", [NVEC, P])
        cols = sb("cols", [P, NVEC])
        Alog_sb = sb("Alog_sb", [P, NS])
        A_sb = sb("A_sb", [P, NS + 1])
        wd_sb = sb("wd_sb", [P, P])
        wbc_sb = sb("wbc_sb", [P, 2 * NS])
        wr_sb = sb("wr_sb", [P, E1])
        wq_sb = sb("wq_sb", [P, P])
        wk_sb = sb("wk_sb", [CTXD, P])
        wv_sb = sb("wv_sb", [CTXD, P])
        wg_sb = sb("wg_sb", [P, E2])
        bbc_b = sb("bbc_b", [P, 2 * NS])
        br_b = sb("br_b", [P, E1])
        bias1 = sb("bias1", [8, P])
        gT = sb("gT", [8, GW])
        affine = sb("affine", [P, 5, P])
        stats = sb("stats", [P, TILES, 6])
        mv = sb("mv", [P, TILES, 2])
        vpe = sb("vpe", [P, TILES])
        rstd = sb("rstd", [P, TILES])
        bound = sb("bound", [P, G])
        hmax = sb("hmax", [P, G])
        worst = sb("worst", [1, G])
        flags = sb("flags", [1, G], I32)
        lg = sb("lg", [P, 2, TILES, 8])
        mx = sb("mx", [P, 2, TILES, 8])
        ix = sb("ix", [P, 2, TILES, 8], U32)
        ixf = sb("ixf", [P, 2, TILES, 8])
        dif = sb("dif", [P, 2, TILES, 10])
        ex = sb("ex", [P, 2, TILES, 10])
        zs = sb("zs", [P, 2, TILES])
        rz = sb("rz", [P, 2, TILES])
        gate = sb("gate", [P, TILES, 8])
        g2 = sb("g2", [P, TILES, 2])
        den = sb("den", [P, TILES])
        oh = sb("oh", [P, 2, TILES, 8])
        oh_bf = sb("oh_bf", [P, 2, TILES, 8], BF16)
        off = sb("off", [P, TILES + 1, 2, 8])
        loc = sb("loc", [P, 2, TILES, 8])
        locs = sb("locs", [P, 2, TILES])
        keep = sb("keep", [P, 2, TILES])
        ahead = sb("ahead", [P, TILES, 8])
        aheads = sb("aheads", [P, TILES])
        nmx = sb("nmx", [P, TILES])
        psums = sb("psums", [P, TILES])
        rps = sb("rps", [P, TILES])

        bank = [st.enter_context(nc.psum_tensor(f"bank{i}", [P, GW], F32)) for i in range(8)]
        B_BANK, C_BANK, MIX_BANK, DOWN_BANK, PRE_BANK, ATT_BANK = 0, 1, 2, 5, 6, 7
        UP_BANKS = (3, 4)

        ld_x = [sem(f"ld_x{g}") for g in range(G)]
        ld_vec, ld_w, ld_w2, ld_ctx = sem("ld_vec"), sem("ld_w"), sem("ld_w2"), sem("ld_ctx")
        ld_moe1, ld_fc, ld_fb, ld_affine = sem("ld_moe1"), sem("ld_fc"), sem("ld_fb"), sem("ld_affine")
        dve_done = sem("dve_done")
        slow_done = sem("slow_done")
        const_done, pool_step = sem("const_done"), sem("pool_step")
        rstd_done = [sem(f"rstd_done{k}") for k in range(5)]
        u_done, w_done = sem("u_done"), sem("w_done")
        relu_done, delta_done = sem("relu_done"), sem("delta_done")
        acc_done, fin_done = sem("acc_done"), sem("fin_done")
        biased = {w: sem(f"biased{w}") for w in (1, 3, 4)}
        cols_ps, cols_done, A_exp = sem("cols_ps"), sem("cols_done"), sem("A_exp")
        xT_ps = [sem(f"xT_ps{k}") for k in range(3)]
        xT_done = [sem(f"xT_done{k}") for k in range(3)]
        z_ps, bc_ps, sp_exp, sp_ln = sem("z_ps"), sem("bc_ps"), sem("sp_exp"), sem("sp_ln")
        rows_ps, rows_done = sem("rows_ps"), sem("rows_done")
        bmax_ps, absx_done, amax_done = sem("bmax_ps"), sem("absx_done"), sem("amax_done")
        worst_ps = sem("worst_ps")
        a_done, B_ps, C_ps, y_started, summed = sem("a_done"), sem("B_ps"), sem("C_ps"), sem("y_started"), sem("summed")
        fcT_ps, fcT_done = sem("fcT_ps"), sem("fcT_done")
        ctxT_ps, ctxT_done = sem("ctxT_ps"), sem("ctxT_done")
        k_ps, k_done, v_ps, v_done = sem("k_ps"), sem("k_done"), sem("v_ps"), sem("v_done")
        lg_ps = [sem(f"lg_ps{k}") for k in range(2)]
        ex_done = [sem(f"ex_done{k}") for k in range(2)]
        gT_ps, gT_done, init_ps, init_done = sem("gT_ps"), sem("gT_done"), sem("init_ps"), sem("init_done")
        up_ps, hid_done, dn_ps = sem("up_ps"), sem("hid_done"), sem("dn_ps")
        q_ps, q_done, sc_ps, p_step, p_done = sem("q_ps"), sem("q_done"), sem("sc_ps"), sem("p_step"), sem("p_done")
        pT_ps, pT_done, o_ps, cum_ps = sem("pT_ps"), sem("pT_done"), sem("o_ps"), sem("cum_ps")
        zeroed, scattered = sem("zeroed"), sem("scattered")
        ld_xe = [sem(f"ld_xe{k}") for k in range(2)]
        xeT_ps, xeT_done = sem("xeT_ps"), sem("xeT_done")
        up2_ps, hid2_done, dn2_ps = sem("up2_ps"), sem("hid2_done"), sem("dn2_ps")
        y_sent = [sem(f"y_sent{k}") for k in range(2)]
        ld_y = [sem(f"ld_y{g}") for g in range(G)]
        weighted, stored = sem("weighted"), sem("stored")

        block = st.enter_context(nc.Block())
        N_W, N_W2, N_VEC, N_MOE1, N_FC, N_AFFINE = 6, 6, 6, 3, 2, 5
        N_CONST = 13
        at = {}

        def grp(t, g):
            return t[:, g * GW:(g + 1) * GW]

        def gsl(g):
            return slice(g * GT, (g + 1) * GT)

        def count_bank(g):
            return ATT_BANK if g < G - 2 else PRE_BANK

        def tiles3(t):
            return t.rearrange("p (j n) -> p j n", n=P)

        @block.vector
        def _(v):
            n = [0]

            def do(ins):
                ins.then_inc(dve_done, 1)
                n[0] += 1
                return n[0]

            def link(ins):
                v.wait_ge(dve_done, do(ins))

            def ln_stats(src, g, k):
                for j in range(GT):
                    do(v.bn_stats(stats[:, g * GT + j, :], src[:, g * GT + j, :]))
                v.wait_ge(dve_done, n[0])
                for j in range(GT):
                    do(v.bn_aggr(mv[:, g * GT + j, :], stats[:, g * GT + j, :]))
                v.wait_ge(dve_done, n[0])
                do(v.tensor_scalar_add(vpe[:, gsl(g)], mv[:, gsl(g), 1], EPS))
                at["vpe", k, g] = n[0]

            def ln_apply(dst, src, g, k):
                v.wait_ge(rstd_done[k], g + 1)
                v.wait_ge(dve_done, at["vpe", k, g])
                for j in range(GT):
                    i = g * GT + j
                    do(v.tensor_scalar(dst[:, i, :], src[:, i, :], mv[:, i, 0:1], rstd[:, i:i + 1],
                                       ALU.subtract, ALU.mult))
                at["norm", k, g] = n[0]

            def ln_center(g, w):
                v.wait_ge(ld_affine, 16 * N_AFFINE)
                v.wait_ge(dve_done, n[0])
                for j in range(GT):
                    i = g * GT + j
                    do(v.scalar_tensor_tensor(acc[:, i, :], acc[:, i, :], mv[:, i, 0:1], affine[:, w, :],
                                              ALU.subtract, ALU.mult))

            def ln_scale_add(dst, g):
                v.wait_ge(dve_done, n[0])
                for j in range(GT):
                    i = g * GT + j
                    do(v.scalar_tensor_tensor(dst[:, i, :], acc[:, i, :], rstd[:, i:i + 1], x_tok[:, i, :],
                                              ALU.mult, ALU.add))
                v.wait_ge(dve_done, n[0])

            def decays():
                v.wait_ge(A_exp, 1)
                link(v.tensor_scalar_mul(A_sb[:, 0:NS], Alog_sb[:], -1.0))
                link(v.tensor_reduce(A_sb[:, NS:NS + 1], A_sb[:, 0:NS], AX.X, ALU.max))
                at["A"] = n[0]
                v.wait_ge(const_done, N_CONST)
                v.wait_ge(cols_done, 1)

            def split_rows(g):
                v.wait_ge(bc_ps, g + 1)
                v.wait_ge(ld_w, 16 * N_W)
                if g:
                    v.wait_ge(rows_ps, g)
                link(v.tensor_tensor(bcm[:, :, 0:2 * NS],
                                     bank[PRE_BANK][:, 0:GT * 2 * NS].rearrange("p (j s) -> p j s", j=GT),
                                     bbc_b[:].unsqueeze(1).to_broadcast([P, GT, 2 * NS]), ALU.add))
                at["bc", g] = n[0]
                link(v.tensor_reduce(bcm[:, :, 2 * NS], bcm[:, :, 0:NS], AX.X, ALU.max,
                                     apply_absolute_value=True))
                link(v.tensor_copy(parts[:, :, 0:NROW], bcm[:]))
                link(v.tensor_tensor(rem[:], bcm[:], parts[:, :, 0:NROW], ALU.subtract))
                link(v.tensor_copy(parts[:, :, NROW:2 * NROW], rem[:]))
                link(v.tensor_tensor(bcm[:], rem[:], parts[:, :, NROW:2 * NROW], ALU.subtract))
                link(v.tensor_copy(parts[:, :, 2 * NROW:3 * NROW], bcm[:]))
                at["parts", g] = n[0]

            def bound_drive(g):
                v.wait_ge(bmax_ps, g + 1)
                v.wait_ge(delta_done, g + 1)
                if g:
                    v.wait_ge(dve_done, at["hbound", g - 1])
                link(v.tensor_tensor(z2[:], grp(delta, g), bank[PRE_BANK][:], ALU.mult))
                at["bmax", g] = n[0]
                do(v.tensor_reduce(bound[:, g:g + 1], z2[:], AX.X, ALU.max))
                at["boundmax", g] = n[0]

            def bound_state(g):
                v.wait_ge(amax_done, g + 1)
                v.wait_ge(w_done, g + 1)
                v.wait_ge(dve_done, at["boundmax", g])
                link(v.tensor_tensor_scan(hb[:], am[:].rearrange("p j n -> p (j n)"), z2[:], 0.0,
                                          ALU.mult, ALU.add))
                at["hbound", g] = n[0]
                link(v.tensor_reduce(hmax[:, g:g + 1], hb[:], AX.X, ALU.max))
                link(v.tensor_scalar_mul(bound[:, g:g + 1], bound[:, g:g + 1], CLIP_H / CLIP_DB))
                link(v.tensor_tensor(bound[:, g:g + 1], bound[:, g:g + 1], hmax[:, g:g + 1], ALU.max))
                at["bound", g] = n[0]

            def decide(g):
                v.wait_ge(worst_ps, g + 1)
                link(v.tensor_reduce(worst[:, g:g + 1], bank[PRE_BANK][0:1, 0:P], AX.X, ALU.max))
                at["worst", g] = n[0]
                link(v.tensor_scalar(flags[:, g:g + 1], worst[:, g:g + 1], CLIP_H * 0.999, None, ALU.is_gt))

            def drive(k):
                g = k // NS
                v.wait_ge(B_ps, k + 1)
                v.wait_ge(u_done, g + 1)
                if k >= 2:
                    v.wait_ge(dve_done, at["h", k - 2])
                do(v.tensor_tensor(bu[:, k % 2, :], grp(u, g), bank[B_BANK][:], ALU.mult))
                at["b", k] = n[0]

            def scan(k, clipped):
                v.wait_ge(dve_done, at["b", k])
                v.wait_ge(a_done, k + 1)
                if k >= 2:
                    v.wait_ge(dve_done, at["hc", k - 2])
                if clipped:
                    scan_clipped(k)
                    ins = v.tensor_scalar(h[:, k % 2, :], h[:, k % 2, :], CLIP_H, -CLIP_H, ALU.min, ALU.max)
                else:
                    ins = v.tensor_tensor_scan(h[:, k % 2, :], a[:, k % A_RING, :, :].rearrange("p j n -> p (j n)"),
                                               bu[:, k % 2, :], 0.0, ALU.mult, ALU.add)
                do(ins)
                at["h", k] = n[0]

            def scan_clipped(k):
                g = k // NS
                hk = tiles3(h[:, k % 2, :])
                bk_ = tiles3(bu[:, k % 2, :])
                ak = a[:, k % A_RING, :, :]

                def step(ins):
                    ins.then_inc(slow_done, 1)
                    v.wait_ge(slow_done, 1)
                    v.sem_clear(slow_done)

                bk2 = bu[:, k % 2, :]
                hk2 = h[:, k % 2, :]
                step(v.scalar_tensor_tensor(hk2, grp(xT, g), -1.0, grp(xT, g), ALU.mult, ALU.max))
                step(v.scalar_tensor_tensor(bk2, hk2, CLIP_DB, bk2, ALU.mult, ALU.min))
                step(v.scalar_tensor_tensor(bk2, hk2, -CLIP_DB, bk2, ALU.mult, ALU.max))
                step(v.tensor_scalar(hk[:, :, 0:1], bk_[:, :, 0:1], CLIP_H, -CLIP_H, ALU.min, ALU.max))
                with v.Fori(1, P) as t:
                    now, before = bass.ds(t, 1), bass.ds(t - 1, 1)
                    step(v.tensor_tensor(hk[:, :, now], ak[:, :, now], hk[:, :, before], ALU.mult))
                    step(v.tensor_tensor(hk[:, :, now], hk[:, :, now], bk_[:, :, now], ALU.add))
                    step(v.tensor_scalar(hk[:, :, now], hk[:, :, now], CLIP_H, -CLIP_H, ALU.min, ALU.max))

            def read_out(k):
                v.wait_ge(dve_done, at["h", k])
                v.wait_ge(C_ps, k + 1)
                if k >= HC_RING:
                    v.wait_ge(summed, k - HC_RING + 1)
                do(v.tensor_tensor(hc[:, k % HC_RING, :], h[:, k % 2, :], bank[C_BANK][:], ALU.mult))
                at["hc", k] = n[0]

            def rank(g, k):
                sl = gsl(g)
                v.wait_ge(dve_done, n[0])
                for i in range(g * GT, (g + 1) * GT):
                    do(v.max(mx[:, k, i, :], lg[:, k, i, :]))
                v.wait_ge(dve_done, n[0])
                for i in range(g * GT, (g + 1) * GT):
                    do(v.max_index(ix[:, k, i, :], mx[:, k, i, :], lg[:, k, i, :]))
                top = mx[:, k, sl, 0:1]
                do(v.tensor_tensor(dif[:, k, sl, 0:8], lg[:, k, sl, :], top.to_broadcast([P, GT, 8]), ALU.subtract))
                do(v.tensor_tensor(dif[:, k, sl, 8:10], mx[:, k, sl, 0:2], top.to_broadcast([P, GT, 2]),
                                   ALU.subtract))
                at["dif", k, g] = n[0]
                v.wait_ge(dve_done, n[0])
                do(v.tensor_copy(ixf[:, k, sl, 0:2], ix[:, k, sl, 0:2]))
                at["ixf", k, g] = n[0]

            def one_hot(dst, g, k, r):
                return v.tensor_tensor(dst, ixf[:, k, gsl(g), r:r + 1].to_broadcast([P, GT, 8]),
                                       iota8[:].unsqueeze(1).to_broadcast([P, GT, 8]), ALU.is_equal)

            def route_first(g):
                v.wait_ge(lg_ps[0], g + 1)
                v.wait_ge(ld_w2, 16 * N_W2)
                do(v.tensor_tensor(lg[:, 0, gsl(g), 0:E1],
                                   bank[MIX_BANK][:, 0:GT * E1].rearrange("p (i e) -> p i e", e=E1),
                                   br_b[:].unsqueeze(1).to_broadcast([P, GT, E1]), ALU.add))
                at["lg", 0, g] = n[0]
                rank(g, 0)

            def inverse_sum(g, k):
                sl = gsl(g)
                v.wait_ge(ex_done[k], g + 1)
                v.wait_ge(dve_done, at["ixf", k, g])
                link(v.tensor_reduce(zs[:, k, sl], ex[:, k, sl, 0:8], AX.X, ALU.add))
                link(v.reciprocal(rz[:, k, sl], zs[:, k, sl]))

            def gate_first(g):
                sl = gsl(g)
                inverse_sum(g, 0)
                link(one_hot(gate[:, sl, :], g, 0, 0))
                do(v.tensor_tensor(gate[:, sl, :], gate[:, sl, :],
                                   rz[:, 0, sl].unsqueeze(2).to_broadcast([P, GT, 8]), ALU.mult))
                at["gate", g] = n[0]

            def add_expert(g, e):
                v.wait_ge(dn_ps, (g * E1 + e + 1) * GT)
                v.wait_ge(init_done, g + 1)
                v.wait_ge(dve_done, at["acc", g, e - 1] if e else at["gate", g])
                for j in range(GT):
                    i = g * GT + j
                    do(v.scalar_tensor_tensor(acc[:, i, :], bank[DOWN_BANK][:, j * P:(j + 1) * P],
                                              gate[:, i, e:e + 1], acc[:, i, :], ALU.mult, ALU.add))
                at["acc", g, e] = n[0]

            def row_max(g):
                v.wait_ge(sc_ps, g + 1)
                do(v.tensor_reduce(nmx[:, gsl(g)], tiles3(bank[ATT_BANK][:]), AX.X, ALU.max, negate=True))
                at["nmx", g] = n[0]

            def add_attention(g):
                v.wait_ge(p_done, g + 1)
                link(v.reciprocal(rps[:, gsl(g)], psums[:, gsl(g)]))
                v.wait_ge(o_ps, g + 1)
                v.wait_ge(biased[4], g + 1)
                for j in range(GT):
                    i = g * GT + j
                    do(v.scalar_tensor_tensor(x_tok[:, i, :], bank[ATT_BANK][:, j * P:(j + 1) * P],
                                              rps[:, i:i + 1], x_tok[:, i, :], ALU.mult, ALU.add))
                at["x2", g] = n[0]
                v.wait_ge(dve_done, n[0])

            def number_tokens(g):
                do(v.tensor_copy(xrow[:, gsl(g), P:P + 1].bitcast(I32), token[:, gsl(g)].unsqueeze(2)))
                at["row", g] = n[0]

            def route_second(g):
                v.wait_ge(lg_ps[1], g + 1)
                do(v.tensor_copy(lg[:, 1, gsl(g), :],
                                 bank[ATT_BANK][:, 0:GT * E2].rearrange("p (i e) -> p i e", e=E2)))
                at["lg", 1, g] = n[0]
                rank(g, 1)

            def choices(g):
                sl = gsl(g)
                v.wait_ge(dve_done, at["ixf", 1, g])
                for r in range(2):
                    do(one_hot(oh[:, r, sl, :], g, 1, r))
                v.wait_ge(dve_done, n[0])
                do(v.tensor_copy(oh_bf[:, :, sl, :], oh[:, :, sl, :]))
                at["oh", g] = n[0]

            def gate_second(g):
                sl = gsl(g)
                inverse_sum(g, 1)
                link(v.tensor_tensor(g2[:, sl, :], ex[:, 1, sl, 8:10],
                                     rz[:, 1, sl].unsqueeze(2).to_broadcast([P, GT, 2]), ALU.mult))
                link(v.tensor_tensor(den[:, sl], g2[:, sl, 0], g2[:, sl, 1], ALU.add))
                link(v.tensor_scalar_max(den[:, sl], den[:, sl], GATE_EPS))
                link(v.reciprocal(den[:, sl], den[:, sl]))
                link(v.tensor_tensor(g2[:, sl, :], g2[:, sl, :], den[:, sl].unsqueeze(2).to_broadcast([P, GT, 2]),
                                     ALU.mult))

            def places(g):
                sl = gsl(g)
                v.wait_ge(cum_ps, g + 1)
                cum = bank[count_bank(g)][:, 0:2 * GT * 8].rearrange("p (r i e) -> p r i e", r=2, i=GT)
                tot = bank[count_bank(g)][:, 2 * GT * 8:4 * GT * 8].rearrange("p (r i e) -> p r i e", r=2, i=GT)
                for j in range(GT):
                    i = g * GT + j
                    link(v.tensor_tensor(off[:, i + 1, :, :], off[:, i, :, :], tot[:, :, j, :], ALU.add))
                link(v.tensor_scalar_add(loc[:, :, sl, :], cum, -1.0))
                at["cum", g] = n[0]
                for r in range(2):
                    do(v.tensor_tensor(loc[:, r, sl, :], loc[:, r, sl, :], off[:, sl, r, :], ALU.add))
                v.wait_ge(dve_done, n[0])
                for r in range(2):
                    choose(g, r)

            def keep_second(sl, seen):
                first = off[:, seen:seen + 1, 0, :].to_broadcast([P, sl.stop - sl.start, 8])
                link(v.tensor_tensor(ahead[:, sl, :], oh[:, 1, sl, :], first, ALU.mult))
                link(v.tensor_reduce(aheads[:, sl], ahead[:, sl, :], AX.X, ALU.add))
                link(v.tensor_tensor(aheads[:, sl], aheads[:, sl], locs[:, 1, sl], ALU.add))
                link(v.tensor_scalar(keep[:, 1, sl], aheads[:, sl], CAP - 0.5, None, ALU.is_lt))

            def choose(g, r):
                sl = gsl(g)
                link(v.tensor_tensor(loc[:, r, sl, :], loc[:, r, sl, :], oh[:, r, sl, :], ALU.mult))
                link(v.tensor_reduce(locs[:, r, sl], loc[:, r, sl, :], AX.X, ALU.add))
                if r == 0:
                    do(v.tensor_scalar(keep[:, 0, sl], locs[:, 0, sl], CAP - 0.5, None, ALU.is_lt))
                    link(v.scalar_tensor_tensor(pos[:, 0, sl], ixf[:, 1, sl, 0], float(CAP), locs[:, 0, sl],
                                                ALU.mult, ALU.add))
                else:
                    keep_second(sl, sl.stop)
                    link(v.scalar_tensor_tensor(pos[:, 1, sl], ixf[:, 1, sl, 1], float(CAP), locs[:, 1, sl],
                                                ALU.mult, ALU.subtract))
                    link(v.tensor_scalar_add(pos[:, 1, sl], pos[:, 1, sl], float(CAP - 1)))
                link(v.scalar_tensor_tensor(pos[:, r, sl], pos[:, r, sl], -float(SLOTS), keep[:, r, sl],
                                            ALU.add, ALU.mult))
                link(v.tensor_scalar_add(posu[:, r, sl], pos[:, r, sl], float(SLOTS)))
                at["pos", r, g] = n[0]

            def around(k):
                for e in range(E1):
                    if (g := mix_at(k, 4 * e + 9)) is not None:
                        add_expert(g, e)
                if (g := pre_at(k, 0)) is not None:
                    v.wait_ge(ld_x[g], 16)
                    ln_stats(x_tok, g, 0)
                if (g := pre_at(k, 1)) is not None:
                    ln_apply(xn, x_tok, g, 0)
                    if g == 0:
                        decays()
                if (g := pre_at(k, 4)) is not None:
                    split_rows(g)
                if (g := pre_at(k, 12)) is not None:
                    bound_drive(g)
                if (g := pre_at(k, 13)) is not None:
                    bound_state(g)
                if (g := pre_at(k, 15)) is not None:
                    decide(g)
                if (g := mix_at(k, 1)) is not None:
                    route_first(g)
                if (g := mix_at(k, 4)) is not None:
                    gate_first(g)
                if (g := att_at(k, 0)) is not None:
                    v.wait_ge(dve_done, at["acc", g, E1 - 1])
                    ln_stats(acc, g, 1)
                if (g := att_at(k, 1)) is not None:
                    ln_center(g, 0)
                if (g := att_at(k, 2)) is not None:
                    v.wait_ge(rstd_done[1], g + 1)
                    v.wait_ge(biased[1], g + 1)
                    ln_scale_add(x_tok, g)
                if (g := att_at(k, 3)) is not None:
                    ln_stats(x_tok, g, 2)
                if (g := att_at(k, 4)) is not None:
                    ln_apply(xn, x_tok, g, 2)
                if (g := att_at(k, 9)) is not None:
                    row_max(g)
                if (g := att_at(k, 13)) is not None:
                    add_attention(g)
                    ln_stats(x_tok, g, 3)
                if (g := att_at(k, 14)) is not None:
                    ln_apply(xn, x_tok, g, 3)
                    number_tokens(g)
                if (g := att_at(k, 17)) is not None:
                    route_second(g)
                if (g := att_at(k, 19)) is not None:
                    choices(g)
                if (g := att_at(k, 21)) is not None:
                    places(g)
                if (g := att_at(k, 22)) is not None:
                    gate_second(g)

            def slot(k, clipped=False):
                if 0 <= k + 1 < UNITS and k >= 0:
                    drive(k + 1)
                if 0 <= k < UNITS:
                    scan(k, clipped)
                if 1 <= k <= UNITS:
                    read_out(k - 1)
                around(k)

            link(v.memset(lg[:], LOW))
            link(v.memset(off[:, 0, :, :], 0.0))
            for k in range(FIRST_SLOT, 0):
                slot(k)
            drive(0)
            for g in range(G):
                flag = v.value_load(flags[0:1, g:g + 1], min_val=0, max_val=1)
                before = n[0]
                with v.If(flag == 1):
                    for k in range(NS * g, NS * (g + 1)):
                        slot(k, True)
                n[0] = before
                with v.Else():
                    for k in range(NS * g, NS * (g + 1)):
                        slot(k)
            for k in range(UNITS, LAST_SLOT + 1):
                slot(k)

            keep_second(slice(0, TILES), TILES)
            for r in range(2):
                link(v.tensor_tensor(g2[:, :, r], g2[:, :, r], keep[:, r, :], ALU.mult))
            at["gates"] = n[0]

            def destinations(e):
                v.wait_ge(ld_xe[e % 2], 16 * (e // 2 + 1))
                link(v.tensor_scalar(second[:], slot_no[:], off[:, TILES, 0, e:e + 1], float(TOKENS),
                                     ALU.is_ge, ALU.mult))
                link(v.tensor_tensor(dest[:, e, :], xe_tok[:, e % 2, :, P].bitcast(I32), second[:], ALU.add))
                at["dest", e] = n[0]

            def take_out(t):
                q = t // GT
                v.wait_ge(dn2_ps, t + 1)
                if t % GT == 0 and q >= 2:
                    v.wait_ge(y_sent[q % 2], 16 * GT * (q // 2))
                do(v.tensor_tensor(yslot[:, q % 2, t % GT * P:(t % GT + 1) * P], bank[4 + t % 2][:, 0:P],
                                   fb_b[:, t // CT, :], ALU.add))
                at["yslot", t] = n[0]

            v.wait_ge(ld_fb, 16)
            for e in range(E2 + 1):
                if e < E2:
                    destinations(e)
                if e:
                    for t in range(CT * (e - 1), CT * e):
                        take_out(t)
            for g in range(G):
                v.wait_ge(acc_done, g + 1)
                if g == 0:
                    v.wait_ge(ld_y[0], 32)
                    for i in range(GT):
                        do(v.scalar_tensor_tensor(acc[:, i, :], first_y[:, i, :], g2[:, i, 0:1], acc[:, i, :],
                                                  ALU.mult, ALU.add))
                    v.wait_ge(dve_done, n[0])
                for r, src in enumerate((first_y, second_y)):
                    if g or r:
                        v.wait_ge(weighted, GT * (2 * g + r))
                        link(v.tensor_tensor(acc[:, gsl(g), :], acc[:, gsl(g), :], src[:, gsl(g), :], ALU.add))
                ln_stats(acc, g, 4)
                ln_center(g, 2)
                at["centered", g] = n[0]
            v.wait_ge(biased[3], G)
            v.wait_ge(rstd_done[4], G)
            ln_scale_add(acc, G - 1)
            at["out"] = n[0]

        @block.sync
        def _(sp):
            def load(dst, src, done):
                sp.dma_start(dst, src).then_inc(done, 16)

            def everywhere(t, k):
                return t.rearrange("(o d) -> o d", o=1).broadcast_to([P, k])

            load(x_tok[:, gsl(0), :], x[gsl(0)].rearrange("b t d -> t b d"), ld_x[0])
            for dst, src in ((wd_sb[:], Wd), (Alog_sb[:], A_log), (wbc_sb[:, 0:NS], WB), (wbc_sb[:, NS:2 * NS], WC),
                             (bbc_b[:, 0:NS], everywhere(bB, NS)), (bbc_b[:, NS:2 * NS], everywhere(bC, NS))):
                load(dst, src, ld_w)
            for k, t in enumerate((ln_w, ln_b, ln_gamma, ln_beta, bv)):
                load(affine[:, k, :], everywhere(t, P), ld_affine)
            load(x_tok[:, gsl(1), :], x[gsl(1)].rearrange("b t d -> t b d"), ld_x[1])
            load(fc1raw, fc1_w.rearrange("e (t p) d -> p e t d", p=P), ld_fc)
            load(w1[:], up_w.rearrange("e d f -> d e f"), ld_moe1)
            load(w2[:], down_w.rearrange("e (t p) d -> p e t d", p=P), ld_moe1)
            sp.wait_ge(const_done, N_CONST)
            load(bias1[0:E1, :], down_b, ld_moe1)
            load(wr_sb[:], Wr, ld_w2)
            load(br_b[:], everywhere(br, E1), ld_w2)
            load(wq_sb[:], Wq, ld_w2)
            load(wk_sb[:], Wk, ld_w2)
            load(wv_sb[:], Wv, ld_w2)
            load(wg_sb[:], wg, ld_w2)
            load(ctx_tok[:], ctx.rearrange("b t d -> t b d"), ld_ctx)
            for g in range(2, G):
                load(x_tok[:, gsl(g), :], x[gsl(g)].rearrange("b t d -> t b d"), ld_x[g])
            load(fc2[:], fc2_w.rearrange("e (t p) d -> p e t d", p=P), ld_fc)
            for q in range(QN):
                load(slots_in[q * GW:(q + 1) * GW, :].rearrange("(p r) d -> p r d", p=P), blank, zeroed)
            for q in range(2 * G):
                load(y_rows[q * GW:(q + 1) * GW, :].rearrange("(p r) d -> p r d", p=P), blank[:, :, 0:P], zeroed)
            sp.wait_ge(up_ps, G * E1 * FT)
            sp.dma_start(fb_b, fc2_b.rearrange("(o e) d -> o e d", o=1).broadcast_to([P, E2, P])).then_inc(ld_fb, 16)
            sp.wait_ge(scattered, 16 * 2 * TILES)
            for e in range(E2):
                if e >= 2:
                    sp.wait_ge(xeT_ps, e - 1)
                    sp.wait_ge(dve_done, at["dest", e - 2])
                sp.dma_start(xe_tok[:, e % 2, :, :], slots_in[e * CAP:(e + 1) * CAP, :].rearrange(
                    "(j p) d -> p j d", p=P)).then_inc(ld_xe[e % 2], 16)
            for k in range(2):
                sp.wait_ge(y_sent[k], 16 * GT * (QN // 2))
            for g in range(G):
                for r, dst in enumerate((first_y, second_y)):
                    sp.dma_start(dst[:, gsl(g), :], y_rows[r * TOKENS + g * GW:r * TOKENS + (g + 1) * GW, :]
                                 .rearrange("(j p) d -> p j d", p=P)).then_inc(ld_y[g], 16)
            for g in range(G):
                if g < G - 1:
                    sp.wait_ge(fin_done, 2 * (g + 1))
                else:
                    sp.wait_ge(dve_done, at["out"])
                sp.dma_start(out[gsl(g)].rearrange("b t d -> t b d"), acc[:, gsl(g), :]).then_inc(stored, 16)
            sp.wait_ge(stored, 16 * G)

        @block.gpsimd
        def _(pool):
            made = [0]

            def step(ins):
                ins.then_inc(pool_step, 1)
                made[0] += 1

            def const(ins):
                ins.then_inc(const_done, 1)

            step(pool.memset(ident[:], 0.0))
            step(pool.memset(blank, 0.0))
            step(pool.memset(ident_bf[:], 0.0))
            step(pool.memset(tri[:], 1.0))
            step(pool.memset(selid[:], 0.0))
            const(pool.memset(nhalf[:], -0.5))
            pool.wait_ge(pool_step, made[0])
            for m in (ident, ident_bf):
                const(pool.affine_select(out=m[:], in_=m[:], compare_op=ALU.not_equal, fill=1.0, base=0,
                                         pattern=[[-1, P]], channel_multiplier=1))
            for r in range(3):
                ins = pool.affine_select(out=selid[:], in_=selid[:], compare_op=ALU.not_equal, fill=1.0,
                                         base=-NROW * r, pattern=[[-1, NROW]], channel_multiplier=1)
                if r < 2:
                    step(ins)
                    pool.wait_ge(pool_step, made[0])
                else:
                    const(ins)
            const(pool.memset(am[:, :, 0:1], 0.0))
            const(pool.memset(a[:, :, :, 0:1], 0.0))
            const(pool.affine_select(out=tri[:], in_=tri[:], compare_op=ALU.is_ge, fill=0.0, base=0,
                                     pattern=[[1, P]], channel_multiplier=-1))
            const(pool.memset(ones_bf[:], 1.0))
            const(pool.iota(iota8[:], pattern=[[1, 8]], base=0, channel_multiplier=0,
                            allow_small_or_imprecise_dtypes=True))
            const(pool.iota(slot_no[:], pattern=[[P, CT]], base=0, channel_multiplier=1,
                            allow_small_or_imprecise_dtypes=True))
            const(pool.iota(token[:], pattern=[[P, TILES]], base=0, channel_multiplier=1))
            const(pool.memset(bias1[:], 0.0))
            const(pool.memset(blank[:, :, P:P + 1].bitcast(I32), NOWHERE))

            def add_bias(g, w):
                pool.tensor_tensor(x_tok[:, gsl(g), :], x_tok[:, gsl(g), :],
                                   affine[:, w, :].unsqueeze(1).to_broadcast([P, GT, P]), ALU.add
                                   ).then_inc(biased[w], 1)

            def inverse_root(g, k):
                pool.wait_ge(dve_done, at["vpe", k, g])
                pool.tensor_tensor(rstd[:, gsl(g)], vpe[:, gsl(g)], nhalf[:], ALU.pow).then_inc(rstd_done[k], 1)

            def dispatch(r, i):
                pool.indirect_dma_start(slots_in[:], bass.IndirectOffsetOnAxis(ap=posu[:, r, i:i + 1], axis=0),
                                        xrow[:, i, :], None, bounds_check=SLOTS - 1,
                                        oob_is_err=False).then_inc(scattered, 16)

            def add_state(k):
                g = k // NS
                if k % NS == 0:
                    pool.wait_ge(y_started, g + 1)
                else:
                    pool.wait_ge(summed, k)
                pool.wait_ge(dve_done, at["hc", k])
                pool.tensor_tensor(grp(yD, g), grp(yD, g), hc[:, k % HC_RING, :], ALU.add).then_inc(summed, 1)

            for k in range(FIRST_SLOT, LAST_SLOT + 1):
                if 0 <= k - 1 < UNITS:
                    add_state(k - 1)
                if (g := pre_at(k, 0)) is not None:
                    inverse_root(g, 0)
                if (g := pre_at(k, 13)) is not None:
                    pool.wait_ge(dve_done, at["norm", 0, g])
                    pool.wait_ge(ld_affine, 16 * N_AFFINE)
                    add_bias(g, 1)
                if (g := pre_at(k, 7)) is not None:
                    pool.wait_ge(sp_ln, g + 1)
                    pool.wait_ge(relu_done, g + 1)
                    pool.tensor_tensor(grp(delta, g), grp(delta, g), z1[:], ALU.add).then_inc(delta_done, 1)
                if (g := pre_at(k, 8)) is not None:
                    pool.wait_ge(delta_done, g + 1)
                    pool.wait_ge(xT_done[0], g + 1)
                    pool.tensor_tensor(grp(u, g), grp(delta, g), grp(xT, g), ALU.mult).then_inc(u_done, 1)
                if (g := pre_at(k, 12)) is not None:
                    pool.wait_ge(dve_done, at["boundmax", g])
                    pool.wait_ge(absx_done, g + 1)
                    pool.tensor_tensor(z2[:], z2[:], absx[:], ALU.mult).then_inc(w_done, 1)
                if (g := att_at(k, 0)) is not None:
                    inverse_root(g, 1)
                if (g := att_at(k, 3)) is not None:
                    inverse_root(g, 2)
                if (g := att_at(k, 5)) is not None:
                    pool.wait_ge(dve_done, at["norm", 2, g])
                    add_bias(g, 4)
                if (g := att_at(k, 13)) is not None:
                    inverse_root(g, 3)
                if (g := att_at(k, 14)) is not None:
                    pool.wait_ge(dve_done, at["norm", 3, g])
                    pool.tensor_copy(acc[:, gsl(g), :], xn[:, gsl(g), :]).then_inc(acc_done, 1)
                    pool.wait_ge(biased[4], g + 1)
                    add_bias(g, 3)
                for g, r, j in dispatches_at(k):
                    if j == 0 and r == 0:
                        if g:
                            pool.wait_ge(scattered, 16 * 2 * GT * g)
                        else:
                            pool.wait_ge(zeroed, 16 * (QN + 2 * G))
                    if j == 0:
                        pool.wait_ge(dve_done, at["pos", r, g])
                    dispatch(r, g * GT + j)
            for q in range(QN):
                for j in range(GT):
                    t = q * GT + j
                    pool.wait_ge(dve_done, at["yslot", t])
                    pool.wait_ge(dve_done, at["dest", t // CT])
                    pool.indirect_dma_start(
                        y_rows[:], bass.IndirectOffsetOnAxis(ap=dest[:, t // CT, t % CT:t % CT + 1], axis=0),
                        yslot[:, q % 2, j * P:(j + 1) * P], None, bounds_check=2 * TOKENS - 1,
                        oob_is_err=False).then_inc(y_sent[q % 2], 16)
            for g in range(G):
                inverse_root(g, 4)
                if g < G - 1:
                    pool.wait_ge(dve_done, at["centered", g])
                    pool.wait_ge(rstd_done[4], g + 1)
                    pool.tensor_tensor(acc[:, gsl(g), :], acc[:, gsl(g), :],
                                       rstd[:, gsl(g)].unsqueeze(2).to_broadcast([P, GT, P]), ALU.mult
                                       ).then_inc(fin_done, 1)
                    pool.wait_ge(fin_done, 2 * g + 1)
                    pool.tensor_tensor(acc[:, gsl(g), :], acc[:, gsl(g), :], x_tok[:, gsl(g), :], ALU.add
                                       ).then_inc(fin_done, 1)

        @block.scalar
        def _(act):
            def load(dst, src, done):
                act.dma_start(dst, src).then_inc(done, 16)

            for src, r in ((bd, C_BD), (D_param, C_D), (bq, C_BQ), (bk, C_BK)):
                load(vecs[r:r + 1, :], src.rearrange("(o d) -> o d", o=1), ld_vec)
            load(vecs[C_UPB:C_UPB + E1 * FT, :], up_b.rearrange("e (t p) -> (e t) p", p=P), ld_vec)
            load(vecs[C_FCB:C_FCB + E2 * FT, :], fc1_b.rearrange("e (t p) -> (e t) p", p=P), ld_vec)
            act.wait_ge(ld_w, 16 * N_W)
            act.activation(Alog_sb[:], Alog_sb[:], ACT.Exp).then_inc(A_exp, 1)
            act.wait_ge(cols_ps, 1)
            act.activation(cols[:], bank[ATT_BANK][:, 0:NVEC], ACT.Copy).then_inc(cols_done, 1)
            act.wait_ge(cols_done, 1)
            act.wait_ge(const_done, N_CONST)

            def turn(k, g, b):
                act.wait_ge(xT_ps[k], g + 1)
                act.activation(grp(xT, g), bank[b][:], ACT.Copy).then_inc(xT_done[k], 1)

            def decay(k):
                g, s = k // NS, k % NS
                if s == 0:
                    act.wait_ge(delta_done, g + 1)
                if k >= A_RING:
                    act.wait_ge(dve_done, at["h", k - A_RING])
                act.activation(a[:, k % A_RING, :, 1:P], tiles3(grp(delta, g))[:, :, 1:P], ACT.Exp,
                               scale=A_sb[:, s:s + 1]).then_inc(a_done, 1)

            def exp_scores(g, k):
                act.wait_ge(dve_done, at["dif", k, g])
                act.activation(ex[:, k, gsl(g), :], dif[:, k, gsl(g), :], ACT.Exp).then_inc(ex_done[k], 1)

            def silu(g, i):
                e, f = i // FT, i % FT
                m = g * E1 + e
                act.wait_ge(up_ps, m * FT + f + 1)
                if f == 0 and m >= 2:
                    act.wait_ge(dn_ps, GT * (m - 1))
                act.activation(hid[:, m % 2, f, :], bank[UP_BANKS[f % 2]][:], ACT.Silu,
                               bias=cols[:, C_UPB + i:C_UPB + i + 1]).then_inc(hid_done, 1)

            for k in range(FIRST_SLOT, LAST_SLOT + 1):
                if (g := pre_at(k, 4)) is not None:
                    act.wait_ge(sp_exp, 2 * g + 1)
                    act.activation(z0[:], z0[:], ACT.Exp, scale=-1.0).then_inc(sp_exp, 1)
                if (g := mix_at(k, 3)) is not None:
                    exp_scores(g, 0)
                if (g := pre_at(k, 12)) is not None:
                    if g:
                        act.wait_ge(dve_done, at["hbound", g - 1])
                    act.wait_ge(delta_done, g + 1)
                    act.activation(am[:, :, 1:P], tiles3(grp(delta, g))[:, :, 1:P], ACT.Exp,
                                   scale=A_sb[:, NS:NS + 1]).then_inc(amax_done, 1)
                if (g := att_at(k, 10)) is not None:
                    act.wait_ge(dve_done, at["nmx", g])
                    for j in range(GT):
                        i = g * GT + j
                        act.activation(xn[:, i, :], bank[ATT_BANK][:, j * P:(j + 1) * P], ACT.Exp,
                                       bias=nmx[:, i:i + 1], accum_out=psums[:, i:i + 1]
                                       ).then_inc(p_done if j == GT - 1 else p_step, 1)
                if (g := att_at(k, 18)) is not None:
                    exp_scores(g, 1)
                if k % A_BATCH == 0:
                    for i in range(k + A_BATCH, k + 2 * A_BATCH):
                        if 0 <= i < UNITS:
                            decay(i)
                if (g := pre_at(k, 4)) is not None:
                    act.wait_ge(sp_exp, 2 * g + 2)
                    if g:
                        act.wait_ge(dve_done, at["bound", g - 1])
                    act.activation(z1[:], z0[:], ACT.Ln, bias=1.0).then_inc(sp_ln, 1)
                if (g := pre_at(k, 7)) is not None:
                    act.wait_ge(xT_done[0], g + 1)
                    act.activation(grp(yD, g), grp(xT, g), ACT.Copy, scale=cols[:, C_D:C_D + 1]
                                   ).then_inc(y_started, 1)
                if (g := pre_at(k, 2)) is not None:
                    turn(0, g, PRE_BANK)
                if (g := pre_at(k, 3)) is not None:
                    act.wait_ge(z_ps, g + 1)
                    if g:
                        act.wait_ge(w_done, g)
                    act.activation(z0[:], bank[MIX_BANK][:], ACT.Abs,
                                   bias=cols[:, C_BD:C_BD + 1]).then_inc(sp_exp, 1)
                    act.activation(grp(delta, g), bank[MIX_BANK][:], ACT.Relu,
                                   bias=cols[:, C_BD:C_BD + 1]).then_inc(relu_done, 1)
                if (g := pre_at(k, 5)) is not None:
                    act.wait_ge(rows_ps, g + 1)
                    if g >= 2:
                        act.wait_ge(summed, NS * (g - 1))
                    act.activation(rows[:, g % 2, :], bank[PRE_BANK][0:3 * NROW, 0:GW // 2].bitcast(BF16),
                                   ACT.Copy).then_inc(rows_done, 1)
                if (g := pre_at(k, 6)) is not None:
                    act.wait_ge(sp_ln, g + 1)
                    act.activation(absx[:], grp(xT, g), ACT.Abs).then_inc(absx_done, 1)
                if 0 <= (e := k - FC_SLOT) < E2:
                    act.wait_ge(fcT_ps, e + 1)
                    act.activation(fc1T[:, e, :], bank[ATT_BANK][:], ACT.Copy).then_inc(fcT_done, 1)
                if (g := mix_at(k, 6)) is not None:
                    act.wait_ge(gT_ps, g + 1)
                    act.activation(gT[:], bank[MIX_BANK][0:8, :], ACT.Copy).then_inc(gT_done, 1)
                if (g := mix_at(k, 8)) is not None:
                    act.wait_ge(init_ps, g + 1)
                    act.activation(acc[:, gsl(g), :], tiles3(bank[MIX_BANK][:]), ACT.Copy).then_inc(init_done, 1)
                if (g := kv_at(k, 0)) is not None:
                    act.wait_ge(ctxT_ps, g + 1)
                    act.activation(ctxT[:], bank[MIX_BANK][0:CTXD, :], ACT.Copy).then_inc(ctxT_done, 1)
                if (g := kv_at(k, 1)) is not None:
                    act.wait_ge(k_ps, g + 1)
                    if g == G - 1:
                        act.wait_ge(dve_done, at["bound", g])
                    act.activation(keys(g), bank[MIX_BANK][:], ACT.Identity,
                                   bias=cols[:, C_BK:C_BK + 1]).then_inc(k_done, 1)
                if (g := kv_at(k, 2)) is not None:
                    act.wait_ge(v_ps, g + 1)
                    act.activation(values(g), tiles3(bank[MIX_BANK][:]), ACT.Copy).then_inc(v_done, 1)
                if (g := att_at(k, 5)) is not None:
                    turn(1, g, ATT_BANK)
                if (g := att_at(k, 6)) is not None:
                    act.wait_ge(q_ps, g + 1)
                    act.activation(grp(yD, g), bank[ATT_BANK][:], ACT.Identity,
                                   bias=cols[:, C_BQ:C_BQ + 1]).then_inc(q_done, 1)
                if (g := att_at(k, 11)) is not None:
                    act.wait_ge(pT_ps, g + 1)
                    act.activation(grp(xT, g), bank[ATT_BANK][:], ACT.Copy).then_inc(pT_done, 1)
                if (g := att_at(k, 15)) is not None:
                    turn(2, g, ATT_BANK)
                for i in range(E1 * FT):
                    if (g := mix_at(k, i)) is not None:
                        silu(g, i)

            def copy_expert(e):
                act.wait_ge(xeT_ps, e + 1)
                if e >= 2:
                    act.wait_ge(up2_ps, 2 * FT * (e - 1))
                act.activation(xeT[:, e % 2, 0:GW], bank[6][:], ACT.Copy).then_inc(xeT_done, 1)
                act.activation(xeT[:, e % 2, GW:CAP], bank[7][:, 0:CAP - GW], ACT.Copy).then_inc(xeT_done, 1)

            copy_expert(0)
            for e in range(E2):
                for k in range(2 * FT):
                    hf, f = k // FT, k % FT
                    m = e * 2 * FT + k
                    act.wait_ge(up2_ps, m + 1)
                    if k == 0 and e >= 2:
                        act.wait_ge(dn2_ps, CT * (e - 1))
                    act.activation(hid2[:, e % 2, f, hf * HALF:(hf + 1) * HALF], bank[m % 4][:, 0:HALF],
                                   ACT.Silu, bias=cols[:, C_FCB + e * FT + f:C_FCB + e * FT + f + 1]
                                   ).then_inc(hid2_done, 1)
                if e + 1 < E2:
                    copy_expert(e + 1)
            act.wait_ge(dve_done, at["gates"])
            for g in range(G):
                act.wait_ge(ld_y[g], 32)
                for r, t in enumerate((first_y, second_y)):
                    for i in range(g * GT, (g + 1) * GT) if g or r else ():
                        act.activation(t[:, i, :], t[:, i, :], ACT.Copy, scale=g2[:, i, r:r + 1]
                                       ).then_inc(weighted, 1)

        @block.tensor
        def _(pe):
            pe.wait_ge(const_done, N_CONST)
            pe.wait_ge(ld_vec, 16 * N_VEC)
            pe.transpose(bank[ATT_BANK][:, 0:NVEC], vecs[:], ident[0:NVEC, 0:NVEC]).then_inc(cols_ps, 1)
            read = {MIX_BANK: None, PRE_BANK: None, ATT_BANK: (cols_done, 1)}

            def claim(b, reader):
                if read[b]:
                    pe.wait_ge(*read[b])
                read[b] = reader
                return bank[b]

            def turn_xn(k, g, b):
                o = claim(b, (xT_done[k], g + 1))
                pe.wait_ge(dve_done, at["norm", (0, 2, 3)[k], g])
                for j in range(GT):
                    ins = pe.transpose(o[:, j * P:(j + 1) * P], xn[:, g * GT + j, :], ident[:])
                ins.then_inc(xT_ps[k], 1)

            def send_B(k):
                if k:
                    pe.wait_ge(dve_done, at["b", k - 1])
                broadcast_row(B_BANK, k % NS, k // NS, B_ps)

            def send_C(k):
                if k:
                    pe.wait_ge(dve_done, at["hc", k - 1])
                broadcast_row(C_BANK, NS + k % NS, k // NS, C_ps)

            def broadcast_row(b, row, g, done):
                pe.wait_ge(rows_done, g + 1)
                pe.matmul(bank[b][:], selid[:, row:row + 1].to_broadcast([3 * NROW, P]), rows[:, g % 2, :],
                          start=True, stop=True).then_inc(done, 1)

            def up(g, i):
                e, f = i // FT, i % FT
                m = (g * E1 + e) * FT + f
                if m >= 2:
                    pe.wait_ge(hid_done, m - 1)
                pe.matmul(bank[UP_BANKS[f % 2]][:], w1[:, e, f * P:(f + 1) * P], grp(yD, g),
                          start=True, stop=True).then_inc(up_ps, 1)

            def down(g, e, j):
                m = g * E1 + e
                pe.wait_ge(hid_done, (m + 1) * FT)
                if j == 0 and m:
                    pe.wait_ge(dve_done, at["acc", (m - 1) // E1, (m - 1) % E1])
                for f in range(FT):
                    ins = pe.matmul(bank[DOWN_BANK][:, j * P:(j + 1) * P], hid[:, m % 2, f, j * P:(j + 1) * P],
                                    w2[:, e, f, :], start=(f == 0), stop=(f == FT - 1))
                ins.then_inc(dn_ps, 1)

            def around(k):
                if (g := pre_at(k, 2)) is not None:
                    turn_xn(0, g, PRE_BANK)
                if (g := pre_at(k, 3)) is not None:
                    o = claim(MIX_BANK, (relu_done, g + 1))
                    pe.wait_ge(ld_w, 16 * N_W)
                    pe.wait_ge(xT_done[0], g + 1)
                    pe.matmul(o[:], wd_sb[:], grp(xT, g), start=True, stop=True).then_inc(z_ps, 1)
                if (g := pre_at(k, 3)) is not None:
                    o = claim(PRE_BANK, (dve_done, at["bc", g]))
                    for j in range(GT):
                        i = g * GT + j
                        ins = pe.matmul(o[:, j * 2 * NS:(j + 1) * 2 * NS], xT[:, i * P:(i + 1) * P], wbc_sb[:],
                                        start=True, stop=True)
                    ins.then_inc(bc_ps, 1)
                if (g := pre_at(k, 5)) is not None:
                    o = claim(PRE_BANK, (rows_done, g + 1))
                    pe.wait_ge(dve_done, at["parts", g])
                    for j in range(GT):
                        ins = pe.transpose(o[0:3 * NROW, j * P // 2:(j + 1) * P // 2].bitcast(BF16),
                                           parts[:, j, :], ident_bf[:])
                    ins.then_inc(rows_ps, 1)
                if (g := pre_at(k, 6)) is not None:
                    o = claim(PRE_BANK, (dve_done, at["bmax", g]))
                    pe.matmul(o[:], selid[:, NROW - 1:NROW].to_broadcast([3 * NROW, P]), rows[:, g % 2, :],
                              start=True, stop=True).then_inc(bmax_ps, 1)
                if (g := pre_at(k, 14)) is not None:
                    o = claim(PRE_BANK, (dve_done, at["worst", g]))
                    pe.wait_ge(dve_done, at["bound", g])
                    pe.transpose(o[0:1, 0:P], bound[:, g:g + 1], ident[:]).then_inc(worst_ps, 1)
                if 0 <= (e := k - FC_SLOT) < E2:
                    o = claim(ATT_BANK, (fcT_done, e + 1))
                    pe.wait_ge(ld_fc, 16 * N_FC)
                    for f in range(FT):
                        ins = pe.transpose(o[:, f * P:(f + 1) * P], fc1raw[:, e, f, :], ident[:])
                    ins.then_inc(fcT_ps, 1)
                if k >= 0:
                    around_attention(k)
                    around_mixture(k)

            def next_up(k):
                for i in range(E1 * FT):
                    if (g := mix_at(k, i)) is not None:
                        if i == 0:
                            pe.wait_ge(ld_moe1, 16 * N_MOE1)
                            pe.wait_ge(summed, NS * (g + 1))
                        up(g, i)

            def around_mixture(k):
                if (g := mix_at(k, 0)) is not None:
                    o = claim(MIX_BANK, (dve_done, at["lg", 0, g]))
                    pe.wait_ge(ld_w2, 16 * N_W2)
                    for j in range(GT):
                        i = g * GT + j
                        if j == 0:
                            pe.wait_ge(summed, NS * (g + 1))
                        ins = pe.matmul(o[:, j * E1:(j + 1) * E1], yD[:, i * P:(i + 1) * P], wr_sb[:],
                                        start=True, stop=True)
                    ins.then_inc(lg_ps[0], 1)
                if (g := mix_at(k, 6)) is not None:
                    o = claim(MIX_BANK, (gT_done, g + 1))
                    pe.wait_ge(dve_done, at["gate", g])
                    for j in range(GT):
                        ins = pe.transpose(o[0:8, j * P:(j + 1) * P], gate[:, g * GT + j, :], ident[:])
                    ins.then_inc(gT_ps, 1)
                for half in range(2):
                    if (g := mix_at(k, 7 + half)) is None:
                        continue
                    o = bank[MIX_BANK] if half else claim(MIX_BANK, (init_done, g + 1))
                    if half == 0:
                        pe.wait_ge(gT_done, g + 1)
                    for j in range(half * GT // 2, (half + 1) * GT // 2):
                        i = g * GT + j
                        pe.matmul(o[:, j * P:(j + 1) * P], yD[:, i * P:(i + 1) * P], ident[:],
                                  start=True, stop=False)
                        ins = pe.matmul(o[:, j * P:(j + 1) * P], gT[:, j * P:(j + 1) * P], bias1[:],
                                        start=False, stop=True)
                    if half:
                        ins.then_inc(init_ps, 1)
                for e in range(E1):
                    for j in range(GT):
                        if (g := mix_at(k, 4 * e + 5 + j)) is not None:
                            down(g, e, j)

            def around_attention(k):
                if (g := kv_at(k, 0)) is not None:
                    o = claim(MIX_BANK, (ctxT_done, g + 1))
                    pe.wait_ge(ld_ctx, 16)
                    for j in range(GT):
                        ins = pe.transpose(o[0:CTXD, j * P:(j + 1) * P], ctx_tok[:, g * GT + j, :], ident[:])
                    ins.then_inc(ctxT_ps, 1)
                if (g := kv_at(k, 1)) is not None:
                    o = claim(MIX_BANK, (k_done, g + 1))
                    pe.matmul(o[:], wk_sb[:], ctxT[:], start=True, stop=True).then_inc(k_ps, 1)
                if (g := kv_at(k, 2)) is not None:
                    o = claim(MIX_BANK, (v_done, g + 1))
                    for j in range(GT):
                        ins = pe.matmul(o[:, j * P:(j + 1) * P], ctxT[:, j * P:(j + 1) * P], wv_sb[:],
                                        start=True, stop=True)
                    ins.then_inc(v_ps, 1)
                if (g := att_at(k, 5)) is not None:
                    turn_xn(1, g, ATT_BANK)
                if (g := att_at(k, 6)) is not None:
                    o = claim(ATT_BANK, (q_done, g + 1))
                    pe.matmul(o[:], wq_sb[:], grp(xT, g), start=True, stop=True).then_inc(q_ps, 1)
                if (g := att_at(k, 7)) is not None:
                    o = claim(ATT_BANK, (p_done, g + 1))
                    pe.wait_ge(k_done, g + 1)
                    for j in range(GT):
                        i = g * GT + j
                        ins = pe.matmul(o[:, j * P:(j + 1) * P], yD[:, i * P:(i + 1) * P],
                                        keys(g)[:, j * P:(j + 1) * P], start=True, stop=True)
                    ins.then_inc(sc_ps, 1)
                if (g := att_at(k, 11)) is not None:
                    o = claim(ATT_BANK, (pT_done, g + 1))
                    for j in range(GT):
                        ins = pe.transpose(o[:, j * P:(j + 1) * P], xn[:, g * GT + j, :], ident[:])
                    ins.then_inc(pT_ps, 1)
                if (g := att_at(k, 12)) is not None:
                    o = claim(ATT_BANK, (dve_done, at["x2", g]))
                    pe.wait_ge(v_done, g + 1)
                    for j in range(GT):
                        i = g * GT + j
                        ins = pe.matmul(o[:, j * P:(j + 1) * P], xT[:, i * P:(i + 1) * P], values(g)[:, j, :],
                                        start=True, stop=True)
                    ins.then_inc(o_ps, 1)
                if (g := att_at(k, 15)) is not None:
                    turn_xn(2, g, ATT_BANK)
                if (g := att_at(k, 16)) is not None:
                    o = claim(ATT_BANK, (dve_done, at["lg", 1, g]))
                    for j in range(GT):
                        i = g * GT + j
                        ins = pe.matmul(o[:, j * E2:(j + 1) * E2], xT[:, i * P:(i + 1) * P], wg_sb[:],
                                        start=True, stop=True)
                    ins.then_inc(lg_ps[1], 1)
                if (g := att_at(k, 20)) is not None:
                    o = claim(count_bank(g), (dve_done, at["cum", g]))
                    pe.wait_ge(dve_done, at["oh", g])
                    nc_ = 2 * GT * 8
                    pe.matmul(o[:, 0:nc_], tri[:], oh_bf[:, :, gsl(g), :], start=True, stop=True)
                    pe.matmul(o[:, nc_:2 * nc_], ones_bf[:], oh_bf[:, :, gsl(g), :], start=True,
                              stop=True).then_inc(cum_ps, 1)

            for k in range(FIRST_SLOT, LAST_SLOT + 1):
                if k == 0:
                    send_B(0)
                    send_B(1)
                    send_C(0)
                    send_B(2)
                around(k)
                if 0 <= k and k + 3 < UNITS:
                    send_B(k + 3)
                if k >= 0:
                    next_up(k + 1)
                if 0 <= k and k + 1 < UNITS:
                    send_C(k + 1)

            def turn_expert(e):
                pe.wait_ge(ld_xe[e % 2], 16 * (e // 2 + 1))
                if e:
                    pe.wait_ge(xeT_done, 2 * e)
                else:
                    claim(MIX_BANK, None)
                    claim(PRE_BANK, None)
                    claim(ATT_BANK, None)
                for j in range(CT):
                    b, c = (bank[6], j) if j < GT else (bank[7], 0)
                    ins = pe.transpose(b[:, c * P:(c + 1) * P], xe_tok[:, e % 2, j, 0:P], ident[:])
                ins.then_inc(xeT_ps, 1)

            def expert_up(e):
                pe.wait_ge(xeT_done, 2 * (e + 1))
                for k in range(2 * FT):
                    hf, f = k // FT, k % FT
                    m = e * 2 * FT + k
                    if m >= 4:
                        pe.wait_ge(hid2_done, m - 3)
                    pe.matmul(bank[m % 4][:, 0:HALF], fc1T[:, e, f * P:(f + 1) * P],
                              xeT[:, e % 2, hf * HALF:(hf + 1) * HALF], start=True, stop=True
                              ).then_inc(up2_ps, 1)

            def expert_down(e):
                pe.wait_ge(hid2_done, 2 * FT * (e + 1))
                for j in range(CT):
                    t = e * CT + j
                    if t >= 2:
                        pe.wait_ge(dve_done, at["yslot", t - 2])
                    for f in range(FT):
                        ins = pe.matmul(bank[4 + t % 2][:, 0:P],
                                        hid2[:, e % 2, f, j * P:(j + 1) * P], fc2[:, e, f, :],
                                        start=(f == 0), stop=(f == FT - 1))
                    ins.then_inc(dn2_ps, 1)

            turn_expert(0)
            for e in range(E2):
                expert_up(e)
                if e + 1 < E2:
                    turn_expert(e + 1)
                if e:
                    expert_down(e - 1)
            expert_down(E2 - 1)


_INS = ['x', 'ctx_512', 'L0_attn_A_log', 'L0_attn_D_param', 'L0_attn_Wd', 'L0_attn_bd', 'L0_attn_WB',
        'L0_attn_bB', 'L0_attn_WC', 'L0_attn_bC', 'L0_attn_Wr', 'L0_attn_br', 'L0_attn_up_w',
        'L0_attn_up_b', 'L0_attn_down_w', 'L0_attn_down_b', 'L0_attn_ln_w', 'L0_attn_ln_b',
        'L0_xattn_Wq', 'L0_xattn_bq', 'L0_xattn_Wk', 'L0_xattn_bk', 'L0_xattn_Wv', 'L0_xattn_bv',
        'L0_ffn_wg', 'L0_ffn_fc1_w', 'L0_ffn_fc1_b', 'L0_ffn_fc2_w', 'L0_ffn_fc2_b',
        'L0_ffn_ln_gamma', 'L0_ffn_ln_beta']


def kernel(**inputs):
    import numpy as _np
    import concourse.bacc as _bacc
    from concourse import mybir as _mybir
    from concourse.bass_utils import run_bass_kernel_spmd as _run

    nc = _bacc.Bacc("TRN2", target_bir_lowering=False, num_devices=1)
    arrays, args = {}, []
    for name in _INS:
        arr = _np.ascontiguousarray(inputs[name])
        arrays[f"in_{name}_dram"] = arr
        args.append(nc.dram_tensor(f"in_{name}_dram", arr.shape, _mybir.dt.from_np(arr.dtype),
                                   kind="ExternalInput").ap())
    args.append(nc.dram_tensor("out_0_dram", (TILES, P, P), F32, kind="ExternalOutput").ap())
    decoder_layer(nc, *args)
    r = _run(nc, [arrays], core_ids=[0])
    return r.results[0]["out_0_dram"]
```
